# Optimizing a Trainium2 kernel written in Bass

```python
import numpy as np
import jax
import jax.numpy as jnp

def _softmax(x, axis=-1):
    return jax.nn.softmax(x, axis=axis)

def _gelu(x):
    return jax.nn.gelu(x, approximate=True)

def _silu(x):
    return jax.nn.silu(x)

def _sigmoid(x):
    return jax.nn.sigmoid(x)

def _layernorm(x, axis=-1, eps=1e-05):
    m = jnp.mean(x, axis=axis, keepdims=True)
    v = jnp.var(x, axis=axis, keepdims=True)
    return (x - m) / jnp.sqrt(v + eps)

def _scatter_add(tgt, idx, src, axis=0):
    return tgt.at[idx].add(src)

def _segment_sum(src, seg, n):
    return jax.ops.segment_sum(src, seg, n)
kernel_name = 'mk_vit_tower_cls_d2_tok_img512_r4_f201b2'

def setup_inputs(seed: int=0):
    np.random.seed(seed)
    _w = jnp.asarray

    def _rec_inputs():
        import jax
        import jax.numpy as jnp
        _rk = jax.random.key(seed)
        x = -0.000356955 + 1 * jax.random.normal(jax.random.fold_in(_rk, 1), (32, 3, 96, 96), jnp.float32)
        cls_tok = 0.02 * jax.random.normal(jax.random.fold_in(_rk, 5), (1, 1, 128), jnp.float32)
        return (x, cls_tok)
    x, cls_tok = _rec_inputs()

    def _L0_tok_setup():
        import jax, jax.numpy as jnp
        import numpy as np
        P = 16
        SHIFT = P // 2
        EPS = 1e-05

        def _shift2d(img, dy, dx):
            H, W = (img.shape[2], img.shape[3])
            pad = ((0, 0), (0, 0), (max(dy, 0), max(-dy, 0)), (max(dx, 0), max(-dx, 0)))
            z = jnp.pad(img, pad)
            return z[:, :, max(-dy, 0):max(-dy, 0) + H, max(-dx, 0):max(-dx, 0) + W]

        def _patchify(img):
            B, C, H, W = img.shape
            nH, nW = (H // P, W // P)
            t = img.reshape(B, C, nH, P, nW, P).transpose(0, 2, 4, 1, 3, 5)
            return t.reshape(B, nH * nW, C * P * P)
        key = jax.random.key(seed)
        ks = jax.random.split(key, 8)
        B, C, H, Wd = (128, 3, 224, 224)
        embed_dim = 128
        d_main = embed_dim // 2
        d_shift = embed_dim // 8
        fan_in = C * P * P
        std = 0.02
        x = jax.random.normal(ks[0], (B, C, H, Wd), dtype=jnp.float32)
        W_main = jax.random.normal(ks[1], (d_main, fan_in), dtype=jnp.float32) * std
        b_main = jnp.zeros((d_main,), dtype=jnp.float32)
        W_sx = jax.random.normal(ks[2], (d_shift, fan_in), dtype=jnp.float32) * std
        b_sx = jnp.zeros((d_shift,), dtype=jnp.float32)
        W_sy = jax.random.normal(ks[3], (d_shift, fan_in), dtype=jnp.float32) * std
        b_sy = jnp.zeros((d_shift,), dtype=jnp.float32)
        ln_g = jnp.ones((embed_dim,), dtype=jnp.float32)
        ln_b = jnp.zeros((embed_dim,), dtype=jnp.float32)
        return {'x': x, 'W_main': W_main, 'b_main': b_main, 'W_sx': W_sx, 'b_sx': b_sx, 'W_sy': W_sy, 'b_sy': b_sy, 'ln_g': ln_g, 'ln_b': ln_b}
    _L0_tok_all = _L0_tok_setup()
    _L0_tok_in = {k: v for k, v in _L0_tok_all.items() if k in ('W_main', 'b_main', 'W_sx', 'b_sx', 'W_sy', 'b_sy', 'ln_g', 'ln_b')}
    del _L0_tok_all

    def _L0_attn_setup():
        import jax, jax.numpy as jnp
        import numpy as np
        N_HEAD = 8
        D_MODEL = 128
        D_HEAD = D_MODEL // N_HEAD
        QLEN = 512
        BSZ = 4
        LN_EPS = 1e-05

        def _layer_norm(x, gamma, beta):
            mu = jnp.mean(x, axis=-1, keepdims=True)
            var = jnp.mean(jnp.square(x - mu), axis=-1, keepdims=True)
            return (x - mu) * jax.lax.rsqrt(var + LN_EPS) * gamma + beta

        def _pos_emb(qlen, d_model, dtype):
            pos_seq = jnp.arange(qlen - 1, -1, -1, dtype=dtype)
            inv_freq = 1.0 / 10000.0 ** (jnp.arange(0, d_model, 2, dtype=dtype) / d_model)
            sinusoid = pos_seq[:, None] * inv_freq[None, :]
            return jnp.concatenate([jnp.sin(sinusoid), jnp.cos(sinusoid)], axis=-1)

        def _rel_shift(x):
            q, r, b, n = x.shape
            x_padded = jnp.pad(x, ((0, 0), (1, 0), (0, 0), (0, 0)))
            x_padded = x_padded.reshape(r + 1, q, b, n)
            return x_padded[1:].reshape(q, r, b, n)
        key = jax.random.key(seed)
        ks = jax.random.split(key, 6)
        s = 0.02
        return {'w': jax.random.normal(ks[0], (QLEN, BSZ, D_MODEL), dtype=jnp.float32), 'Wqkv': jax.random.normal(ks[1], (3 * D_MODEL, D_MODEL), dtype=jnp.float32) * s, 'Wr': jax.random.normal(ks[2], (D_MODEL, D_MODEL), dtype=jnp.float32) * s, 'Wo': jax.random.normal(ks[3], (D_MODEL, D_MODEL), dtype=jnp.float32) * s, 'ln_gamma': jnp.ones((D_MODEL,), dtype=jnp.float32), 'ln_beta': jnp.zeros((D_MODEL,), dtype=jnp.float32), 'r_w_bias': jax.random.normal(ks[4], (N_HEAD, D_HEAD), dtype=jnp.float32) * s, 'r_r_bias': jax.random.normal(ks[5], (N_HEAD, D_HEAD), dtype=jnp.float32) * s}
    _L0_attn_all = _L0_attn_setup()
    _L0_attn_in = {k: v for k, v in _L0_attn_all.items() if k in ('Wqkv', 'Wr', 'Wo', 'ln_gamma', 'ln_beta', 'r_w_bias', 'r_r_bias')}
    del _L0_attn_all

    def _L0_ffn_setup():
        import jax, jax.numpy as jnp
        import numpy as np
        S, B, I, O, H, E, K = (128, 32, 128, 128, 128, 8, 2)

        def _expert(x_seq, Wi, Wh, b, Wo, bo):
            Bsz = x_seq.shape[1]
            Hd = Wh.shape[0]

            def step(carry, xt):
                h, c = carry
                gates = xt @ Wi + h @ Wh + b
                i_, f_, g_, o_ = jnp.split(gates, 4, axis=-1)
                c = jax.nn.sigmoid(f_) * c + jax.nn.sigmoid(i_) * jnp.tanh(g_)
                h = jax.nn.sigmoid(o_) * jnp.tanh(c)
                return ((h, c), h @ Wo + bo)
            init = (jnp.zeros((Bsz, Hd), x_seq.dtype), jnp.zeros((Bsz, Hd), x_seq.dtype))
            _, ys = jax.lax.scan(step, init, x_seq)
            return ys
        key = jax.random.key(seed)
        ks = jax.random.split(key, 6)
        s = 0.02
        return {'x': jax.random.normal(ks[0], (S, B, I), dtype=jnp.float32), 'router_w': jax.random.normal(ks[1], (I, E), dtype=jnp.float32) * s, 'router_b': jnp.zeros((E,), dtype=jnp.float32), 'Wi': jax.random.normal(ks[2], (E, I, 4 * H), dtype=jnp.float32) * s, 'Wh': jax.random.normal(ks[3], (E, H, 4 * H), dtype=jnp.float32) * s, 'b': jnp.zeros((E, 4 * H), dtype=jnp.float32), 'Wo': jax.random.normal(ks[4], (E, H, O), dtype=jnp.float32) * s, 'bo': jnp.zeros((E, O), dtype=jnp.float32)}
    _L0_ffn_all = _L0_ffn_setup()
    _L0_ffn_in = {k: v for k, v in _L0_ffn_all.items() if k in ('router_w', 'router_b', 'Wi', 'Wh', 'b', 'Wo', 'bo')}
    del _L0_ffn_all

    def _L1_attn_setup():
        import jax, jax.numpy as jnp
        import numpy as np
        import math
        CYCLES = [5, 6, 7, 8]

        def gamaka_pe(T, D):
            pos = np.arange(T, dtype=np.float32)[:, None]
            div = np.exp(np.arange(0, D, 2, dtype=np.float32) * (-math.log(10000.0) / D))
            pe = np.zeros((T, D), np.float32)
            pe[:, 0::2] = np.sin(pos * div)
            pe[:, 1::2] = np.cos(pos * div[:D // 2])
            tala = np.zeros((T, D), np.float32)
            slots = D // 4
            half = slots // 2
            harm = np.arange(1, half + 1, dtype=np.float32)
            for t_idx, c in enumerate(CYCLES):
                phase = pos % c / c * 2.0 * math.pi
                s = t_idx * slots
                tala[:, s:s + half] = np.sin(phase * harm)
                tala[:, s + half:s + slots] = np.cos(phase * harm)
            return jnp.asarray(0.5 * pe + 0.5 * tala)

        def layer_norm(x, g, b, eps=1e-05):
            m = x.mean(-1, keepdims=True)
            v = ((x - m) ** 2).mean(-1, keepdims=True)
            return (x - m) / jnp.sqrt(v + eps) * g + b

        def gru_all_threads(x, wih, whh, bih, bhh):
            xp = jnp.einsum('kij,btj->kbti', wih, x) + bih[:, None, None, :]
            K, B, T, _ = xp.shape
            D = x.shape[-1]

            def step(h, xt):
                gh = jnp.einsum('kij,kbj->kbi', whh, h) + bhh[:, None, :]
                xr, xz, xn = jnp.split(xt, 3, axis=-1)
                hr, hz, hn = jnp.split(gh, 3, axis=-1)
                r = jax.nn.sigmoid(xr + hr)
                z = jax.nn.sigmoid(xz + hz)
                n = jnp.tanh(xn + r * hn)
                h = (1.0 - z) * n + z * h
                return (h, h)
            h0 = jnp.zeros((K, B, D), x.dtype)
            _, hs = jax.lax.scan(step, h0, jnp.moveaxis(xp, 2, 0))
            return jnp.moveaxis(hs, 0, 2)
        key = jax.random.key(seed)
        ks = jax.random.split(key, 16)
        B, T, D = (4, 512, 128)
        s = 0.02
        return {'x': jax.random.normal(ks[0], (B, T, D), jnp.float32), 'gru_wih': s * jax.random.normal(ks[1], (4, 3 * D, D), jnp.float32), 'gru_whh': s * jax.random.normal(ks[2], (4, 3 * D, D), jnp.float32), 'gru_bih': s * jax.random.normal(ks[3], (4, 3 * D), jnp.float32), 'gru_bhh': s * jax.random.normal(ks[4], (4, 3 * D), jnp.float32), 'wq': s * jax.random.normal(ks[5], (4, D, D), jnp.float32), 'wk': s * jax.random.normal(ks[6], (4, D, D), jnp.float32), 'wv': s * jax.random.normal(ks[7], (4, D, D), jnp.float32), 'w_beat': s * jax.random.normal(ks[8], (4, D, 2 * D), jnp.float32), 'norm_g': jnp.ones((4, D), jnp.float32), 'norm_b': jnp.zeros((4, D), jnp.float32), 'w_mix': s * jax.random.normal(ks[9], (D, 4 * D), jnp.float32), 'bn_g': jnp.ones((D,), jnp.float32), 'bn_b': jnp.zeros((D,), jnp.float32)}
    _L1_attn_all = _L1_attn_setup()
    _L1_attn_in = {k: v for k, v in _L1_attn_all.items() if k in ('gru_wih', 'gru_whh', 'gru_bih', 'gru_bhh', 'wq', 'wk', 'wv', 'w_beat', 'norm_g', 'norm_b', 'w_mix', 'bn_g', 'bn_b')}
    del _L1_attn_all

    def _L1_ffn_setup():
        import jax, jax.numpy as jnp
        import numpy as np
        B, S, H, E, K, DF, SH = (8, 1024, 128, 8, 2, 128, 128)
        key = jax.random.key(seed)
        ks = jax.random.split(key, 10)
        n = lambda i, shape, sc: jax.random.normal(ks[i], shape, jnp.float32) * sc
        return {'hidden_states': n(0, (B, S, H), 1.0), 'gate_w': n(1, (E, H), 0.05), 'w1': n(2, (E, H, DF), 0.05), 'b1': n(3, (E, DF), 0.01), 'w2': n(4, (E, DF, H), 0.05), 'b2': n(5, (E, H), 0.01), 'sw1': n(6, (H, SH), 0.05), 'sb1': n(7, (SH,), 0.01), 'sw2': n(8, (SH, H), 0.05), 'sb2': n(9, (H,), 0.01)}
    _L1_ffn_all = _L1_ffn_setup()
    _L1_ffn_in = {k: v for k, v in _L1_ffn_all.items() if k in ('gate_w', 'w1', 'b1', 'w2', 'b2', 'sw1', 'sb1', 'sw2', 'sb2')}
    del _L1_ffn_all
    return {'x': x, 'cls_tok': cls_tok, 'L0_tok_W_main': _L0_tok_in['W_main'], 'L0_tok_b_main': _L0_tok_in['b_main'], 'L0_tok_W_sx': _L0_tok_in['W_sx'], 'L0_tok_b_sx': _L0_tok_in['b_sx'], 'L0_tok_W_sy': _L0_tok_in['W_sy'], 'L0_tok_b_sy': _L0_tok_in['b_sy'], 'L0_tok_ln_g': _L0_tok_in['ln_g'], 'L0_tok_ln_b': _L0_tok_in['ln_b'], 'L0_attn_Wqkv': _L0_attn_in['Wqkv'], 'L0_attn_Wr': _L0_attn_in['Wr'], 'L0_attn_Wo': _L0_attn_in['Wo'], 'L0_attn_ln_gamma': _L0_attn_in['ln_gamma'], 'L0_attn_ln_beta': _L0_attn_in['ln_beta'], 'L0_attn_r_w_bias': _L0_attn_in['r_w_bias'], 'L0_attn_r_r_bias': _L0_attn_in['r_r_bias'], 'L0_ffn_router_w': _L0_ffn_in['router_w'], 'L0_ffn_router_b': _L0_ffn_in['router_b'], 'L0_ffn_Wi': _L0_ffn_in['Wi'], 'L0_ffn_Wh': _L0_ffn_in['Wh'], 'L0_ffn_b': _L0_ffn_in['b'], 'L0_ffn_Wo': _L0_ffn_in['Wo'], 'L0_ffn_bo': _L0_ffn_in['bo'], 'L1_attn_gru_wih': _L1_attn_in['gru_wih'], 'L1_attn_gru_whh': _L1_attn_in['gru_whh'], 'L1_attn_gru_bih': _L1_attn_in['gru_bih'], 'L1_attn_gru_bhh': _L1_attn_in['gru_bhh'], 'L1_attn_wq': _L1_attn_in['wq'], 'L1_attn_wk': _L1_attn_in['wk'], 'L1_attn_wv': _L1_attn_in['wv'], 'L1_attn_w_beat': _L1_attn_in['w_beat'], 'L1_attn_norm_g': _L1_attn_in['norm_g'], 'L1_attn_norm_b': _L1_attn_in['norm_b'], 'L1_attn_w_mix': _L1_attn_in['w_mix'], 'L1_attn_bn_g': _L1_attn_in['bn_g'], 'L1_attn_bn_b': _L1_attn_in['bn_b'], 'L1_ffn_gate_w': _L1_ffn_in['gate_w'], 'L1_ffn_w1': _L1_ffn_in['w1'], 'L1_ffn_b1': _L1_ffn_in['b1'], 'L1_ffn_w2': _L1_ffn_in['w2'], 'L1_ffn_b2': _L1_ffn_in['b2'], 'L1_ffn_sw1': _L1_ffn_in['sw1'], 'L1_ffn_sb1': _L1_ffn_in['sb1'], 'L1_ffn_sw2': _L1_ffn_in['sw2'], 'L1_ffn_sb2': _L1_ffn_in['sb2']}

def reference(x, cls_tok, L0_tok_W_main, L0_tok_b_main, L0_tok_W_sx, L0_tok_b_sx, L0_tok_W_sy, L0_tok_b_sy, L0_tok_ln_g, L0_tok_ln_b, L0_attn_Wqkv, L0_attn_Wr, L0_attn_Wo, L0_attn_ln_gamma, L0_attn_ln_beta, L0_attn_r_w_bias, L0_attn_r_r_bias, L0_ffn_router_w, L0_ffn_router_b, L0_ffn_Wi, L0_ffn_Wh, L0_ffn_b, L0_ffn_Wo, L0_ffn_bo, L1_attn_gru_wih, L1_attn_gru_whh, L1_attn_gru_bih, L1_attn_gru_bhh, L1_attn_wq, L1_attn_wk, L1_attn_wv, L1_attn_w_beat, L1_attn_norm_g, L1_attn_norm_b, L1_attn_w_mix, L1_attn_bn_g, L1_attn_bn_b, L1_ffn_gate_w, L1_ffn_w1, L1_ffn_b1, L1_ffn_w2, L1_ffn_b2, L1_ffn_sw1, L1_ffn_sb1, L1_ffn_sw2, L1_ffn_sb2):
    import jax
    import jax.numpy as jnp

    def _L0_tok_ref(x, W_main, b_main, W_sx, b_sx, W_sy, b_sy, ln_g, ln_b):
        import jax, jax.numpy as jnp
        import numpy as np
        P = 16
        SHIFT = P // 2
        EPS = 1e-05

        def _shift2d(img, dy, dx):
            H, W = (img.shape[2], img.shape[3])
            pad = ((0, 0), (0, 0), (max(dy, 0), max(-dy, 0)), (max(dx, 0), max(-dx, 0)))
            z = jnp.pad(img, pad)
            return z[:, :, max(-dy, 0):max(-dy, 0) + H, max(-dx, 0):max(-dx, 0) + W]

        def _patchify(img):
            B, C, H, W = img.shape
            nH, nW = (H // P, W // P)
            t = img.reshape(B, C, nH, P, nW, P).transpose(0, 2, 4, 1, 3, 5)
            return t.reshape(B, nH * nW, C * P * P)

        def proj(img, W, b):
            return jnp.einsum('bnf,of->bno', _patchify(img), W) + b
        main = proj(x, W_main, b_main)
        xl = proj(_shift2d(x, 0, -SHIFT), W_sx, b_sx)
        xr = proj(_shift2d(x, 0, SHIFT), W_sx, b_sx)
        yu = proj(_shift2d(x, -SHIFT, 0), W_sy, b_sy)
        yd = proj(_shift2d(x, SHIFT, 0), W_sy, b_sy)
        tok = jnp.concatenate([main, xl, xr, yu, yd], axis=-1)
        mu = jnp.mean(tok, axis=-1, keepdims=True)
        var = jnp.mean(jnp.square(tok - mu), axis=-1, keepdims=True)
        return (tok - mu) * jax.lax.rsqrt(var + EPS) * ln_g + ln_b

    def _L0_attn_ref(w, Wqkv, Wr, Wo, ln_gamma, ln_beta, r_w_bias, r_r_bias):
        import jax, jax.numpy as jnp
        import numpy as np
        N_HEAD = 8
        D_MODEL = 128
        D_HEAD = D_MODEL // N_HEAD
        QLEN = 512
        BSZ = 4
        LN_EPS = 1e-05

        def _layer_norm(x, gamma, beta):
            mu = jnp.mean(x, axis=-1, keepdims=True)
            var = jnp.mean(jnp.square(x - mu), axis=-1, keepdims=True)
            return (x - mu) * jax.lax.rsqrt(var + LN_EPS) * gamma + beta

        def _pos_emb(qlen, d_model, dtype):
            pos_seq = jnp.arange(qlen - 1, -1, -1, dtype=dtype)
            inv_freq = 1.0 / 10000.0 ** (jnp.arange(0, d_model, 2, dtype=dtype) / d_model)
            sinusoid = pos_seq[:, None] * inv_freq[None, :]
            return jnp.concatenate([jnp.sin(sinusoid), jnp.cos(sinusoid)], axis=-1)

        def _rel_shift(x):
            q, r, b, n = x.shape
            x_padded = jnp.pad(x, ((0, 0), (1, 0), (0, 0), (0, 0)))
            x_padded = x_padded.reshape(r + 1, q, b, n)
            return x_padded[1:].reshape(q, r, b, n)
        qlen, bsz, d_model = w.shape
        scale = 1.0 / D_HEAD ** 0.5
        r = _pos_emb(qlen, d_model, w.dtype)
        wn = _layer_norm(w, ln_gamma, ln_beta)
        heads = jnp.einsum('ibd,ed->ibe', wn, Wqkv)
        q_h, k_h, v_h = jnp.split(heads, 3, axis=-1)
        q_h = q_h.reshape(qlen, bsz, N_HEAD, D_HEAD)
        k_h = k_h.reshape(qlen, bsz, N_HEAD, D_HEAD)
        v_h = v_h.reshape(qlen, bsz, N_HEAD, D_HEAD)
        r_k = jnp.einsum('rd,ed->re', r, Wr).reshape(qlen, N_HEAD, D_HEAD)
        AC = jnp.einsum('ibnd,jbnd->ijbn', q_h + r_w_bias, k_h)
        BD = _rel_shift(jnp.einsum('ibnd,jnd->ijbn', q_h + r_r_bias, r_k))
        attn_score = (AC + BD) * scale
        attn_prob = jax.nn.softmax(attn_score, axis=1)
        attn_vec = jnp.einsum('ijbn,jbnd->ibnd', attn_prob, v_h)
        attn_vec = attn_vec.reshape(qlen, bsz, N_HEAD * D_HEAD)
        attn_out = jnp.einsum('ibe,de->ibd', attn_vec, Wo)
        return w + attn_out

    def _L0_ffn_ref(x, router_w, router_b, Wi, Wh, b, Wo, bo):
        import jax, jax.numpy as jnp
        import numpy as np
        S, B, I, O, H, E, K = (128, 32, 128, 128, 128, 8, 2)

        def _expert(x_seq, Wi, Wh, b, Wo, bo):
            Bsz = x_seq.shape[1]
            Hd = Wh.shape[0]

            def step(carry, xt):
                h, c = carry
                gates = xt @ Wi + h @ Wh + b
                i_, f_, g_, o_ = jnp.split(gates, 4, axis=-1)
                c = jax.nn.sigmoid(f_) * c + jax.nn.sigmoid(i_) * jnp.tanh(g_)
                h = jax.nn.sigmoid(o_) * jnp.tanh(c)
                return ((h, c), h @ Wo + bo)
            init = (jnp.zeros((Bsz, Hd), x_seq.dtype), jnp.zeros((Bsz, Hd), x_seq.dtype))
            _, ys = jax.lax.scan(step, init, x_seq)
            return ys
        S_, B_, I_ = x.shape
        N = S_ * B_
        flat_x = x.reshape(N, I_)
        logits = flat_x @ router_w + router_b
        top_vals, top_idx = jax.lax.top_k(logits, K)
        rw = jax.nn.softmax(top_vals, axis=1)
        mask = (top_idx.T[:, None, :] == jnp.arange(E)[None, :, None]).astype(x.dtype)
        expert_x = (mask[..., None] * flat_x[None, None]).reshape(K, E, S_, B_, I_)
        run_e = jax.vmap(_expert, in_axes=(0, 0, 0, 0, 0, 0))
        run_ke = jax.vmap(run_e, in_axes=(0, None, None, None, None, None))
        out = run_ke(expert_x, Wi, Wh, b, Wo, bo)
        out = out.reshape(K, E, N, -1)
        y = jnp.einsum('ken,nk,keno->no', mask, rw, out)
        return y.reshape(S_, B_, -1)

    def _L1_attn_ref(x, gru_wih, gru_whh, gru_bih, gru_bhh, wq, wk, wv, w_beat, norm_g, norm_b, w_mix, bn_g, bn_b):
        import jax, jax.numpy as jnp
        import numpy as np
        import math
        CYCLES = [5, 6, 7, 8]

        def gamaka_pe(T, D):
            pos = np.arange(T, dtype=np.float32)[:, None]
            div = np.exp(np.arange(0, D, 2, dtype=np.float32) * (-math.log(10000.0) / D))
            pe = np.zeros((T, D), np.float32)
            pe[:, 0::2] = np.sin(pos * div)
            pe[:, 1::2] = np.cos(pos * div[:D // 2])
            tala = np.zeros((T, D), np.float32)
            slots = D // 4
            half = slots // 2
            harm = np.arange(1, half + 1, dtype=np.float32)
            for t_idx, c in enumerate(CYCLES):
                phase = pos % c / c * 2.0 * math.pi
                s = t_idx * slots
                tala[:, s:s + half] = np.sin(phase * harm)
                tala[:, s + half:s + slots] = np.cos(phase * harm)
            return jnp.asarray(0.5 * pe + 0.5 * tala)

        def layer_norm(x, g, b, eps=1e-05):
            m = x.mean(-1, keepdims=True)
            v = ((x - m) ** 2).mean(-1, keepdims=True)
            return (x - m) / jnp.sqrt(v + eps) * g + b

        def gru_all_threads(x, wih, whh, bih, bhh):
            xp = jnp.einsum('kij,btj->kbti', wih, x) + bih[:, None, None, :]
            K, B, T, _ = xp.shape
            D = x.shape[-1]

            def step(h, xt):
                gh = jnp.einsum('kij,kbj->kbi', whh, h) + bhh[:, None, :]
                xr, xz, xn = jnp.split(xt, 3, axis=-1)
                hr, hz, hn = jnp.split(gh, 3, axis=-1)
                r = jax.nn.sigmoid(xr + hr)
                z = jax.nn.sigmoid(xz + hz)
                n = jnp.tanh(xn + r * hn)
                h = (1.0 - z) * n + z * h
                return (h, h)
            h0 = jnp.zeros((K, B, D), x.dtype)
            _, hs = jax.lax.scan(step, h0, jnp.moveaxis(xp, 2, 0))
            return jnp.moveaxis(hs, 0, 2)
        B, T, D = x.shape
        x = x + gamaka_pe(T, D)[None]
        gru_out = gru_all_threads(x, gru_wih, gru_whh, gru_bih, gru_bhh)
        q = jnp.einsum('kij,btj->kbti', wq, x)
        k = jnp.einsum('kij,btj->kbti', wk, x)
        v = jnp.einsum('kij,btj->kbti', wv, x)
        idx = jnp.arange(T)
        diff = idx[:, None] - idx[None, :]
        cyc = jnp.asarray(CYCLES)[:, None, None]
        valid = (diff[None] >= 0) & (diff[None] < cyc)
        mask = jnp.where(valid, 0.0, -jnp.inf).astype(x.dtype)
        scores = jnp.einsum('kbtd,kbsd->kbts', q, k) / jnp.sqrt(jnp.asarray(D, x.dtype))
        attn = jax.nn.softmax(scores + mask[:, None], axis=-1)
        attn_out = jnp.einsum('kbts,kbsd->kbtd', attn, v)
        comb = jnp.concatenate([gru_out, attn_out], axis=-1)
        beat = jnp.einsum('kij,kbtj->kbti', w_beat, comb)
        thr = layer_norm(beat + x[None], norm_g[:, None, None, :], norm_b[:, None, None, :])
        merged = jnp.moveaxis(thr, 0, 2).reshape(B, T, 4 * D)
        out = jnp.einsum('ij,btj->bti', w_mix, merged)
        return layer_norm(out + x, bn_g, bn_b)

    def _L1_ffn_ref(hidden_states, gate_w, w1, b1, w2, b2, sw1, sb1, sw2, sb2):
        import jax, jax.numpy as jnp
        import numpy as np
        B, S, H, E, K, DF, SH = (8, 1024, 128, 8, 2, 128, 128)
        x = hidden_states
        xf = x.reshape(-1, x.shape[-1])
        T = xf.shape[0]
        scores = jax.nn.softmax(xf @ gate_w.T, axis=-1)
        topk_w, topk_i = jax.lax.top_k(scores, K)
        topk_w = topk_w / (topk_w.sum(-1, keepdims=True) + 1e-20)
        combine = jnp.zeros((T, E), xf.dtype).at[jnp.arange(T)[:, None], topk_i].add(topk_w)
        h1 = jax.nn.relu(jnp.einsum('th,ehf->tef', xf, w1) + b1)
        eo = jnp.einsum('tef,efh->teh', h1, w2) + b2
        y = jnp.einsum('te,teh->th', combine, eo)
        shared = jax.nn.relu(xf @ sw1 + sb1) @ sw2 + sb2
        return (y + shared).reshape(x.shape)
    h = _L0_tok_ref(x, L0_tok_W_main, L0_tok_b_main, L0_tok_W_sx, L0_tok_b_sx, L0_tok_W_sy, L0_tok_b_sy, L0_tok_ln_g, L0_tok_ln_b)
    h = jnp.concatenate([jnp.broadcast_to(cls_tok, (h.shape[0], 1, h.shape[2])), h], axis=1)
    h = h + _L0_attn_ref(_layernorm(h, axis=-1), L0_attn_Wqkv, L0_attn_Wr, L0_attn_Wo, L0_attn_ln_gamma, L0_attn_ln_beta, L0_attn_r_w_bias, L0_attn_r_r_bias)
    h = h + _L0_ffn_ref(_layernorm(h, axis=-1), L0_ffn_router_w, L0_ffn_router_b, L0_ffn_Wi, L0_ffn_Wh, L0_ffn_b, L0_ffn_Wo, L0_ffn_bo)
    h = h + _L1_attn_ref(_layernorm(h, axis=-1), L1_attn_gru_wih, L1_attn_gru_whh, L1_attn_gru_bih, L1_attn_gru_bhh, L1_attn_wq, L1_attn_wk, L1_attn_wv, L1_attn_w_beat, L1_attn_norm_g, L1_attn_norm_b, L1_attn_w_mix, L1_attn_bn_g, L1_attn_bn_b)
    h = h + _L1_ffn_ref(_layernorm(h, axis=-1), L1_ffn_gate_w, L1_ffn_w1, L1_ffn_b1, L1_ffn_w2, L1_ffn_b2, L1_ffn_sw1, L1_ffn_sb1, L1_ffn_sw2, L1_ffn_sb2)
    return h

_drawn_inputs = setup_inputs


def setup_inputs(seed=0):
    import zlib

    import numpy as np

    out = dict(_drawn_inputs(seed))
    spreads = {'L0_tok_b_main': (0.0, 0.1),
     'L0_tok_b_sx': (0.0, 0.1),
     'L0_tok_b_sy': (0.0, 0.1),
     'L0_tok_ln_g': (1.0, 0.2),
     'L0_tok_ln_b': (0.0, 0.1),
     'L0_attn_ln_gamma': (1.0, 0.6),
     'L0_attn_ln_beta': (0.0, 0.8),
     'L0_ffn_router_b': (0.0, 0.372),
     'L0_ffn_b': (0.0, 0.8),
     'L0_ffn_bo': (0.0, 0.315),
     'L1_attn_norm_g': (1.0, 0.6),
     'L1_attn_norm_b': (0.0, 0.571),
     'L1_attn_bn_g': (1.0, 0.2),
     'L1_attn_bn_b': (0.0, 0.305)}
    factors = {'L0_attn_Wqkv': 5.368,
     'L0_attn_Wr': 8.0,
     'L0_attn_Wo': 5.486,
     'L0_attn_r_w_bias': 8.0,
     'L0_attn_r_r_bias': 8.0,
     'L0_ffn_Wi': 8.0,
     'L0_ffn_Wh': 8.0,
     'L0_ffn_Wo': 6.339,
     'L1_attn_gru_wih': 7.875,
     'L1_attn_gru_whh': 28.955,
     'L1_attn_gru_bih': 64.0,
     'L1_attn_gru_bhh': 64.0,
     'L1_attn_wq': 8.0,
     'L1_attn_wk': 8.0,
     'L1_attn_wv': 8.0,
     'L1_attn_w_beat': 6.856,
     'L1_ffn_b1': 64.0,
     'L1_ffn_b2': 27.443,
     'L1_ffn_sb1': 51.839,
     'L1_ffn_sb2': 8.0}
    for name, (base, spread) in spreads.items():
        noise = np.random.default_rng([zlib.crc32(name.encode()), seed]).standard_normal(out[name].shape)
        drawn = base * np.exp(spread * noise) if base else spread * noise
        out[name] = jnp.asarray(drawn.astype(out[name].dtype))
    for name, factor in factors.items():
        out[name] = (out[name] * factor).astype(out[name].dtype)
    return out
```

```python
from contextlib import ExitStack

import numpy as np

import concourse.bass as bass
from concourse import mybir

F32 = mybir.dt.float32
BF16 = mybir.dt.bfloat16
U32 = mybir.dt.uint32
ALU = mybir.AluOpType
ACT = mybir.ActivationFunctionType
AX_X = mybir.AxisListType.X

P = 128
D = 128
IMGS = 32
TOK = 37
GRID = 6
PATCH = 16
NTOK = IMGS * TOK
TP = 3 * TOK
TILES = -(-NTOK // TP)
LAST = NTOK - (TILES - 1) * TP
COLS = TILES * TP
EPS = 1e-5
HEADS, DH = 8, 16
EXPERTS = 8
THREADS = 4
CYCLES = (5, 6, 7, 8)


def shape_constants():
    c = {}
    c["ident"] = np.eye(P, dtype=np.float32)
    sel = np.zeros((5, P, P), np.float32)
    sel[0] = np.eye(P)
    for m in range(16):
        sel[1, 80 + m, 64 + m] = 1
        sel[2, 64 + m, 80 + m] = 1
        sel[3, 112 + m, 96 + m] = 1
        sel[4, 96 + m, 112 + m] = 1
    c["shift_sel"] = sel.transpose(1, 0, 2).reshape(P, 5 * P)
    pos = np.arange(IMGS - 1, -1, -1, dtype=np.float32)
    inv = (1.0 / 10000.0 ** (np.arange(0, D, 2, dtype=np.float32) / D)).astype(np.float32)
    s = pos[:, None] * inv[None, :]
    c["rel_pos_t"] = np.concatenate([np.sin(s), np.cos(s)], -1).astype(np.float32).T
    c["head_mask"] = (np.arange(P)[:, None] // DH == np.arange(HEADS)[None, :]).astype(np.float32)
    c["head_rows"] = (np.arange(P)[:, None] % HEADS == np.arange(P)[None, :] // DH).astype(np.float32)
    t = np.arange(TOK, dtype=np.float32)[:, None]
    div = np.exp(np.arange(0, D, 2, dtype=np.float32) * np.float32(-np.log(10000.0) / D))
    pe = np.zeros((TOK, D), np.float32)
    pe[:, 0::2] = np.sin(t * div)
    pe[:, 1::2] = np.cos(t * div)
    tala = np.zeros((TOK, D), np.float32)
    slots = D // THREADS
    half = slots // 2
    harm = np.arange(1, half + 1, dtype=np.float32)
    for k, cyc in enumerate(CYCLES):
        phase = t % cyc / cyc * 2.0 * np.pi
        tala[:, k * slots:k * slots + half] = np.sin(phase * harm)
        tala[:, k * slots + half:(k + 1) * slots] = np.cos(phase * harm)
    c["pos_code"] = np.concatenate([np.tile(0.5 * pe + 0.5 * tala, (3, 1)), np.zeros((P - TP, D))], 0).astype(np.float32)
    a = np.arange(TP)
    diff = a[:, None] - a[None, :]
    same = a[:, None] // TOK == a[None, :] // TOK
    win = np.full((P, THREADS, TP), -1e30, np.float32)
    for k, cyc in enumerate(CYCLES):
        win[:TP, k] = np.where(same & (diff >= 0) & (diff < cyc), 0.0, -1e30)
    c["window"] = win.reshape(P, THREADS * TP)
    r = np.zeros((P, 18, P), np.float32)
    for j in range(18):
        r[j, j, :] = 1
    c["row_sel"] = r.reshape(P, 18 * P)
    c["ident_rep"] = np.repeat(np.eye(P, dtype=np.float32), HEADS, axis=1)
    c["gate_half"] = np.where(np.arange(P) % 4 == 2, 1.0, 0.5).astype(np.float32)[:, None]
    c["gru_facts"] = np.stack([(np.arange(P) % 3 < 2), np.ones(P)], 1).astype(np.float32)
    c["iota8"] = np.tile(np.arange(8, dtype=np.float32), (P, 1))
    return c


CONSTS = shape_constants()
CONST_AT = {}
_at = 0
for _n, _a in CONSTS.items():
    CONST_AT[_n] = (_at, _a.shape[1])
    _at += _a.shape[1]
CONST_COLS = _at


class Counts:

    def __init__(self, eng):
        self.eng, self.n = eng, {}

    def chain(self, sem, ins):
        ins.then_inc(sem, 1)
        self.n[sem.name] = self.n.get(sem.name, 0) + 1
        self.eng.wait_ge(sem, self.n[sem.name])


SEMAPHORES = []


def clear_semaphores(nc):
    nc.clear_and_free_semaphores(list(SEMAPHORES))
    SEMAPHORES.clear()
    nc.all_engine_barrier()


class Stage:

    def __init__(self, nc, ctx, tag):
        self.nc, self.ctx, self.tag = nc, ctx, tag

    def sb(self, name, shape, dt=F32):
        return self.ctx.enter_context(self.nc.sbuf_tensor(f"{self.tag}_{name}", shape, dt))

    def ps(self, name, banks=8):
        return self.ctx.enter_context(self.nc.psum_tensor(f"{self.tag}_{name}", [P, banks, 512], F32))

    def sem(self, name):
        s = self.nc.alloc_semaphore(f"{self.tag}_{name}")
        SEMAPHORES.append(s)
        return s


def const(c_all, name, rows=P):
    at, n = CONST_AT[name]
    return c_all[0:rows, at:at + n]


def rows_view(dram):
    full = dram[0:(TILES - 1) * TP, :].rearrange("(t p) d -> p t d", p=TP)
    return full, dram[(TILES - 1) * TP:NTOK, :]


def row_stats(c, s_v, nc, src, stats, mv, tiles=TILES):
    for t in range(tiles):
        ins = nc.vector.bn_stats(stats[:, t, :], src[:, t, :])
    c.chain(s_v, ins)
    for t in range(tiles):
        ins = nc.vector.bn_aggr(mv[:, t, :], stats[:, t, :])
    c.chain(s_v, ins)


def tok_stage(nc, a, h_dram):
    NQ = 6
    HALF = 3 * IMGS
    SIDE = GRID + 1
    CELL = SIDE * SIDE
    CELLS = IMGS * CELL
    GUARD = SIDE + 1
    GT = 14
    GP = CELLS // GT
    with ExitStack() as ctx:
        st = Stage(nc, ctx, "tok")
        ident = st.sb("ident", [P, P])
        sel = st.sb("sel", [P, 5, P])
        wn = st.sb("wn", [P, 3 * 256])
        wt = st.sb("wt", [P, NQ, P])
        img = st.sb("img", [HALF, 2, 3, PATCH * 96])
        pat = st.sb("pat", [HALF, 2, 3, GRID, PATCH * PATCH])
        xt = st.sb("xt", [P, NQ, 4, 3 * HALF])
        grid = st.sb("grid", [P, GUARD + CELLS + GUARD])
        bias = st.sb("bias", [P, D])
        gain = st.sb("gain", [P, D])
        beta = st.sb("beta", [P, D])
        tok = st.sb("tok", [GP, GT, D])
        outp = st.sb("outp", [GP, GT, D])
        stats = st.sb("stats", [GP, GT, 6])
        mv = st.sb("mv", [GP, GT, 2])
        std = st.sb("std", [GP, GT, 1])
        rstd = st.sb("rstd", [GP, GT, 1])
        cls = st.sb("cls", [IMGS, D])
        ps = st.ps("ps")
        s_const, s_w, s_row, s_cls = st.sem("const"), st.sem("w"), st.sem("row"), st.sem("cls")
        s_img = [st.sem(f"img{u}") for u in range(2)]
        s_zero, s_v, s_a = st.sem("zero"), st.sem("v"), st.sem("a")
        s_wtp, s_wt = st.sem("wtp"), st.sem("wt")
        s_tp, s_xt_v, s_xt_a = st.sem("tp"), st.sem("xt_v"), st.sem("xt_a")
        s_pr, s_grid = st.sem("pr"), st.sem("grid")
        s_sh, s_tok = st.sem("sh"), st.sem("tok")
        s_mv, s_std, s_outp, s_out = st.sem("mv"), st.sem("std"), st.sem("outp"), st.sem("out")
        s_pad, s_pat = st.sem("pad"), [st.sem(f"pat{u}") for u in range(2)]

        xi = a["x"].rearrange("b c (i p) w -> b c i (p w)", p=PATCH)
        padded = nc.dram_tensor("grid_rows", (CELLS, D), F32, kind="Internal").ap()

        block = ctx.enter_context(nc.Block())

        @block.sync
        def _(sp):
            for u in range(2):
                for k in range(3):
                    sp.dma_start(img[32 * k:32 * k + 32, u, :, :], xi[:, :, 3 * u + k, :]).then_inc(s_img[u], 16)
            sp.wait_ge(s_std, 1)
            sp.wait_ge(s_cls, 16)
            hv = h_dram.rearrange("(b t) d -> b t d", t=TOK)
            sp.dma_start(hv[:, 0, :], cls[:, :]).then_inc(s_out, 16)
            for n in range(2):
                sp.wait_ge(s_outp, n + 1)
                half = slice(n * GT // 2, (n + 1) * GT // 2)
                sp.dma_start(padded.rearrange("(t p) d -> p t d", p=GP)[:, half, :], outp[:, half, :]).then_inc(s_pad, 16)
            sp.wait_ge(s_pad, 32)
            pv = padded.rearrange("(b i j) d -> b i j d", i=SIDE, j=SIDE)
            for i in range(GRID):
                sp.dma_start(hv[:, 1 + GRID * i:1 + GRID * i + GRID, :], pv[:, i, 0:GRID, :]).then_inc(s_out, 16)
            sp.wait_ge(s_out, 16 * (1 + GRID))

        @block.scalar
        def _(act):
            act.dma_start(ident[:], const(a["consts"], "ident")).then_inc(s_const, 16)
            act.wait_ge(s_zero, 1)
            act.dma_start(wn[0:64, :], a["L0_tok_W_main"]).then_inc(s_w, 16)
            wx = a["L0_tok_W_sx"].rearrange("o (r j) -> o r j", j=PATCH)
            wnx = wn[:, :].rearrange("o (r j) -> o r j", j=PATCH)
            act.dma_start(wnx[64:80, :, 8:16], wx[:, :, 0:8]).then_inc(s_w, 16)
            act.dma_start(wnx[80:96, :, 0:8], wx[:, :, 8:16]).then_inc(s_w, 16)
            wy = a["L0_tok_W_sy"].rearrange("o (c h r) -> o c h r", c=3, h=2)
            wny = wn[:, :].rearrange("o (c h r) -> o c h r", c=3, h=2)
            act.dma_start(wny[96:112, :, 1, :], wy[:, :, 0, :]).then_inc(s_w, 16)
            act.dma_start(wny[112:128, :, 0, :], wy[:, :, 1, :]).then_inc(s_w, 16)
            act.dma_start(sel[:], const(a["consts"], "shift_sel").rearrange("p (s m) -> p s m", s=5)).then_inc(s_const, 16)
            at = 0
            for nm, w in (("L0_tok_b_main", 64), ("L0_tok_b_sx", 16), ("L0_tok_b_sx", 16), ("L0_tok_b_sy", 16), ("L0_tok_b_sy", 16)):
                act.dma_start(bias[:, at:at + w], a[nm].partition_broadcast(P)).then_inc(s_row, 16)
                at += w
            act.dma_start(gain[:], a["L0_tok_ln_g"].partition_broadcast(P)).then_inc(s_row, 16)
            act.dma_start(beta[:], a["L0_tok_ln_b"].partition_broadcast(P)).then_inc(s_row, 16)
            act.dma_start(cls[:], a["cls_tok"].rearrange("a b d -> (a b d)").partition_broadcast(IMGS)).then_inc(s_cls, 16)
            for u in range(2):
                act.wait_ge(s_img[u], 48)
                nc.scalar.copy(pat[:, u, 2, :, :].rearrange("p j (r e) -> p j r e", e=PATCH),
                               img[:, u, 2, :].rearrange("p (r j e) -> p j r e", r=PATCH, j=GRID)).then_inc(s_pat[u], 1)
            for n in range(1, 24, 2):
                act.wait_ge(s_tp, n + 1)
                nc.scalar.copy(xt[:, n % NQ, n // NQ, :], ps[:, n % 4, 0:3 * HALF]).then_inc(s_xt_a, 1)
            act.wait_ge(s_mv, 1)
            nc.scalar.activation(std[:, :, 0], mv[:, :, 1], ACT.Sqrt).then_inc(s_std, 1)

        @block.tensor
        def _(pe):
            pe.wait_ge(s_const, 32)
            pe.wait_ge(s_w, 80)
            for q in range(NQ):
                last = nc.tensor.transpose(ps[:, 4 + q // 4, (q % 4) * P:(q % 4) * P + P], wn[:, q * P:(q + 1) * P], ident[:])
            last.then_inc(s_wtp, 1)
            for n in range(24):
                u, jg, q = n // 12, (n // NQ) % 2, n % NQ
                if n % 12 == 0:
                    pe.wait_ge(s_pat[u], 3)
                if n >= 4:
                    if n % 2:
                        pe.wait_ge(s_xt_a, (n - 4) // 2 + 1)
                    else:
                        pe.wait_ge(s_xt_v, (n - 4) // 2 + 1)
                for k in range(3):
                    src = pat[:, u, q // 2, 3 * jg + k, P * (q % 2):P * (q % 2) + P]
                    last = nc.tensor.transpose(ps[:, n % 4, k * HALF:(k + 1) * HALF], src, ident[0:HALF, 0:HALF])
                last.then_inc(s_tp, 1)
            pe.wait_ge(s_wt, 2)
            for g in range(4):
                for q in range(NQ):
                    n = g * NQ + q
                    if n % 2:
                        pe.wait_ge(s_xt_a, n // 2 + 1)
                    else:
                        pe.wait_ge(s_xt_v, n // 2 + 1)
                    last = nc.tensor.matmul(ps[:, 4 + g, 0:3 * HALF], wt[:, q, :], xt[:, q, g, :], start=(q == 0), stop=(q == NQ - 1))
                last.then_inc(s_pr, 1)
            pe.wait_ge(s_grid, 4)
            for t in range(GT):
                if t >= 4:
                    pe.wait_ge(s_tok, t - 3)
                for k, step in enumerate((0, 1, -1, SIDE, -SIDE)):
                    at = GUARD + t * GP + step
                    last = nc.tensor.matmul(ps[0:GP, t % 4, 0:P], grid[:, at:at + GP], sel[:, k, :], start=(k == 0), stop=(k == 4))
                last.then_inc(s_sh, 1)

        @block.vector
        def _(v):
            c = Counts(v)
            nc.vector.memset(wn[:], 0.0).then_inc(s_zero, 1)
            c.chain(s_v, nc.vector.memset(grid[:], 0.0))
            for u in range(2):
                v.wait_ge(s_img[u], 48)
                for ch in range(2):
                    nc.vector.tensor_copy(pat[:, u, ch, :, :].rearrange("p j (r e) -> p j r e", e=PATCH),
                                          img[:, u, ch, :].rearrange("p (r j e) -> p j r e", r=PATCH, j=GRID)).then_inc(s_pat[u], 1)
            v.wait_ge(s_wtp, 1)
            nc.vector.tensor_copy(wt[:, 0:4, :].rearrange("p q m -> p (q m)"), ps[:, 4, 0:512]).then_inc(s_wt, 1)
            nc.vector.tensor_copy(wt[:, 4:6, :].rearrange("p q m -> p (q m)"), ps[:, 5, 0:256]).then_inc(s_wt, 1)
            for n in range(0, 24, 2):
                v.wait_ge(s_tp, n + 1)
                nc.vector.tensor_copy(xt[:, n % NQ, n // NQ, :], ps[:, n % 4, 0:3 * HALF]).then_inc(s_xt_v, 1)
            for g in range(4):
                u, jg = g // 2, g % 2
                v.wait_ge(s_pr, g + 1)
                for k in range(3):
                    cells = grid[:, GUARD:GUARD + CELLS].rearrange("p (b i j) -> p b i j", i=SIDE, j=SIDE)
                    dst = cells[:, :, 3 * u:3 * u + 3, 3 * jg + k].rearrange("p b i -> p i b")
                    ins = nc.vector.tensor_copy(dst, ps[:, 4 + g, k * HALF:(k + 1) * HALF].rearrange("p (i b) -> p i b", i=3))
                ins.then_inc(s_grid, 1)
            v.wait_ge(s_row, 16 * 7)
            for t in range(GT):
                v.wait_ge(s_sh, t + 1)
                c.chain(s_tok, nc.vector.tensor_tensor(tok[:, t, :], ps[0:GP, t % 4, 0:P], bias[0:GP, :], ALU.add))
            row_stats(c, s_v, nc, tok, stats, mv, GT)
            c.chain(s_v, nc.vector.tensor_scalar(mv[:, :, 1:2], mv[:, :, 1:2], EPS, None, ALU.add))
            c.chain(s_mv, nc.vector.tensor_copy(std[0:1, 0, :], mv[0:1, 0, 1:2]))
            v.wait_ge(s_std, 1)
            c.chain(s_v, nc.vector.reciprocal(rstd[:, :, 0], std[:, :, 0]))
            for t in range(GT):
                ins = nc.vector.tensor_scalar(outp[:, t, :], tok[:, t, :], mv[:, t, 0:1], rstd[:, t, :], ALU.subtract, ALU.mult)
            c.chain(s_v, ins)
            for n in range(2):
                half = slice(n * GT // 2, (n + 1) * GT // 2)
                c.chain(s_v, nc.vector.tensor_tensor(outp[:, half, :], outp[:, half, :], gain[0:GP, :].unsqueeze(1).to_broadcast([GP, GT // 2, D]), ALU.mult))
                c.chain(s_outp, nc.vector.tensor_tensor(outp[:, half, :], outp[:, half, :], beta[0:GP, :].unsqueeze(1).to_broadcast([GP, GT // 2, D]), ALU.add))


class Norm:

    def __init__(self, st, name, rows, tiles):
        self.rows, self.tiles = rows, tiles
        self.stats = st.sb(f"{name}_stats", [rows, tiles, 6])
        self.mv = st.sb(f"{name}_mv", [rows, tiles, 2])
        self.var = st.sb(f"{name}_var", [rows, tiles])
        self.std = st.sb(f"{name}_std", [rows, tiles])
        self.rstd = st.sb(f"{name}_rstd", [rows, tiles])
        self.s_var = st.sem(f"{name}_var_ready")
        self.s_std = st.sem(f"{name}_std_ready")

    def vector(self, nc, v, c, s_v, src, dst, s_dst=None, turn=1):
        row_stats(c, s_v, nc, src, self.stats, self.mv, self.tiles)
        c.chain(self.s_var, nc.vector.tensor_scalar(self.var[:], self.mv[:, :, 1], EPS, None, ALU.add))
        v.wait_ge(self.s_std, turn)
        c.chain(s_v, nc.vector.reciprocal(self.rstd[:], self.std[:]))
        for t in range(self.tiles):
            ins = nc.vector.tensor_scalar(dst[:, t, :], src[:, t, :], self.mv[:, t, 0:1], self.rstd[:, t:t + 1],
                                          ALU.subtract, ALU.mult)
            if s_dst is not None:
                ins.then_inc(s_dst, 1)
        if s_dst is None:
            c.chain(s_v, ins)
        else:
            v.wait_ge(s_dst, turn * self.tiles)

    def scalar(self, nc, act, turn=1):
        act.wait_ge(self.s_var, turn)
        nc.scalar.activation(self.std[:], self.var[:], ACT.Sqrt).then_inc(self.s_std, 1)


def load_rows(eng, dst, dram, sem):
    full, last = rows_view(dram)
    eng.dma_start(dst[:, 0:TILES - 1, :], full).then_inc(sem, 16)
    eng.dma_start(dst[0:LAST, TILES - 1, :], last).then_inc(sem, 16)


def rel_attn_stage(nc, a, h_dram, resid):
    NB = 40
    QT = NB // 4
    HJ = HEADS * IMGS
    PITCH = (IMGS + 1) * HEADS
    with ExitStack() as ctx:
        st = Stage(nc, ctx, "rel")
        ident = st.sb("ident", [P, P])
        rep = st.sb("rep", [P, P * HEADS])
        hmask = st.sb("hmask", [P, HEADS])
        hrows = st.sb("hrows", [P, P])
        post = st.sb("post", [P, IMGS])
        wnat = st.sb("wnat", [P, 5, P])
        wt = st.sb("wt", [P, 5, P])
        cols = st.sb("cols", [P, 4])
        w = st.sb("w", [TP, TILES, D])
        wn = st.sb("wn", [TP, TILES, D])
        wnt = st.sb("wnt", [P, NB, IMGS])
        qw = st.sb("qw", [P, NB * IMGS])
        qr = st.sb("qr", [P, NB * IMGS])
        kexp = st.sb("kexp", [P, NB * IMGS, HEADS])
        rk = st.sb("rk", [P, IMGS])
        rexp = st.sb("rexp", [P, IMGS, HEADS])
        bdp = st.sb("bdp", [P, QT, PITCH])
        bds = st.sb("bds", [P, QT, HJ])
        vrow = st.sb("vrow", [P, QT, P])
        vexp = st.sb("vexp", [P, NB * 2, P])
        sc = st.sb("sc", [P, 2, HJ])
        mx = st.sb("mx", [P, 2, HEADS])
        pr = st.sb("pr", [P, 2, HJ])
        den = st.sb("den", [P, 2, HEADS])
        rden = st.sb("rden", [P, 4, HEADS])
        pt = st.sb("pt", [P, 2, 2, P])
        av = st.sb("av", [P, 2, P])
        avt = st.sb("avt", [P, 2, P])
        ao = st.sb("ao", [P, QT, P])
        aor = st.sb("aor", [TP, TILES, D])
        ps = st.ps("ps")
        ln1, ln2 = Norm(st, "ln1", TP, TILES), Norm(st, "ln2", TP, TILES)
        names = ("const", "w", "h", "zero", "v", "wn", "wnt_tp", "wnt", "wt_tp", "wt", "rk", "rexp", "q", "qr", "k", "kx",
                 "v_mm", "v_sb", "vr", "vx", "bd", "bd_sb", "bd_out", "bd_in", "ac", "s", "sub", "e", "den", "pt", "pt_sb",
                 "pv", "av", "avt", "avt_sb", "wo", "ao", "ao_out", "ao_in")
        S = {n: st.sem(n) for n in names}
        bd_dram = nc.dram_tensor("rel_pos_scores", (NB, IMGS * PITCH), F32, kind="Internal").ap()
        ao_dram = nc.dram_tensor("rel_out_rows", (NTOK, D), F32, kind="Internal").ap()
        block = ctx.enter_context(nc.Block())

        @block.sync
        def _(sp):
            sp.wait_ge(S["zero"], 1)
            load_rows(sp, resid, h_dram, S["h"])
            sp.dma_start(ident[:], const(a["consts"], "ident")).then_inc(S["const"], 16)
            sp.dma_start(post[:], const(a["consts"], "rel_pos_t")).then_inc(S["const"], 16)
            sp.dma_start(hmask[:], const(a["consts"], "head_mask")).then_inc(S["const"], 16)
            sp.dma_start(hrows[:], const(a["consts"], "head_rows")).then_inc(S["const"], 16)
            sp.dma_start(rep[:], const(a["consts"], "ident_rep")).then_inc(S["const"], 16)
            sp.wait_ge(S["bd_sb"], QT // 2)
            sp.dma_start(bd_dram.rearrange("n (i c) -> (n i) c", i=IMGS).rearrange("(t p) c -> p t c", p=P), bdp[:]).then_inc(S["bd_out"], 16)
            sp.wait_ge(S["bd_out"], 16)
            shifted = bd_dram[:, HJ:HJ + IMGS * HJ].rearrange("(t b) (i c) -> b i t c", b=4, i=IMGS)
            for b in range(4):
                sp.dma_start(bds[32 * b:32 * b + 32, :, :], shifted[b]).then_inc(S["bd_in"], 16)
            sp.wait_ge(S["ao"], QT)
            dst = ao_dram.rearrange("(i n) d -> i n d", n=TOK)
            for b in range(4):
                n = QT if b == 0 else QT - 1
                sp.dma_start(dst[:, b:b + 4 * (n - 1) + 1:4, :], ao[32 * b:32 * b + 32, 0:n, :]).then_inc(S["ao_out"], 16)
            sp.wait_ge(S["ao_out"], 64)
            load_rows(sp, aor, ao_dram, S["ao_in"])

        @block.scalar
        def _(act):
            for k in range(3):
                act.dma_start(wnat[:, k, :], a["L0_attn_Wqkv"][k * D:(k + 1) * D, :]).then_inc(S["w"], 16)
            act.dma_start(wnat[:, 3, :], a["L0_attn_Wr"]).then_inc(S["w"], 16)
            act.dma_start(wnat[:, 4, :], a["L0_attn_Wo"]).then_inc(S["w"], 16)
            act.dma_start(cols[:, 0:1], a["L0_attn_ln_gamma"].rearrange("(d o) -> d o", o=1)).then_inc(S["w"], 16)
            act.dma_start(cols[:, 1:2], a["L0_attn_ln_beta"].rearrange("(d o) -> d o", o=1)).then_inc(S["w"], 16)
            act.dma_start(cols[:, 2:3], a["L0_attn_r_w_bias"].rearrange("n (d o) -> (n d) o", o=1)).then_inc(S["w"], 16)
            act.dma_start(cols[:, 3:4], a["L0_attn_r_r_bias"].rearrange("n (d o) -> (n d) o", o=1)).then_inc(S["w"], 16)
            ln1.scalar(nc, act)
            ln2.scalar(nc, act)
            act.wait_ge(S["w"], 16 * 9)
            for n in range(3):
                act.wait_ge(S["q"], n + 1)
                wd = min(512, NB * IMGS - 512 * n)
                nc.scalar.activation(qr[:, 512 * n:512 * n + wd], ps[:, n, 0:wd], ACT.Identity, bias=cols[:, 3:4]).then_inc(S["qr"], 1)
            for n in range(5):
                act.wait_ge(S["bd"], 2 * n + 2)
                nc.scalar.copy(bdp[:, 2 * n:2 * n + 2, HEADS:PITCH], ps[:, 4 + n % 2, :].rearrange("p (t c) -> p t c", t=2)).then_inc(S["bd_sb"], 1)
            for n in range(3):
                act.wait_ge(S["v_mm"], n + 1)
                wd = min(4, QT - 4 * n)
                nc.scalar.copy(vrow[:, 4 * n:4 * n + wd, :].rearrange("p t d -> p (t d)"), ps[:, 6 + n % 2, 0:wd * P]).then_inc(S["v_sb"], 1)
            for t in range(QT + 5):
                if t < QT:
                    act.wait_ge(S["sub"], t + 1)
                    if t >= 2:
                        act.wait_ge(S["pt"], t - 1)
                        act.wait_ge(S["den"], t - 1)
                    nc.scalar.activation(pr[:, t % 2, :], sc[:, t % 2, :], ACT.Exp, scale=float(DH) ** -0.5).then_inc(S["e"], 1)
                u = t - 1
                if 0 <= u < QT:
                    act.wait_ge(S["pt"], u + 1)
                    if u >= 2:
                        act.wait_ge(S["pv"], u - 1)
                    nc.scalar.copy(pt[:, u % 2, :, :].rearrange("p a b -> p (a b)"), ps[:, 2 + u % 2, 0:2 * P]).then_inc(S["pt_sb"], 1)
                u = t - 3
                if 0 <= u < QT:
                    act.wait_ge(S["avt"], u + 1)
                    if u >= 2:
                        act.wait_ge(S["wo"], u - 1)
                    nc.scalar.copy(avt[:, u % 2, :], ps[:, 6, 0:P]).then_inc(S["avt_sb"], 1)
                u = t - 4
                if 0 <= u < QT:
                    act.wait_ge(S["wo"], u + 1)
                    nc.scalar.copy(ao[:, u, :], ps[:, 7, 0:P]).then_inc(S["ao"], 1)

        @block.tensor
        def _(pe):
            pe.wait_ge(S["const"], 80)
            pe.wait_ge(S["w"], 16 * 9)
            for k in range(5):
                last = nc.tensor.transpose(ps[:, 6 + k // 4, (k % 4) * P:(k % 4) * P + P], wnat[:, k, :], ident[:])
            last.then_inc(S["wt_tp"], 1)
            for t in range(TILES):
                pe.wait_ge(S["wn"], t + 1)
                last = nc.tensor.transpose(ps[:, 3 + t // 4, (t % 4) * TP:(t % 4) * TP + TP], wn[:, t, :], ident[0:TP, 0:TP])
                if t % 4 == 3 or t == TILES - 1:
                    last.then_inc(S["wnt_tp"], 1)
            pe.wait_ge(S["wt"], 1)
            nc.tensor.matmul(ps[:, 7, 128:128 + IMGS], wt[:, 3, :], post[:], start=True, stop=True).then_inc(S["rk"], 1)
            flat = wnt[:].rearrange("p n i -> p (n i)")
            pe.wait_ge(S["wnt"], 3)
            for n in range(3):
                wd = min(512, NB * IMGS - 512 * n)
                nc.tensor.matmul(ps[:, n, 0:wd], wt[:, 0, :], flat[:, 512 * n:512 * n + wd], start=True, stop=True).then_inc(S["q"], 1)
            for n in range(3):
                wd = min(512, NB * IMGS - 512 * n)
                nc.tensor.matmul(ps[:, 3 + n, 0:wd], wt[:, 1, :], flat[:, 512 * n:512 * n + wd], start=True, stop=True).then_inc(S["k"], 1)
            pe.wait_ge(S["kx"], 3)
            pe.wait_ge(S["rexp"], 2)
            pe.wait_ge(S["qr"], 3)
            for t in range(QT):
                if t % 2 == 0 and t >= 4:
                    pe.wait_ge(S["bd_sb"], t // 2 - 1)
                nc.tensor.matmul(ps[:, 4 + (t // 2) % 2, (t % 2) * HJ:(t % 2) * HJ + HJ], qr[:, t * P:(t + 1) * P],
                                 rexp[:].rearrange("p j n -> p (j n)"), start=True, stop=True).then_inc(S["bd"], 1)
            for t in range(QT):
                if t == 8:
                    pe.wait_ge(S["v_sb"], 1)
                last = nc.tensor.matmul(ps[:, 6 + (t // 4) % 2, (t % 4) * P:(t % 4) * P + P], flat[:, t * P:(t + 1) * P], wt[:, 2, :], start=True, stop=True)
                if t % 4 == 3 or t == QT - 1:
                    last.then_inc(S["v_mm"], 1)
            pe.wait_ge(S["v_sb"], 3)
            pe.wait_ge(S["bd_sb"], 5)
            for n in range(2 * NB):
                t, b, half = n // 8, (n // 2) % 4, n % 2
                if n % 4 == 0 and n >= 8:
                    pe.wait_ge(S["vx"], n // 4 - 1)
                at = (32 * b + 16 * half) * HEADS
                last = nc.tensor.matmul(ps[:, 4 + (n // 4) % 2, (n % 4) * P:(n % 4) * P + P], rep[:, at:at + P], vrow[:, t, :], start=True, stop=True)
                if n % 4 == 3:
                    last.then_inc(S["vr"], 1)
            pe.wait_ge(S["vx"], 2 * NB // 4)
            for t in range(QT + 4):
                if t < QT:
                    if t >= 2:
                        pe.wait_ge(S["s"], t - 1)
                    for b in range(4):
                        tok = 4 * t + b
                        last = nc.tensor.matmul(ps[32 * b:32 * b + 32, t % 2, 0:HJ], qw[:, tok * IMGS:(tok + 1) * IMGS],
                                                kexp[:, tok * IMGS:(tok + 1) * IMGS, :].rearrange("p j n -> p (j n)"), start=True, stop=True)
                    last.then_inc(S["ac"], 1)
                u = t - 1
                if 0 <= u < QT:
                    pe.wait_ge(S["e"], u + 1)
                    if u >= 2:
                        pe.wait_ge(S["pt_sb"], u - 1)
                    for half in range(2):
                        last = nc.tensor.transpose(ps[:, 2 + u % 2, half * P:half * P + P], pr[:, u % 2, half * P:half * P + P], ident[:])
                    last.then_inc(S["pt"], 1)
                u = t - 2
                if 0 <= u < QT:
                    pe.wait_ge(S["pt_sb"], u + 1)
                    if u >= 2:
                        pe.wait_ge(S["av"], u - 1)
                    for b in range(4):
                        for half in range(2):
                            last = nc.tensor.matmul(ps[32 * b:32 * b + 32, 4 + u % 2, 0:P], pt[:, u % 2, half, 32 * b:32 * b + 32],
                                                    vexp[:, (4 * u + b) * 2 + half, :], start=(half == 0), stop=(half == 1))
                    last.then_inc(S["pv"], 1)
                u = t - 3
                if 0 <= u < QT:
                    pe.wait_ge(S["av"], u + 1)
                    if u >= 1:
                        pe.wait_ge(S["avt_sb"], u)
                    nc.tensor.transpose(ps[:, 6, 0:P], av[:, u % 2, :], ident[:]).then_inc(S["avt"], 1)
                u = t - 4
                if 0 <= u < QT:
                    pe.wait_ge(S["avt_sb"], u + 1)
                    if u >= 1:
                        pe.wait_ge(S["ao"], u)
                    nc.tensor.matmul(ps[:, 7, 0:P], avt[:, u % 2, :], wt[:, 4, :], start=True, stop=True).then_inc(S["wo"], 1)

        @block.vector
        def _(v):
            c = Counts(v)
            nc.vector.memset(resid[:, TILES - 1, :], 0.0).then_inc(S["zero"], 1)
            c.chain(S["v"], nc.vector.memset(wnt[:, TOK:NB, :], 0.0))
            c.chain(S["v"], nc.vector.memset(bdp[:, :, 0:HEADS], 0.0))
            v.wait_ge(S["h"], 32)
            ln1.vector(nc, v, c, S["v"], resid, w)
            ln2.vector(nc, v, c, S["v"], w, wn, S["wn"])
            c.chain(S["v"], nc.vector.tensor_tensor(resid[:], resid[:], w[:], ALU.add))
            v.wait_ge(S["wt_tp"], 1)
            c.chain(S["v"], nc.vector.tensor_copy(wt[:, 0:4, :].rearrange("p q m -> p (q m)"), ps[:, 6, :]))
            nc.vector.tensor_copy(wt[:, 4, :], ps[:, 7, 0:P]).then_inc(S["wt"], 1)
            v.wait_ge(S["w"], 16 * 9)
            for n in range(3):
                v.wait_ge(S["wnt_tp"], n + 1)
                m = min(12, IMGS - 12 * n)
                nc.vector.tensor_scalar(wnt[:, 0:TOK, 12 * n:12 * n + m].rearrange("p t i -> p i t"),
                                        ps[:, 3 + n, 0:m * TOK].rearrange("p (i t) -> p i t", t=TOK),
                                        cols[:, 0:1], cols[:, 1:2], ALU.mult, ALU.add).then_inc(S["wnt"], 1)
            v.wait_ge(S["rk"], 1)
            c.chain(S["rexp"], nc.vector.tensor_copy(rk[:], ps[:, 7, 128:128 + IMGS]))
            c.chain(S["rexp"], nc.vector.tensor_tensor(rexp[:], rk[:].unsqueeze(2).to_broadcast([P, IMGS, HEADS]),
                                                       hmask[:].unsqueeze(1).to_broadcast([P, IMGS, HEADS]), ALU.mult))
            for n in range(3):
                wd = min(512, NB * IMGS - 512 * n)
                v.wait_ge(S["qr"], n + 1)
                c.chain(S["v"], nc.vector.tensor_scalar(qw[:, 512 * n:512 * n + wd], ps[:, n, 0:wd], cols[:, 2:3], None, ALU.add))
            for n in range(3):
                wd = min(512, NB * IMGS - 512 * n)
                v.wait_ge(S["k"], n + 1)
                nc.vector.tensor_tensor(kexp[:, 512 * n:512 * n + wd, :], ps[:, 3 + n, 0:wd].unsqueeze(2).to_broadcast([P, wd, HEADS]),
                                        hmask[:].unsqueeze(1).to_broadcast([P, wd, HEADS]), ALU.mult).then_inc(S["kx"], 1)
            for n in range(2 * NB // 4):
                v.wait_ge(S["vr"], n + 1)
                nc.vector.tensor_tensor(vexp[:, 4 * n:4 * n + 4, :], ps[:, 4 + n % 2, :].rearrange("p (a d) -> p a d", a=4),
                                        hrows[:].unsqueeze(1).to_broadcast([P, 4, P]), ALU.mult).then_inc(S["vx"], 1)
            v.wait_ge(S["bd_in"], 64)
            for t in range(QT + 2):
                if t < QT:
                    v.wait_ge(S["ac"], t + 1)
                    if t >= 2:
                        v.wait_ge(S["e"], t - 1)
                    c.chain(S["s"], nc.vector.tensor_tensor(sc[:, t % 2, :], ps[:, t % 2, 0:HJ], bds[:, t, :], ALU.add))
                    sv = sc[:, t % 2, :].rearrange("p (j n) -> p j n", n=HEADS)
                    c.chain(S["v"], nc.vector.tensor_reduce(mx[:, t % 2, :], sv.rearrange("p j n -> p n j"), AX_X, ALU.max))
                    nc.vector.tensor_tensor(sv, sv, mx[:, t % 2, :].unsqueeze(1).to_broadcast([P, IMGS, HEADS]), ALU.subtract).then_inc(S["sub"], 1)
                u = t - 1
                if 0 <= u < QT:
                    v.wait_ge(S["e"], u + 1)
                    c.chain(S["den"], nc.vector.tensor_reduce(den[:, u % 2, :], pr[:, u % 2, :].rearrange("p (j n) -> p n j", n=HEADS), AX_X, ALU.add))
                    c.chain(S["v"], nc.vector.reciprocal(rden[:, u % 4, :], den[:, u % 2, :]))
                u = t - 2
                if 0 <= u < QT:
                    v.wait_ge(S["pv"], u + 1)
                    if u >= 2:
                        v.wait_ge(S["avt"], u - 1)
                    nc.vector.tensor_tensor(av[:, u % 2, :].rearrange("p (n d) -> p n d", n=HEADS),
                                            ps[:, 4 + u % 2, 0:P].rearrange("p (n d) -> p n d", n=HEADS),
                                            rden[:, u % 4, :].unsqueeze(2).to_broadcast([P, HEADS, DH]), ALU.mult).then_inc(S["av"], 1)
            v.wait_ge(S["ao_in"], 32)
            c.chain(S["v"], nc.vector.tensor_tensor(resid[:, 0:TILES - 1, :], resid[:, 0:TILES - 1, :], aor[:, 0:TILES - 1, :], ALU.add))
            c.chain(S["v"], nc.vector.tensor_tensor(resid[0:LAST, TILES - 1, :], resid[0:LAST, TILES - 1, :], aor[0:LAST, TILES - 1, :], ALU.add))


def transpose_rows(nc, pe, rows, ident, ps, bank0, s_rows, s_tp):
    for t in range(TILES):
        pe.wait_ge(s_rows, t + 1)
        last = nc.tensor.transpose(ps[:, bank0 + t // 4, (t % 4) * TP:(t % 4) * TP + TP], rows[:, t, :], ident[0:TP, 0:TP])
        if t % 4 == 3 or t == TILES - 1:
            last.then_inc(s_tp, 1)


SPANS = [(4 * n * TP, min(4, TILES - 4 * n) * TP) for n in range(3)]


def lstm_stage(nc, a, resid):
    F16 = mybir.dt.float16
    KE = 2 * EXPERTS
    G = 4
    EG = EXPERTS // 2
    N = 2 * TOK
    with ExitStack() as ctx:
        st = Stage(nc, ctx, "moe")
        gate_half = st.sb("gate_half", [P, 1])
        w_hi = [st.sb(f"w_hi{n}", [P, EXPERTS, G, P], F16) for n in range(2)]
        w_lo = [st.sb(f"w_lo{n}", [P, EXPERTS, G, P], F16) for n in range(2)]
        scale = st.sb("scale", [P, 6])
        sbits = st.sb("sbits", [P, 2], U32)
        brow = st.sb("brow", [P, 32, P], BF16)
        ones = st.sb("ones", [P, N], BF16)
        wo = st.sb("wo", [P, EXPERTS, P])
        bo = st.sb("bo", [EXPERTS, P])
        x_hi = st.sb("x_hi", [P, COLS], F16)
        x_lo = st.sb("x_lo", [P, COLS], F16)
        ct = st.sb("ct", [EXPERTS, COLS])
        mask = st.sb("mask", [P, KE, COLS], F16)
        rwt = st.sb("rwt", [P, 2, COLS])
        cell = st.sb("cell", [P, 2, EG, N])
        hs = st.sb("hs", [P, EXPERTS, COLS])
        ps = st.ps("ps")
        names = ("const", "w", "bias", "wo", "zero", "v", "pool", "xn", "xt_tp", "xt", "lg", "top", "e1", "pack", "mt_tp", "mt",
                 "bc", "bc_v", "bc_a", "amax", "allmax", "scale", "w_hi", "w_lo", "wf_used", "wf1", "bparts", "brow", "y", "y_sb",
                 "lv", "xm", "hm", "wst", "hs", "table")
        S = {n: st.sem(n) for n in names}
        s_gates = [st.sem(f"gates_mm{g}") for g in range(2)]
        s_tanh = [st.sem(f"gates_tanh{g}") for g in range(2)]
        s_cell = [st.sem(f"cell{g}") for g in range(2)]
        s_tc = [st.sem(f"cell_tanh{g}") for g in range(2)]
        s_h = [st.sem(f"state{g}") for g in range(2)]
        blocks = [(j, n) for j in range(18) for n in range(3)]

        def by_vector(b):
            return b % 2 == 0

        with ExitStack() as before:
            pre = Stage(nc, before, "moe")
            ident = pre.sb("ident", [P, P])
            iota = pre.sb("iota", [P, 8])
            row_sel = pre.sb("row_sel", [18, 18, P])
            row_sel16 = pre.sb("row_sel16", [18, KE, P], F16)
            rw = pre.sb("rw", [P, EXPERTS])
            rb = pre.sb("rb", [TP, EXPERTS])
            wf = pre.sb("wf", [P, EXPERTS, G, P])
            amax = pre.sb("amax", [P, 4])
            bf = pre.sb("bf", [32, P])
            bparts = pre.sb("bparts", [32, 3, P], BF16)
            brem = pre.sb("brem", [32, 2, P])
            xn = pre.sb("xn", [TP, TILES, D])
            xt = pre.sb("xt", [P, COLS])
            lg = pre.sb("lg", [TP, TILES, 8])
            top = pre.sb("top", [TP, TILES, 8])
            topi = pre.sb("topi", [TP, TILES, 8], U32)
            topf = pre.sb("topf", [TP, TILES, 2])
            pack = pre.sb("pack", [TP, TILES, 18])
            comb = pre.sb("comb", [TP, TILES, 2, 8])
            e1 = pre.sb("e1", [TP, TILES, 3])
            mt = pre.sb("mt", [18, COLS])
            mt16 = pre.sb("mt16", [18, COLS], F16)
            ln = Norm(pre, "ln", TP, TILES)
            with nc.Block() as block:
                @block.sync
                def _(sp):
                    sp.dma_start(ident[:], const(a["consts"], "ident")).then_inc(S["const"], 16)
                    sp.dma_start(rw[:], a["L0_ffn_router_w"]).then_inc(S["const"], 16)
                    sp.dma_start(rb[:], a["L0_ffn_router_b"].partition_broadcast(TP)).then_inc(S["const"], 16)
                    sp.dma_start(iota[:], const(a["consts"], "iota8")).then_inc(S["const"], 16)
                    sp.dma_start(gate_half[:], const(a["consts"], "gate_half"), allow_slow_non_contiguous=True).then_inc(S["const"], 16)
                    sp.dma_start(row_sel[:], const(a["consts"], "row_sel", 18).rearrange("p (j m) -> p j m", j=18)).then_inc(S["const"], 16)
                    sp.dma_start(bf[:], a["L0_ffn_b"].rearrange("e (g h) -> (e g) h", g=G)).then_inc(S["bias"], 16)
                    sp.dma_start(wo[:], a["L0_ffn_Wo"].rearrange("e h o -> h e o")).then_inc(S["wo"], 16)
                    sp.dma_start(bo[:], a["L0_ffn_bo"]).then_inc(S["wo"], 16)
                    sp.wait_ge(S["bparts"], 5)
                    sp.wait_ge(S["zero"], 2)
                    for k in range(3):
                        sp.dma_start(brow[k:k + 1, :, :], bparts[:, k, :]).then_inc(S["brow"], 16)
                    sp.wait_ge(S["brow"], 48)

                @block.scalar
                def _(act):
                    act.dma_start(wf[:], a["L0_ffn_Wi"].rearrange("e i (g h) -> i e g h", g=G)).then_inc(S["w"], 16)
                    act.dma_start(hs_as_w(hs), a["L0_ffn_Wh"].rearrange("e i (g h) -> i e g h", g=G)).then_inc(S["w"], 16)
                    ln.scalar(nc, act)
                    act.wait_ge(S["top"], 2)
                    nc.scalar.activation(e1[:, :, 1], e1[:, :, 0], ACT.Exp).then_inc(S["e1"], 1)
                    act.wait_ge(S["scale"], 6)
                    act.wait_ge(S["w"], 32)
                    for n, src in enumerate((wf[:], hs_as_w(hs))):
                        for g0, g1, col in ((0, 2, 1 + n), (2, 3, n), (3, 4, 1 + n)):
                            nc.scalar.activation(w_hi[n][:, :, g0:g1, :], src[:, :, g0:g1, :], ACT.Copy, scale=scale[:, col:col + 1]).then_inc(S["w_hi"], 1)
                    for b, (j, n) in enumerate(blocks):
                        if not by_vector(b):
                            act.wait_ge(S["bc"], b + 1)
                            at, wd = SPANS[n]
                            dst = mask[:, j, at:at + wd] if j < KE else rwt[:, j - KE, at:at + wd]
                            nc.scalar.copy(dst, ps[:, b % 6, 0:wd]).then_inc(S["bc_a"], 1)

                @block.gpsimd
                def _(pool):
                    nc.gpsimd.memset(ones[:], 1.0).then_inc(S["zero"], 1)
                    nc.gpsimd.memset(brow[:], 0.0).then_inc(S["zero"], 1)
                    for g in range(2):
                        nc.gpsimd.memset(cell[:, g, :, :], 0.0).then_inc(S["zero"], 1)
                    pool.wait_ge(S["amax"], 1)
                    nc.gpsimd.partition_all_reduce(amax[:, 3:4], amax[:, 2:3], P, bass.bass_isa.ReduceOp.max).then_inc(S["allmax"], 1)

                @block.tensor
                def _(pe):
                    pe.wait_ge(S["const"], 96)
                    transpose_rows(nc, pe, xn, ident, ps, 0, S["xn"], S["xt_tp"])
                    pe.wait_ge(S["xt"], 3)
                    for t in range(TILES):
                        last = nc.tensor.matmul(ps[0:TP, 3, 8 * t:8 * t + 8], xt[:, t * TP:(t + 1) * TP], rw[:], start=True, stop=True)
                    last.then_inc(S["lg"], 1)
                    pe.wait_ge(S["pack"], 1)
                    for t in range(TILES):
                        last = nc.tensor.transpose(ps[0:18, t // 4, (t % 4) * TP:(t % 4) * TP + TP], pack[:, t, :], ident[0:TP, 0:TP])
                    for t in range(TILES):
                        last = nc.tensor.transpose(ps[0:8, 3 + t // 4, (t % 4) * TP:(t % 4) * TP + TP], comb[:, t, 0, :], ident[0:TP, 0:TP])
                    last.then_inc(S["mt_tp"], 1)
                    pe.wait_ge(S["mt"], 10)
                    for b, (j, n) in enumerate(blocks):
                        at, wd = SPANS[n]
                        if b >= 6:
                            o = b - 6
                            pe.wait_ge(S["bc_v"] if by_vector(o) else S["bc_a"], o // 2 + 1)
                        lhs, rhs = (row_sel16, mt16) if j < KE else (row_sel, mt)
                        nc.tensor.matmul(ps[:, b % 6, 0:wd], lhs[:, j, :], rhs[:, at:at + wd], start=True, stop=True).then_inc(S["bc"], 1)

                @block.vector
                def _(v):
                    c = Counts(v)
                    ln.vector(nc, v, c, S["v"], resid, xn, S["xn"])
                    for n, (at, wd) in enumerate(SPANS):
                        v.wait_ge(S["xt_tp"], n + 1)
                        nc.vector.tensor_copy(xt[:, at:at + wd], ps[:, n, 0:wd]).then_inc(S["xt"], 1)
                    v.wait_ge(S["xt"], 3)
                    c.chain(S["v"], nc.vector.tensor_copy(x_hi[:], xt[:]))
                    c.chain(S["v"], nc.vector.tensor_tensor(x_lo[:], xt[:], x_hi[:], ALU.subtract))
                    v.wait_ge(S["lg"], 1)
                    v.wait_ge(S["const"], 96)
                    c.chain(S["v"], nc.vector.tensor_tensor(lg[:], ps[0:TP, 3, 0:8 * TILES].rearrange("p (t e) -> p t e", e=8),
                                                            rb[:].unsqueeze(1).to_broadcast([TP, TILES, 8]), ALU.add))
                    for t in range(TILES):
                        ins = nc.vector.max(top[:, t, :], lg[:, t, :])
                    c.chain(S["v"], ins)
                    for t in range(TILES):
                        ins = nc.vector.max_index(topi[:, t, :], top[:, t, :], lg[:, t, :])
                    c.chain(S["top"], ins)
                    c.chain(S["top"], nc.vector.tensor_tensor(e1[:, :, 0], top[:, :, 1], top[:, :, 0], ALU.subtract))
                    c.chain(S["v"], nc.vector.tensor_copy(topf[:], topi[:, :, 0:2]))
                    for k in range(2):
                        ins = nc.vector.tensor_tensor(pack[:, :, 8 * k:8 * k + 8], iota[0:TP, :].unsqueeze(1).to_broadcast([TP, TILES, 8]),
                                                      topf[:, :, k:k + 1].to_broadcast([TP, TILES, 8]), ALU.is_equal)
                    v.wait_ge(S["e1"], 1)
                    c.chain(S["v"], nc.vector.tensor_scalar(e1[:, :, 2], e1[:, :, 1], 1.0, None, ALU.add))
                    c.chain(S["v"], nc.vector.reciprocal(pack[:, :, 16], e1[:, :, 2]))
                    c.chain(S["v"], nc.vector.tensor_tensor(pack[:, :, 17], pack[:, :, 16], e1[:, :, 1], ALU.mult))
                    for k in range(2):
                        ins = nc.vector.tensor_tensor(comb[:, :, k, :], pack[:, :, 8 * k:8 * k + 8],
                                                      pack[:, :, 16 + k:17 + k].to_broadcast([TP, TILES, 8]), ALU.mult)
                    c.chain(S["v"], ins)
                    c.chain(S["pack"], nc.vector.tensor_tensor(comb[:, :, 0, :], comb[:, :, 0, :], comb[:, :, 1, :], ALU.add))
                    v.wait_ge(S["mt_tp"], 1)
                    nc.vector.tensor_copy(row_sel16[:], row_sel[:, 0:KE, :]).then_inc(S["mt"], 1)
                    for n, (at, wd) in enumerate(SPANS):
                        nc.vector.tensor_copy(mt[:, at:at + wd], ps[0:18, n, 0:wd]).then_inc(S["mt"], 1)
                        nc.vector.tensor_copy(mt16[:, at:at + wd], ps[0:18, n, 0:wd]).then_inc(S["mt"], 1)
                        nc.vector.tensor_scalar(ct[:, at:at + wd], ps[0:8, 3 + n, 0:wd], 2.0, None, ALU.mult).then_inc(S["mt"], 1)
                    v.wait_ge(S["w"], 32)
                    nc.vector.tensor_reduce(amax[:, 0:1], wf[:].rearrange("p e g h -> p (e g h)"), AX_X, ALU.max, apply_absolute_value=True)
                    c.chain(S["v"], nc.vector.tensor_reduce(amax[:, 1:2], hs_as_w(hs).rearrange("p e g h -> p (e g h)"), AX_X, ALU.max, apply_absolute_value=True))
                    c.chain(S["v"], nc.vector.tensor_tensor(amax[:, 2:3], amax[:, 0:1], amax[:, 1:2], ALU.max))
                    c.chain(S["amax"], nc.vector.tensor_copy(amax[:, 0:1], amax[:, 2:3]))
                    v.wait_ge(S["allmax"], 1)
                    c.chain(S["v"], nc.vector.tensor_scalar(amax[:, 3:4], amax[:, 3:4], 1e-25, None, ALU.max))
                    c.chain(S["v"], nc.vector.tensor_scalar(sbits[:, 0:1], amax[:, 3:4].bitcast(U32), 0x7F800000, None, ALU.bitwise_and))
                    c.chain(S["v"], nc.vector.tensor_scalar(sbits[:, 1:2], sbits[:, 0:1], -1.0, float(267 << 23), ALU.mult, ALU.add))
                    c.chain(S["scale"], nc.vector.tensor_copy(scale[:, 0:1], sbits[:, 1:2].bitcast(F32)))
                    c.chain(S["scale"], nc.vector.tensor_scalar(scale[:, 1:2], scale[:, 0:1], 0.5, None, ALU.mult))
                    c.chain(S["scale"], nc.vector.tensor_scalar(scale[:, 2:3], scale[:, 0:1], 0.25, None, ALU.mult))
                    c.chain(S["scale"], nc.vector.tensor_scalar(scale[:, 3:4], sbits[:, 0:1].bitcast(F32), 2.0 ** -13, None, ALU.mult))
                    c.chain(S["scale"], nc.vector.tensor_tensor(scale[:, 4:5], scale[:, 0:1], gate_half[:], ALU.mult))
                    c.chain(S["scale"], nc.vector.tensor_copy(scale[:, 5:6], scale[:, 0:1]))
                    v.wait_ge(S["bias"], 16)
                    c.chain(S["v"], nc.vector.tensor_scalar(brem[:, 0, :], bf[:], scale[0:32, 4:5], None, ALU.mult))
                    c.chain(S["bparts"], nc.vector.tensor_copy(bparts[:, 0, :], brem[:, 0, :]))
                    c.chain(S["bparts"], nc.vector.tensor_tensor(brem[:, 1, :], brem[:, 0, :], bparts[:, 0, :], ALU.subtract))
                    c.chain(S["bparts"], nc.vector.tensor_copy(bparts[:, 1, :], brem[:, 1, :]))
                    c.chain(S["bparts"], nc.vector.tensor_tensor(brem[:, 0, :], brem[:, 1, :], bparts[:, 1, :], ALU.subtract))
                    c.chain(S["bparts"], nc.vector.tensor_copy(bparts[:, 2, :], brem[:, 0, :]))
                    for n, src in enumerate((wf[:], hs_as_w(hs))):
                        for k, (g0, g1, col) in enumerate(((0, 2, 1 + n), (2, 3, n), (3, 4, 1 + n))):
                            v.wait_ge(S["w_hi"], 3 * n + k + 1)
                            for e in range(EXPERTS):
                                nc.vector.scalar_tensor_tensor(out=w_lo[n][:, e, g0:g1, :], in0=src[:, e, g0:g1, :], scalar=scale[:, col:col + 1],
                                                               in1=w_hi[n][:, e, g0:g1, :], op0=ALU.mult, op1=ALU.subtract).then_inc(S["w_lo"], 1)
                    for b, (j, n) in enumerate(blocks):
                        if by_vector(b):
                            v.wait_ge(S["bc"], b + 1)
                            at, wd = SPANS[n]
                            dst = mask[:, j, at:at + wd] if j < KE else rwt[:, j - KE, at:at + wd]
                            nc.vector.tensor_copy(dst, ps[:, b % 6, 0:wd]).then_inc(S["bc_v"], 1)


        STEPS = 2
        TURNS = IMGS // STEPS
        with ExitStack() as during:
            loop = Stage(nc, during, "moe")
            xm_hi = loop.sb("xm_hi", [P, 2, KE, TOK], F16)
            xm_lo = loop.sb("xm_lo", [P, 2, KE, TOK], F16)
            gates = loop.sb("gates", [P, 2, EG, G, N])
            fc = loop.sb("fc", [P, 2, EG, N])
            ig = loop.sb("ig", [P, 2, EG, N])
            tc = loop.sb("tc", [P, 2, EG, N])
            hf = loop.sb("hf", [P, 2, 2, EG, N])
            hm = loop.sb("hm", [P, 2, EXPERTS, N])
            h_hi = loop.sb("h_hi", [P, 2, EG, N], F16)
            h_lo = loop.sb("h_lo", [P, 2, EG, N], F16)
            wst = loop.sb("wst", [P, 2, 2, EXPERTS, TOK])
            with nc.Block() as block:
                @block.tensor
                def _(pe):
                    with pe.Fori(0, TURNS) as i:
                        for s in range(STEPS):
                            pe.wait_ge(S["xm"], i * (2 * STEPS) + (2 * s + 2))
                            for g in range(2):
                                pe.wait_ge(s_tanh[g], i * STEPS + (s + 1))
                                for e in range(EG):
                                    ex = g * EG + e
                                    rhs = [m[:, s, ex:KE:EXPERTS, :] for m in (xm_hi, xm_hi, xm_lo)]
                                    for q in range(G):
                                        dst = ps[:, g * EG + e, q * N:(q + 1) * N]
                                        nc.tensor.matmul(dst, brow[:, ex * G + q, :], ones[:], start=(q == 0), stop=False, skip_group_check=True)
                                        for k, wgt in enumerate((w_hi, w_lo, w_hi)):
                                            nc.tensor.matmul(dst, wgt[0][:, ex, q, :], rhs[k], start=False, stop=False, skip_group_check=True)
                                pe.wait_ge(s_h[g], i * STEPS + (s + 1))
                                for e in range(EG):
                                    ex = g * EG + e
                                    for q in range(G):
                                        dst = ps[:, g * EG + e, q * N:(q + 1) * N]
                                        for k, (wgt, h) in enumerate(((w_hi, h_hi), (w_lo, h_hi), (w_hi, h_lo))):
                                            last = nc.tensor.matmul(dst, wgt[1][:, ex, q, :], h[:, g, e, :], start=False, stop=(k == 2), skip_group_check=True)
                                last.then_inc(s_gates[g], 1)

                @block.scalar
                def _(act):
                    for g in range(2):
                        nc.scalar.activation(tc[:, g, 0, 0:1], cell[:, g, 0, 0:1], ACT.Tanh).then_inc(s_tanh[g], 1)
                        act.wait_ge(s_tanh[g], 1)
                    with act.Fori(0, TURNS) as i:
                        for s in range(STEPS):
                            for g in range(2):
                                act.wait_ge(s_gates[g], i * STEPS + (s + 1))
                                nc.scalar.activation(gates[:, g, :, :, :].rearrange("p e q n -> p e (q n)"), ps[:, g * EG:(g + 1) * EG, 0:G * N],
                                                     ACT.Tanh, scale=scale[:, 3:4]).then_inc(s_tanh[g], 1)
                                act.wait_ge(s_cell[g], i * STEPS + (s + 1))
                                nc.scalar.activation(tc[:, g, :, :], cell[:, g, :, :], ACT.Tanh, scale=0.5).then_inc(s_tc[g], 1)

                @block.vector
                def _(v):
                    LV = 2 * 3
                    def mask_inputs(s, cols):
                        for n, (x, m) in enumerate(((x_hi, xm_hi), (x_lo, xm_lo))):
                            nc.vector.tensor_tensor(m[:, s, :, :], x[:, cols].unsqueeze(1).to_broadcast([P, KE, TOK]),
                                                    mask[:, :, cols], ALU.mult).then_inc(S["xm"], 1)

                    def cell_step(i, s, g):
                        v.wait_ge(s_tanh[g], i * STEPS + (s + 2))
                        nc.vector.scalar_tensor_tensor(out=fc[:, g, :, :], in0=gates[:, g, :, 1, :], scalar=1.0, in1=cell[:, g, :, :], op0=ALU.add, op1=ALU.mult)
                        nc.vector.scalar_tensor_tensor(out=ig[:, g, :, :], in0=gates[:, g, :, 0, :], scalar=1.0, in1=gates[:, g, :, 2, :],
                                                       op0=ALU.add, op1=ALU.mult).then_inc(S["lv"], 1)
                        v.wait_ge(S["lv"], i * (LV * STEPS) + (LV * s + 3 * g + 1))
                        nc.vector.scalar_tensor_tensor(out=cell[:, g, :, :], in0=fc[:, g, :, :], scalar=0.5, in1=ig[:, g, :, :],
                                                       op0=ALU.mult, op1=ALU.add).then_inc(s_cell[g], 1)

                    def state_step(i, s, g):
                        v.wait_ge(s_tc[g], i * STEPS + (s + 1))
                        nc.vector.scalar_tensor_tensor(out=h_hi[:, g, :, :], in0=gates[:, g, :, 3, :], scalar=1.0, in1=tc[:, g, :, :], op0=ALU.add,
                                                       op1=ALU.mult).then_inc(S["lv"], 1)
                        nc.vector.scalar_tensor_tensor(out=hf[:, s, g, :, :], in0=gates[:, g, :, 3, :], scalar=1.0, in1=tc[:, g, :, :], op0=ALU.add,
                                                       op1=ALU.mult).then_inc(S["lv"], 1)
                        v.wait_ge(S["lv"], i * (LV * STEPS) + (LV * s + 3 * g + 3))
                        nc.vector.tensor_tensor(h_lo[:, g, :, :], hf[:, s, g, :, :], h_hi[:, g, :, :], ALU.subtract).then_inc(s_h[g], 1)

                    def pick(s, cols):
                        nc.vector.tensor_tensor(hs[:, :, cols], hm[:, s, :, 0:TOK], hm[:, s, :, TOK:N], ALU.add).then_inc(S["hs"], 1)

                    for g in range(2):
                        nc.vector.memset(h_hi[:, g, :, :], 0.0).then_inc(S["hs"], 1)
                        v.wait_ge(S["hs"], g + 1)
                        nc.vector.memset(h_lo[:, g, :, :], 0.0).then_inc(s_h[g], 1)
                    mask_inputs(0, slice(0, TOK))
                    with v.Fori(0, TURNS) as i:
                        for s in range(STEPS):
                            if s == 0:
                                mask_inputs(1, bass.ds(i * (STEPS * TOK) + TOK, TOK))
                            else:
                                mask_inputs(0, bass.ds(i * (STEPS * TOK) + (STEPS * TOK), TOK))
                            v.wait_ge(S["hm"], i * (2 * STEPS) + (2 * s + 2))
                            pick(1 - s, bass.ds(i * (STEPS * TOK) + s * TOK, TOK))
                            cell_step(i, s, 0)
                            state_step(i, s, 0)
                            cell_step(i, s, 1)
                            state_step(i, s, 1)
                    v.wait_ge(S["hm"], 2 * IMGS + 2)
                    pick(1, slice(NTOK, COLS))

                @block.gpsimd
                def _(pool):
                    for g in range(2):
                        nc.gpsimd.memset(hm[:, 1, g * EG:(g + 1) * EG, :], 0.0).then_inc(S["hm"], 1)
                    with pool.Fori(0, TURNS) as i:
                        for s in range(STEPS):
                            cols = bass.ds(i * (STEPS * TOK) + s * TOK, TOK)
                            nc.gpsimd.tensor_tensor(wst[:, s, :, :, :], mask[:, :, cols].rearrange("p (k e) n -> p k e n", k=2),
                                                    rwt[:, :, cols].unsqueeze(2).to_broadcast([P, 2, EXPERTS, TOK]), ALU.mult).then_inc(S["wst"], 1)
                            pool.wait_ge(S["wst"], i * STEPS + (s + 1))
                            for g in range(2):
                                pool.wait_ge(s_h[g], i * STEPS + (s + 2))
                                nc.gpsimd.tensor_tensor(hm[:, s, g * EG:(g + 1) * EG, :].rearrange("p e (k n) -> p e k n", k=2),
                                                        hf[:, s, g, :, :].rearrange("p e (k n) -> p e k n", k=2),
                                                        wst[:, s, :, g * EG:(g + 1) * EG, :].rearrange("p k e n -> p e k n"), ALU.mult).then_inc(S["hm"], 1)

        with nc.Block() as block:
            @block.tensor
            def _(pe):
                pe.wait_ge(S["wo"], 32)
                for t in range(TILES):
                    if t >= 4:
                        pe.wait_ge(S["y_sb"], t - 2)
                    n = TP if t < TILES - 1 else LAST
                    dst = ps[0:n, t % 4, 0:P]
                    nc.tensor.matmul(dst, ct[:, t * TP:t * TP + n], bo[:], start=True, stop=False)
                    for e in range(EXPERTS):
                        last = nc.tensor.matmul(dst, hs[:, e, TOK + t * TP:TOK + t * TP + n], wo[:, e, :], start=False, stop=(e == EXPERTS - 1))
                    last.then_inc(S["y"], 1)

            @block.vector
            def _(v):
                for t in range(TILES):
                    n = TP if t < TILES - 1 else LAST
                    v.wait_ge(S["y"], t + 1)
                    nc.vector.scalar_tensor_tensor(out=resid[0:n, t, :], in0=ps[0:n, t % 4, 0:P], scalar=0.5, in1=resid[0:n, t, :],
                                                   op0=ALU.mult, op1=ALU.add).then_inc(S["y_sb"], 1)


def hs_as_w(hs):
    return hs[:].rearrange("p e n -> p (e n)")[:, 0:4096].rearrange("p (e g h) -> p e g h", e=EXPERTS, g=4)


def power_of_two(nc, c, s_v, top, bits, scale, inverse):
    c.chain(s_v, nc.vector.tensor_scalar(top, top, 1e-25, None, ALU.max))
    c.chain(s_v, nc.vector.tensor_scalar(bits[:, 0:1], top.bitcast(U32), 0x7F800000, None, ALU.bitwise_and))
    c.chain(s_v, nc.vector.tensor_scalar(bits[:, 1:2], bits[:, 0:1], -1.0, float(267 << 23), ALU.mult, ALU.add))
    c.chain(s_v, nc.vector.tensor_copy(scale, bits[:, 1:2].bitcast(F32)))
    c.chain(s_v, nc.vector.tensor_scalar(inverse, bits[:, 0:1].bitcast(F32), 2.0 ** -13, None, ALU.mult))


def thread_stage(nc, a, resid):
    F16 = mybir.dt.float16
    K = THREADS
    B = IMGS
    KT = K * TILES
    WIH, WHH, WQ, WK, WV, WB, WM = 0, 12, 24, 28, 32, 36, 44
    NW = 48
    with ExitStack() as ctx:
        st = Stage(nc, ctx, "thr")
        ident = st.sb("ident", [P, P])
        x1 = st.sb("x1", [TP, TILES, D])
        wt = st.sb("wt", [P, NW, P])

        scale = st.sb("scale", [P, 4])
        x_hi = st.sb("x_hi", [P, TOK, B], F16)
        x_lo = st.sb("x_lo", [P, TOK, B], F16)
        wi_hi = st.sb("wi_hi", [P, 12, P], F16)
        wi_lo = st.sb("wi_lo", [P, 12, P], F16)
        wh_hi = st.sb("wh_hi", [P, 12, P], F16)
        wh_lo = st.sb("wh_lo", [P, 12, P], F16)
        brow = st.sb("brow", [P, 12, P], BF16)
        ones = st.sb("ones", [P, B], BF16)
        ncols = st.sb("ncols", [P, 4 + 4])
        aot = st.sb("aot", [P, K, COLS])
        xn_in = st.sb("xn_in", [P, TOK, K, B])
        hist = st.sb("hist", [P, K, TOK + 1, B])
        bn_rows = st.sb("bn_rows", [TP, 2, D])
        ps = st.ps("ps")
        names = ("const", "pool", "w", "v", "xn", "xt_tp", "xt", "wtp", "wt_sb", "amax", "allmax", "whi", "wlo", "rows", "bparts", "brow", "col_tp", "cols",
                 "pj", "pj_sb", "zero", "sc", "sub", "e", "p", "pt", "pt_sb", "ao", "ao_sb", "gru_in", "lv", "table", "gbt", "beat",
                 "rden", "th", "tht", "tht_sb", "mix", "mix_sb", "thn", "xh")
        S = {n: st.sem(n) for n in names}
        s_r, s_z, s_n = st.sem("r_mm"), st.sem("z_mm"), st.sem("n_mm")
        s_tr, s_tz, s_tn, s_np, s_hi, s_lo = (st.sem(n) for n in ("r_tanh", "z_tanh", "n_tanh", "n_pre", "state_hi", "state_lo"))

        with ExitStack() as inner:
            sa = Stage(nc, inner, "thr")
            win = sa.sb("win", [TP, K, TP])
            qt = sa.sb("qt", [P, K, COLS])
            kt = sa.sb("kt", [P, K, COLS])
            vr = sa.sb("vr", [TP, TILES, K, P])
            with ExitStack() as first:
                sp_ = Stage(nc, first, "thr")
                xt = sp_.sb("xt", [P, COLS])
                pos = sp_.sb("pos", [TP, D])
                amax = sp_.sb("amax", [P, 2])
                sbits = sp_.sb("sbits", [P, 2], U32)
                rows = sp_.sb("rows", [12, 2, P])
                nrows = sp_.sb("nrows", [2 * K, P])
                facts = sp_.sb("facts", [12, 2])
                brem = sp_.sb("brem", [12, 2, P])
                bparts = sp_.sb("bparts", [12, 3, P], BF16)
                bcols = sp_.sb("bcols", [P, 12])
                ln = Norm(sp_, "ln", TP, TILES)
                jobs = [("q", k, n) for k in range(K) for n in range(3)] + [("k", k, n) for k in range(K) for n in range(3)] \
                    + [("n", k, n) for k in range(K) for n in range(3)] + [("v", 0, t) for t in range(TILES)]
                with nc.Block() as block:
                    @block.sync
                    def _(sp):
                        sp.dma_start(ident[:], const(a["consts"], "ident")).then_inc(S["const"], 16)
                        sp.dma_start(pos[:], const(a["consts"], "pos_code", TP)).then_inc(S["const"], 16)
                        sp.dma_start(win[:], const(a["consts"], "window", TP).rearrange("p (k s) -> p k s", k=K)).then_inc(S["const"], 16)
                        sp.dma_start(facts[:], const(a["consts"], "gru_facts", 12)).then_inc(S["const"], 16)
                        sp.dma_start(rows[:, 0, :], a["L1_attn_gru_bih"].rearrange("k (g i) -> (k g) i", g=3)).then_inc(S["rows"], 16)
                        sp.dma_start(rows[:, 1, :], a["L1_attn_gru_bhh"].rearrange("k (g i) -> (k g) i", g=3)).then_inc(S["rows"], 16)
                        sp.dma_start(nrows[0:K, :], a["L1_attn_norm_g"]).then_inc(S["rows"], 16)
                        sp.dma_start(nrows[K:2 * K, :], a["L1_attn_norm_b"]).then_inc(S["rows"], 16)
                        sp.dma_start(bn_rows[:, 0, :], a["L1_attn_bn_g"].partition_broadcast(TP)).then_inc(S["rows"], 16)
                        sp.dma_start(bn_rows[:, 1, :], a["L1_attn_bn_b"].partition_broadcast(TP)).then_inc(S["rows"], 16)
                        sp.wait_ge(S["bparts"], 5)
                        sp.wait_ge(S["pool"], 2)
                        for k in range(3):
                            sp.dma_start(brow[k:k + 1, :, :], bparts[:, k, :]).then_inc(S["brow"], 16)
                        sp.wait_ge(S["brow"], 48)

                    @block.scalar
                    def _(act):
                        for nm, at, n in (("L1_attn_gru_wih", WIH, 12), ("L1_attn_gru_whh", WHH, 12)):
                            act.dma_start(wt[:, at:at + n, :], a[nm].rearrange("k (g i) j -> i (k g) j", g=3)).then_inc(S["w"], 16)
                        for nm, at in (("L1_attn_wq", WQ), ("L1_attn_wk", WK), ("L1_attn_wv", WV)):
                            act.dma_start(wt[:, at:at + K, :], a[nm].rearrange("k i j -> i k j")).then_inc(S["w"], 16)
                        for k in range(K):
                            act.dma_start(wt[:, WB + 2 * k:WB + 2 * k + 2, :].rearrange("p a j -> p (a j)"), a["L1_attn_w_beat"][k]).then_inc(S["w"], 16)
                        act.dma_start(wt[:, WM:WM + K, :].rearrange("p a j -> p (a j)"), a["L1_attn_w_mix"]).then_inc(S["w"], 16)
                        ln.scalar(nc, act)
                        for n, (kind, k, m) in enumerate(jobs):
                            act.wait_ge(S["pj"], n + 1)
                            if kind == "v":
                                ins = nc.scalar.copy(vr[:, m, :, :].rearrange("p k d -> p (k d)"), ps[0:TP, n % 8, :])
                            elif kind == "n":
                                t0, tn = 16 * m, min(16, TOK - 16 * m)
                                ins = nc.scalar.activation(xn_in[:, t0:t0 + tn, k, :], ps[:, n % 8, 0:tn * B].rearrange("p (t b) -> p t b", b=B),
                                                           ACT.Identity, bias=bcols[:, 3 * k + 2:3 * k + 3])
                            else:
                                at, wd = SPANS[m]
                                ins = nc.scalar.copy((qt if kind == "q" else kt)[:, k, at:at + wd], ps[:, n % 8, 0:wd])
                            ins.then_inc(S["pj_sb"], 1)

                    @block.gpsimd
                    def _(pool):
                        nc.gpsimd.memset(ones[:], 1.0).then_inc(S["pool"], 1)
                        nc.gpsimd.memset(brow[:], 0.0).then_inc(S["pool"], 1)
                        nc.gpsimd.memset(hist[:, :, 0, :], 0.0).then_inc(S["pool"], 1)
                        pool.wait_ge(S["amax"], 1)
                        nc.gpsimd.partition_all_reduce(amax[:, 1:2], amax[:, 0:1], P, bass.bass_isa.ReduceOp.max).then_inc(S["allmax"], 1)

                    @block.tensor
                    def _(pe):
                        pe.wait_ge(S["const"], 64)
                        pe.wait_ge(S["w"], 16 * 10)
                        for n in range(NW // 4):
                            if n >= 4:
                                pe.wait_ge(S["wt_sb"], n - 3)
                            for k in range(4):
                                last = nc.tensor.transpose(ps[:, n % 4, k * P:(k + 1) * P], wt[:, 4 * n + k, :], ident[:])
                            last.then_inc(S["wtp"], 1)
                        pe.wait_ge(S["rows"], 96)
                        nc.tensor.transpose(ps[:, 7, 0:12], rows[:, 0, :], ident[0:12, 0:12])
                        nc.tensor.transpose(ps[:, 7, 16:16 + 2 * K], nrows[:], ident[0:2 * K, 0:2 * K]).then_inc(S["col_tp"], 1)
                        transpose_rows(nc, pe, x1, ident, ps, 4, S["xn"], S["xt_tp"])
                        pe.wait_ge(S["cols"], 2)
                        pe.wait_ge(S["xt"], 3)
                        pe.wait_ge(S["wt_sb"], NW // 4)
                        xtb = xt[:, 0:NTOK].rearrange("p (b t) -> p t b", t=TOK)
                        for n, (kind, k, m) in enumerate(jobs):
                            if n >= 8:
                                pe.wait_ge(S["pj_sb"], n - 7)
                            if kind == "v":
                                mm = nc.tensor.matmul(ps[0:TP, n % 8, :], xt[:, m * TP:(m + 1) * TP], wt[:, WV:WV + K, :].rearrange("p k d -> p (k d)"), start=True, stop=True)
                            elif kind == "n":
                                t0, tn = 16 * m, min(16, TOK - 16 * m)
                                mm = nc.tensor.matmul(ps[:, n % 8, 0:tn * B], wt[:, WIH + 3 * k + 2, :], xtb[:, t0:t0 + tn, :], start=True, stop=True)
                            else:
                                at, wd = SPANS[m]
                                mm = nc.tensor.matmul(ps[:, n % 8, 0:wd], wt[:, (WQ if kind == "q" else WK) + k, :], xt[:, at:at + wd], start=True, stop=True)
                            mm.then_inc(S["pj"], 1)

                    @block.vector
                    def _(v):
                        c = Counts(v)
                        ln.vector(nc, v, c, S["v"], resid, x1)
                        v.wait_ge(S["const"], 64)
                        for t in range(TILES):
                            nc.vector.tensor_tensor(x1[:, t, :], x1[:, t, :], pos[:], ALU.add).then_inc(S["xn"], 1)
                        v.wait_ge(S["w"], 16 * 10)
                        c.chain(S["v"], nc.vector.tensor_reduce(amax[:, 0:1], wt[:, 0:24, :].rearrange("p a j -> p (a j)"), AX_X, ALU.max, apply_absolute_value=True))
                        c.chain(S["amax"], nc.vector.tensor_copy(scale[:, 3:4], amax[:, 0:1]))
                        for n in range(NW // 4):
                            v.wait_ge(S["wtp"], n + 1)
                            nc.vector.tensor_copy(wt[:, 4 * n:4 * n + 4, :].rearrange("p a j -> p (a j)"), ps[:, n % 4, :]).then_inc(S["wt_sb"], 1)
                        v.wait_ge(S["allmax"], 1)
                        power_of_two(nc, c, S["v"], amax[:, 1:2], sbits, scale[:, 0:1], scale[:, 3:4])
                        c.chain(S["v"], nc.vector.tensor_scalar(scale[:, 1:2], scale[:, 0:1], 0.5, None, ALU.mult))
                        c.chain(S["v"], nc.vector.tensor_scalar(scale[:, 2:3], scale[:, 0:1], 0.25, None, ALU.mult))
                        v.wait_ge(S["wt_sb"], NW // 4)
                        for hi, lo, at, col in ((wi_hi, wi_lo, WIH, 1), (wh_hi, wh_lo, WHH, 2)):
                            src, sc_ = wt[:, at:at + 12, :].rearrange("p a j -> p (a j)"), scale[:, col:col + 1]
                            c.chain(S["whi"], nc.vector.tensor_scalar(hi[:].rearrange("p a j -> p (a j)"), src, sc_, None, ALU.mult))
                            c.chain(S["v"], nc.vector.scalar_tensor_tensor(out=lo[:].rearrange("p a j -> p (a j)"), in0=src, scalar=sc_,
                                                                           in1=hi[:].rearrange("p a j -> p (a j)"), op0=ALU.mult, op1=ALU.subtract))
                        for k in range(K):
                            ins = nc.vector.tensor_scalar(wt[:, WB + 2 * k, :], wt[:, WB + 2 * k, :], 0.5, None, ALU.mult)
                        c.chain(S["v"], ins)
                        v.wait_ge(S["rows"], 96)
                        c.chain(S["v"], nc.vector.scalar_tensor_tensor(out=brem[:, 0, :], in0=rows[:, 0, :], scalar=facts[:, 0:1], in1=rows[:, 1, :],
                                                                       op0=ALU.mult, op1=ALU.add))
                        c.chain(S["v"], nc.vector.tensor_scalar(brem[:, 0, :], brem[:, 0, :], scale[0:12, 1:2], None, ALU.mult))
                        c.chain(S["bparts"], nc.vector.tensor_copy(bparts[:, 0, :], brem[:, 0, :]))
                        c.chain(S["bparts"], nc.vector.tensor_tensor(brem[:, 1, :], brem[:, 0, :], bparts[:, 0, :], ALU.subtract))
                        c.chain(S["bparts"], nc.vector.tensor_copy(bparts[:, 1, :], brem[:, 1, :]))
                        c.chain(S["bparts"], nc.vector.tensor_tensor(brem[:, 0, :], brem[:, 1, :], bparts[:, 1, :], ALU.subtract))
                        c.chain(S["bparts"], nc.vector.tensor_copy(bparts[:, 2, :], brem[:, 0, :]))
                        v.wait_ge(S["col_tp"], 1)
                        nc.vector.tensor_copy(bcols[:], ps[:, 7, 0:12]).then_inc(S["cols"], 1)
                        nc.vector.tensor_copy(ncols[:], ps[:, 7, 16:16 + 2 * K]).then_inc(S["cols"], 1)
                        for n, (at, wd) in enumerate(SPANS):
                            v.wait_ge(S["xt_tp"], n + 1)
                            nc.vector.tensor_copy(xt[:, at:at + wd], ps[:, 4 + n, 0:wd]).then_inc(S["xt"], 1)
                        v.wait_ge(S["xt"], 3)
                        xtb = xt[:, 0:NTOK].rearrange("p (b t) -> p t b", t=TOK)
                        c.chain(S["v"], nc.vector.tensor_copy(x_hi[:], xtb))
                        c.chain(S["v"], nc.vector.tensor_tensor(x_lo[:], xtb, x_hi[:], ALU.subtract))

            sc = sa.sb("sc", [TP, 2, K, TP])
            mx = sa.sb("mx", [TP, 2, K])
            den = sa.sb("den", [TP, 2, K])
            rden = sa.sb("rden", [TP, 2, K])
            pr = sa.sb("pr", [TP, 2, K, TP])
            pn = sa.sb("pn", [TP, 2, K, TP])
            pt = sa.sb("pt", [TP, 2, K, TP])
            with nc.Block() as block:
                @block.tensor
                def _(pe):
                    for t in range(TILES + 2):
                        if t < TILES:
                            if t >= 2:
                                pe.wait_ge(S["sc"], t - 1)
                            for k in range(K):
                                cols = slice(t * TP, (t + 1) * TP)
                                last = nc.tensor.matmul(ps[0:TP, t % 2, k * TP:(k + 1) * TP], qt[:, k, cols], kt[:, k, cols], start=True, stop=True)
                            last.then_inc(S["th"], 1)
                        if 1 <= t <= TILES:
                            u = t - 1
                            pe.wait_ge(S["p"], u + 1)
                            if u >= 2:
                                pe.wait_ge(S["pt_sb"], u - 1)
                            for k in range(K):
                                last = nc.tensor.transpose(ps[0:TP, 2 + u % 2, k * TP:(k + 1) * TP], pn[:, u % 2, k, :], ident[0:TP, 0:TP])
                            last.then_inc(S["pt"], 1)
                        if t >= 2:
                            u = t - 2
                            pe.wait_ge(S["pt_sb"], u + 1)
                            if u >= 2:
                                pe.wait_ge(S["ao_sb"], u - 1)
                            for k in range(K):
                                last = nc.tensor.matmul(ps[:, 4 + u % 2, k * TP:(k + 1) * TP], vr[:, u, k, :], pt[:, u % 2, k, :], start=True, stop=True)
                            last.then_inc(S["ao"], 1)

                @block.scalar
                def _(act):
                    for t in range(TILES + 2):
                        if t < TILES:
                            act.wait_ge(S["sub"], t + 1)
                            if t >= 2:
                                act.wait_ge(S["p"], t - 1)
                            nc.scalar.activation(pr[:, t % 2, :, :], sc[:, t % 2, :, :], ACT.Exp, scale=float(D) ** -0.5).then_inc(S["e"], 1)
                        if 1 <= t <= TILES:
                            u = t - 1
                            act.wait_ge(S["pt"], u + 1)
                            if u >= 2:
                                act.wait_ge(S["ao"], u - 1)
                            nc.scalar.copy(pt[:, u % 2, :, :].rearrange("p k s -> p (k s)"), ps[0:TP, 2 + u % 2, 0:K * TP]).then_inc(S["pt_sb"], 1)
                        if t >= 2:
                            u = t - 2
                            act.wait_ge(S["ao"], u + 1)
                            nc.scalar.copy(aot[:, :, u * TP:(u + 1) * TP], ps[:, 4 + u % 2, 0:K * TP].rearrange("p (k s) -> p k s", k=K)).then_inc(S["ao_sb"], 1)

                @block.gpsimd
                def _(pool):
                    for t in range(TILES):
                        b = t % 2
                        pool.wait_ge(S["rden"], t + 1)
                        if t >= 2:
                            pool.wait_ge(S["pt"], t - 1)
                        nc.gpsimd.tensor_tensor(pn[:, b, :, :], pr[:, b, :, :], rden[:, b, :].unsqueeze(2).to_broadcast([TP, K, TP]), ALU.mult).then_inc(S["p"], 1)

                @block.vector
                def _(v):
                    c = Counts(v)
                    for t in range(TILES + 1):
                        if t < TILES:
                            b = t % 2
                            v.wait_ge(S["th"], t + 1)
                            if t >= 2:
                                v.wait_ge(S["e"], t - 1)
                            c.chain(S["sc"], nc.vector.tensor_tensor(sc[:, b, :, :], ps[0:TP, b, 0:K * TP].rearrange("p (k s) -> p k s", k=K), win[:], ALU.add))
                            c.chain(S["lv"], nc.vector.tensor_reduce(mx[:, b, :], sc[:, b, :, :], AX_X, ALU.max))
                            nc.vector.tensor_tensor(sc[:, b, :, :], sc[:, b, :, :], mx[:, b, :].unsqueeze(2).to_broadcast([TP, K, TP]), ALU.subtract).then_inc(S["sub"], 1)
                        if t >= 1:
                            u = t - 1
                            b = u % 2
                            v.wait_ge(S["e"], u + 1)
                            c.chain(S["lv"], nc.vector.tensor_reduce(den[:, b, :], pr[:, b, :, :], AX_X, ALU.add))
                            if u >= 2:
                                v.wait_ge(S["p"], u - 1)
                            nc.vector.reciprocal(rden[:, b, :], den[:, b, :]).then_inc(S["rden"], 1)

        TURNS = TOK // 2
        KB = K * B
        with ExitStack() as inner:
            sg = Stage(nc, inner, "gru")
            tr = sg.sb("tr", [P, KB])
            tz = sg.sb("tz", [P, K, B])
            rn = sg.sb("rn", [P, KB])
            npre = sg.sb("npre", [P, KB])
            tn = sg.sb("tn", [P, K, B])
            omz = sg.sb("omz", [P, K, B])
            zh = sg.sb("zh", [P, K, B])
            pz = sg.sb("pz", [P, K, B])
            h_hi = sg.sb("h_hi", [P, K, B], F16)
            h_lo = sg.sb("h_lo", [P, K, B], F16)
            gv = sg.sem("gv")
            with nc.Block() as block:
                @block.tensor
                def _(pe):
                    def inputs(s, t):
                        for gate in range(3):
                            for k in range(K):
                                dst = ps[:, 3 * s + gate, k * B:(k + 1) * B]
                                w = 3 * k + gate
                                nc.tensor.matmul(dst, brow[:, w, :], ones[:], start=(k == 0), stop=False, skip_group_check=True)
                                if gate < 2:
                                    for wgt, x in ((wi_hi, x_hi), (wi_lo, x_hi), (wi_hi, x_lo)):
                                        nc.tensor.matmul(dst, wgt[:, w, :], x[:, t, :], start=False, stop=False, skip_group_check=True)

                    def states(s, n):
                        pe.wait_ge(s_hi, n)
                        for gate in (0, 2, 1):
                            for k in range(K):
                                dst = ps[:, 3 * s + gate, k * B:(k + 1) * B]
                                for wgt in (wh_hi, wh_lo):
                                    nc.tensor.matmul(dst, wgt[:, 3 * k + gate, :], h_hi[:, k, :], start=False, stop=False, skip_group_check=True)
                        pe.wait_ge(s_lo, n)
                        for gate, done in ((0, s_r), (2, s_n), (1, s_z)):
                            for k in range(K):
                                dst = ps[:, 3 * s + gate, k * B:(k + 1) * B]
                                last = nc.tensor.matmul(dst, wh_hi[:, 3 * k + gate, :], h_lo[:, k, :], start=False, stop=True, skip_group_check=True)
                            last.then_inc(done, 1)

                    inputs(0, 0)
                    with pe.Fori(0, TURNS) as i:
                        for s in range(2):
                            states(s, i * 2 + (s + 1))
                            inputs(1 - s, i * 2 + (s + 1))
                    states(0, TOK)

                @block.scalar
                def _(act):
                    nc.scalar.activation(tr[:, 0:1], scale[:, 0:1], ACT.Tanh).then_inc(S["table"], 1)
                    act.wait_ge(S["table"], 1)

                    def step(s, n):
                        act.wait_ge(s_r, n)
                        nc.scalar.activation(tr[:], ps[:, 3 * s, 0:KB], ACT.Tanh, scale=scale[:, 3:4]).then_inc(s_tr, 1)
                        act.wait_ge(s_z, n)
                        nc.scalar.activation(tz[:].rearrange("p k b -> p (k b)"), ps[:, 3 * s + 1, 0:KB], ACT.Tanh, scale=scale[:, 3:4]).then_inc(s_tz, 1)
                        act.wait_ge(s_np, n)
                        nc.scalar.activation(tn[:].rearrange("p k b -> p (k b)"), npre[:], ACT.Tanh).then_inc(s_tn, 1)

                    with act.Fori(0, TURNS) as i:
                        for s in range(2):
                            step(s, i * 2 + (s + 1))
                    step(0, TOK)

                @block.vector
                def _(v):
                    nc.vector.memset(h_hi[:], 0.0).then_inc(s_hi, 1)
                    nc.vector.memset(h_lo[:], 0.0).then_inc(s_lo, 1)
                    GV = 6

                    def step(s, t, n, base):
                        before, after = hist[:, :, slot(t, 0), :], hist[:, :, slot(t, 1), :]
                        v.wait_ge(s_tr, n)
                        v.wait_ge(s_n, n)
                        nc.vector.scalar_tensor_tensor(out=rn[:], in0=tr[:], scalar=1.0, in1=ps[:, 3 * s + 2, 0:KB], op0=ALU.add, op1=ALU.mult).then_inc(gv, 1)
                        v.wait_ge(gv, base + 1)
                        nc.vector.scalar_tensor_tensor(out=npre[:], in0=rn[:], scalar=scale[:, 3:4], in1=xn_at(t), op0=ALU.mult, op1=ALU.add).then_inc(s_np, 1)
                        v.wait_ge(s_tz, n)
                        nc.vector.tensor_scalar(omz[:], tz[:], -1.0, 1.0, ALU.mult, ALU.add).then_inc(gv, 1)
                        nc.vector.scalar_tensor_tensor(out=zh[:], in0=tz[:], scalar=1.0, in1=before, op0=ALU.add, op1=ALU.mult).then_inc(gv, 1)
                        v.wait_ge(s_tn, n)
                        v.wait_ge(gv, base + 3)
                        nc.vector.tensor_tensor(pz[:], omz[:], tn[:], ALU.mult).then_inc(gv, 1)
                        v.wait_ge(gv, base + 4)
                        nc.vector.scalar_tensor_tensor(out=h_hi[:], in0=zh[:], scalar=0.5, in1=pz[:], op0=ALU.mult, op1=ALU.add).then_inc(s_hi, 1)
                        nc.vector.scalar_tensor_tensor(out=after, in0=zh[:], scalar=0.5, in1=pz[:], op0=ALU.mult, op1=ALU.add).then_inc(gv, 1)
                        v.wait_ge(gv, base + 5)
                        v.wait_ge(s_hi, n + 1)
                        nc.vector.tensor_tensor(h_lo[:], after, h_hi[:], ALU.subtract).then_inc(s_lo, 1)

                    def slot(t, d):
                        return t + d

                    def xn_at(t):
                        return xn_in[:, t, :, :].rearrange("p k b -> p (k b)")

                    with v.Fori(0, TURNS) as i:
                        for s in range(2):
                            step(s, i * 2 + s, i * 2 + (s + 1), i * (2 * 5) + 5 * s)
                    step(0, TOK - 1, TOK, 5 * (TOK - 1))

        with ExitStack() as inner:
            sf = Stage(nc, inner, "mix")
            gbt = sf.sb("gbt", [P, K, COLS])
            th = sf.sb("th", [TP, KT, P])
            tht = sf.sb("tht", [P, K, COLS])
            mixed = sf.sb("mixed", [TP, TILES, D])
            lt = Norm(sf, "lt", TP, KT)
            lm = Norm(sf, "lm", TP, TILES)
            fv, s_thr = sf.sem("fv"), sf.sem("thr")
            with nc.Block() as block:
                @block.tensor
                def _(pe):
                    for t in range(TILES):
                        if t == 0:
                            pe.wait_ge(S["gbt"], K + 1)
                        if t >= 4:
                            pe.wait_ge(s_thr, t - 3)
                        cols = slice(t * TP, (t + 1) * TP)
                        for k in range(K):
                            dst = ps[0:TP, t % 4, k * P:(k + 1) * P]
                            nc.tensor.matmul(dst, gbt[:, k, cols], wt[:, WB + 2 * k, :], start=True, stop=False)
                            last = nc.tensor.matmul(dst, aot[:, k, cols], wt[:, WB + 2 * k + 1, :], start=False, stop=True)
                        last.then_inc(S["beat"], 1)
                    for t in range(TILES):
                        pe.wait_ge(S["thn"], 4 * t + 4)
                        if t >= 2:
                            pe.wait_ge(S["tht_sb"], 4 * (t - 1))
                        for k in range(K):
                            last = nc.tensor.transpose(ps[:, 4 + t % 2, k * TP:(k + 1) * TP], th[:, 4 * t + k, :], ident[0:TP, 0:TP])
                        last.then_inc(S["tht"], 1)
                    for t in range(TILES):
                        pe.wait_ge(S["tht_sb"], 4 * (t + 1))
                        if t >= 2:
                            pe.wait_ge(S["mix_sb"], t - 1)
                        for k in range(K):
                            last = nc.tensor.matmul(ps[0:TP, 6 + t % 2, 0:P], tht[:, k, t * TP:(t + 1) * TP], wt[:, WM + k, :], start=(k == 0), stop=(k == K - 1))
                        last.then_inc(S["mix"], 1)

                @block.scalar
                def _(act):
                    lt.scalar(nc, act)
                    for t in range(TILES):
                        act.wait_ge(S["tht"], t + 1)
                        for k in range(K):
                            nc.scalar.activation(tht[:, k, t * TP:(t + 1) * TP], ps[:, 4 + t % 2, k * TP:(k + 1) * TP], ACT.Identity,
                                                 scale=ncols[:, k:k + 1], bias=ncols[:, K + k:K + k + 1]).then_inc(S["tht_sb"], 1)
                    lm.scalar(nc, act)

                @block.vector
                def _(v):
                    c = Counts(v)
                    c.chain(S["gbt"], nc.vector.memset(gbt[:, :, NTOK:COLS], 0.0))
                    for k in range(K):
                        nc.vector.tensor_copy(gbt[:, k, 0:NTOK].rearrange("p (b t) -> p b t", t=TOK),
                                              hist[:, k, 1:TOK + 1, :].rearrange("p t b -> p b t")).then_inc(S["gbt"], 1)
                    for t in range(TILES):
                        v.wait_ge(S["beat"], t + 1)
                        c.chain(s_thr, nc.vector.tensor_tensor(th[:, 4 * t:4 * t + 4, :], ps[0:TP, t % 4, :].rearrange("p (k d) -> p k d", k=K),
                                                               x1[:, t, :].unsqueeze(1).to_broadcast([TP, K, P]), ALU.add))
                    lt.vector(nc, v, c, fv, th, th, S["thn"])
                    for t in range(TILES):
                        v.wait_ge(S["mix"], t + 1)
                        c.chain(S["mix_sb"], nc.vector.tensor_tensor(mixed[:, t, :], ps[0:TP, 6 + t % 2, 0:P], x1[:, t, :], ALU.add))
                    lm.vector(nc, v, c, fv, mixed, mixed)
                    c.chain(fv, nc.vector.tensor_tensor(mixed[:], mixed[:], bn_rows[:, 0, :].unsqueeze(1).to_broadcast([TP, TILES, D]), ALU.mult))
                    c.chain(fv, nc.vector.tensor_tensor(mixed[:], mixed[:], bn_rows[:, 1, :].unsqueeze(1).to_broadcast([TP, TILES, D]), ALU.add))
                    c.chain(fv, nc.vector.tensor_tensor(resid[:], resid[:], mixed[:], ALU.add))


def expert_stage(nc, a, resid):
    E, NE = EXPERTS, EXPERTS + 1
    with ExitStack() as ctx:
        st = Stage(nc, ctx, "ffn")
        ident = st.sb("ident", [P, P])
        iota = st.sb("iota", [P, 8])
        w1 = st.sb("w1", [P, NE, P])
        w2 = st.sb("w2", [P, NE, P])
        gw = st.sb("gw", [E, P])
        gwt = st.sb("gwt", [P, E])
        b1 = st.sb("b1", [NE, P])
        b1c = st.sb("b1c", [P, NE])
        b2 = st.sb("b2", [E, P])
        sb2 = st.sb("sb2", [TP, P])
        xn = st.sb("xn", [TP, TILES, D])
        xt = st.sb("xt", [P, COLS])
        lg = st.sb("lg", [TP, TILES, E])
        red = st.sb("red", [TP, TILES, 4])
        top = st.sb("top", [TP, TILES, 8])
        topi = st.sb("topi", [TP, TILES, 8], U32)
        topf = st.sb("topf", [TP, TILES, 2])
        hot = st.sb("hot", [TP, TILES, 2, E])
        comb = st.sb("comb", [TP, TILES, E])
        ct = st.sb("ct", [E, COLS])
        h1 = st.sb("h1", [P, NE, COLS])
        ps = st.ps("ps")
        ln = Norm(st, "ln", TP, TILES)
        names = ("const", "w", "v", "xn", "xt_tp", "xt", "wtp", "wts", "lg", "sub", "e", "comb", "ct_tp", "ct", "h1", "h1_sb", "base", "ya", "yb", "acc")
        S = {n: st.sem(n) for n in names}
        block = ctx.enter_context(nc.Block())

        @block.sync
        def _(sp):
            sp.dma_start(ident[:], const(a["consts"], "ident")).then_inc(S["const"], 16)
            sp.dma_start(iota[:], const(a["consts"], "iota8")).then_inc(S["const"], 16)
            sp.dma_start(gw[:], a["L1_ffn_gate_w"]).then_inc(S["const"], 16)
            sp.dma_start(b1[0:E, :], a["L1_ffn_b1"]).then_inc(S["const"], 16)
            sp.dma_start(b1[E:NE, :], a["L1_ffn_sb1"].partition_broadcast(1)).then_inc(S["const"], 16)
            sp.dma_start(b2[:], a["L1_ffn_b2"]).then_inc(S["const"], 16)
            sp.dma_start(sb2[:], a["L1_ffn_sb2"].partition_broadcast(TP)).then_inc(S["const"], 16)

        @block.scalar
        def _(act):
            act.dma_start(w1[:, 0:E, :], a["L1_ffn_w1"].rearrange("e h f -> h e f")).then_inc(S["w"], 16)
            act.dma_start(w1[:, E, :], a["L1_ffn_sw1"]).then_inc(S["w"], 16)
            act.dma_start(w2[:, 0:E, :], a["L1_ffn_w2"].rearrange("e f h -> f e h")).then_inc(S["w"], 16)
            act.dma_start(w2[:, E, :], a["L1_ffn_sw2"]).then_inc(S["w"], 16)
            ln.scalar(nc, act)
            act.wait_ge(S["sub"], 1)
            nc.scalar.activation(lg[:], lg[:], ACT.Exp).then_inc(S["e"], 1)
            act.wait_ge(S["wts"], 2)
            for n in range(3 * NE):
                e, (at, wd) = n // 3, SPANS[n % 3]
                act.wait_ge(S["h1"], n + 1)
                nc.scalar.activation(h1[:, e, at:at + wd], ps[:, n % 3, 0:wd], ACT.Relu, bias=b1c[:, e:e + 1]).then_inc(S["h1_sb"], 1)

        @block.tensor
        def _(pe):
            pe.wait_ge(S["const"], 16 * 7)
            nc.tensor.transpose(ps[:, 7, 0:E], gw[:], ident[0:E, 0:E])
            nc.tensor.transpose(ps[:, 7, 16:16 + NE], b1[:], ident[0:NE, 0:NE]).then_inc(S["wtp"], 1)
            transpose_rows(nc, pe, xn, ident, ps, 0, S["xn"], S["xt_tp"])
            pe.wait_ge(S["xt"], 3)
            pe.wait_ge(S["wts"], 2)
            for t in range(TILES):
                last = nc.tensor.matmul(ps[0:TP, 6, E * t:E * t + E], xt[:, t * TP:(t + 1) * TP], gwt[:], start=True, stop=True)
            last.then_inc(S["lg"], 1)
            pe.wait_ge(S["w"], 64)
            for n in range(3 * NE):
                e, (at, wd) = n // 3, SPANS[n % 3]
                if n >= 3:
                    pe.wait_ge(S["h1_sb"], n - 2)
                nc.tensor.matmul(ps[:, n % 3, 0:wd], w1[:, e, :], xt[:, at:at + wd], start=True, stop=True).then_inc(S["h1"], 1)
                if n == 12:
                    pe.wait_ge(S["comb"], 1)
                    for t in range(TILES):
                        last = nc.tensor.transpose(ps[0:E, 3 + t // 4, (t % 4) * TP:(t % 4) * TP + TP], comb[:, t, :], ident[0:TP, 0:TP])
                    last.then_inc(S["ct_tp"], 1)
            pe.wait_ge(S["h1_sb"], 3 * NE)
            pe.wait_ge(S["ct"], 3)
            for t in range(TILES):
                bank = 3 * (t % 2)
                cols = slice(t * TP, (t + 1) * TP)
                if t >= 2:
                    pe.wait_ge(S["acc"], t - 1)
                nc.tensor.matmul(ps[0:TP, bank, 0:P], ct[:, cols], b2[:], start=True, stop=False)
                nc.tensor.matmul(ps[0:TP, bank, 0:P], h1[:, E, cols], w2[:, E, :], start=False, stop=True).then_inc(S["base"], 1)
                for e in range(E):
                    last = nc.tensor.matmul(ps[0:TP, bank + 1 + e // 4, (e % 4) * P:(e % 4) * P + P], h1[:, e, cols], w2[:, e, :], start=True, stop=True)
                    if e % 4 == 3:
                        last.then_inc(S["ya"] if e < 4 else S["yb"], 1)

        @block.vector
        def _(v):
            c = Counts(v)
            v.wait_ge(S["wtp"], 1)
            nc.vector.tensor_copy(gwt[:], ps[:, 7, 0:E]).then_inc(S["wts"], 1)
            nc.vector.tensor_copy(b1c[:], ps[:, 7, 16:16 + NE]).then_inc(S["wts"], 1)
            ln.vector(nc, v, c, S["v"], resid, xn, S["xn"])
            for n, (at, wd) in enumerate(SPANS):
                v.wait_ge(S["xt_tp"], n + 1)
                nc.vector.tensor_copy(xt[:, at:at + wd], ps[:, n, 0:wd]).then_inc(S["xt"], 1)
            v.wait_ge(S["lg"], 1)
            v.wait_ge(S["const"], 16 * 7)
            lgp = ps[0:TP, 6, 0:E * TILES].rearrange("p (t e) -> p t e", e=E)
            c.chain(S["v"], nc.vector.tensor_reduce(red[:, :, 0], lgp, AX_X, ALU.max))
            c.chain(S["sub"], nc.vector.tensor_tensor(lg[:], lgp, red[:, :, 0:1].to_broadcast([TP, TILES, E]), ALU.subtract))
            v.wait_ge(S["e"], 1)
            c.chain(S["v"], nc.vector.tensor_reduce(red[:, :, 1], lg[:], AX_X, ALU.add))
            c.chain(S["v"], nc.vector.reciprocal(red[:, :, 2], red[:, :, 1]))
            c.chain(S["v"], nc.vector.tensor_tensor(lg[:], lg[:], red[:, :, 2:3].to_broadcast([TP, TILES, E]), ALU.mult))
            for t in range(TILES):
                ins = nc.vector.max(top[:, t, :], lg[:, t, :])
            c.chain(S["v"], ins)
            for t in range(TILES):
                ins = nc.vector.max_index(topi[:, t, :], top[:, t, :], lg[:, t, :])
            c.chain(S["v"], ins)
            c.chain(S["v"], nc.vector.tensor_copy(topf[:], topi[:, :, 0:2]))
            c.chain(S["v"], nc.vector.tensor_tensor(red[:, :, 0], top[:, :, 0], top[:, :, 1], ALU.add))
            c.chain(S["v"], nc.vector.tensor_scalar(red[:, :, 0], red[:, :, 0], 1e-20, None, ALU.add))
            c.chain(S["v"], nc.vector.reciprocal(red[:, :, 1], red[:, :, 0]))
            c.chain(S["v"], nc.vector.tensor_tensor(red[:, :, 2:4], top[:, :, 0:2], red[:, :, 1:2].to_broadcast([TP, TILES, 2]), ALU.mult))
            for k in range(2):
                ins = nc.vector.tensor_tensor(hot[:, :, k, :], iota[0:TP, :].unsqueeze(1).to_broadcast([TP, TILES, E]),
                                              topf[:, :, k:k + 1].to_broadcast([TP, TILES, E]), ALU.is_equal)
            c.chain(S["v"], ins)
            for k in range(2):
                ins = nc.vector.tensor_tensor(hot[:, :, k, :], hot[:, :, k, :], red[:, :, 2 + k:3 + k].to_broadcast([TP, TILES, E]), ALU.mult)
            c.chain(S["v"], ins)
            c.chain(S["comb"], nc.vector.tensor_tensor(comb[:], hot[:, :, 0, :], hot[:, :, 1, :], ALU.add))
            c.chain(S["v"], nc.vector.tensor_tensor(resid[:], resid[:], sb2[:].unsqueeze(1).to_broadcast([TP, TILES, D]), ALU.add))
            v.wait_ge(S["ct_tp"], 1)
            for n, (at, wd) in enumerate(SPANS):
                nc.vector.tensor_copy(ct[:, at:at + wd], ps[0:E, 3 + n, 0:wd]).then_inc(S["ct"], 1)
            for t in range(TILES):
                bank = 3 * (t % 2)
                v.wait_ge(S["base"], t + 1)
                c.chain(S["v"], nc.vector.tensor_tensor(resid[:, t, :], ps[0:TP, bank, 0:P], resid[:, t, :], ALU.add))
                for e in range(E):
                    if e % 4 == 0:
                        v.wait_ge(S["ya"] if e < 4 else S["yb"], t + 1)
                    c.chain(S["acc"] if e == E - 1 else S["v"],
                            nc.vector.scalar_tensor_tensor(out=resid[:, t, :], in0=ps[0:TP, bank + 1 + e // 4, (e % 4) * P:(e % 4) * P + P],
                                                           scalar=comb[:, t, e:e + 1], in1=resid[:, t, :], op0=ALU.mult, op1=ALU.add))


def dump_rows(nc, resid, dram, tag):
    with ExitStack() as ctx:
        s_out = nc.alloc_semaphore(f"{tag}_rows_out")
        block = ctx.enter_context(nc.Block())

        @block.sync
        def _(sp):
            full, last = rows_view(dram)
            sp.dma_start(full, resid[:, 0:TILES - 1, :]).then_inc(s_out, 16)
            sp.dma_start(last, resid[0:LAST, TILES - 1, :]).then_inc(s_out, 16)
            sp.wait_ge(s_out, 32)


def vit_tower_kernel(nc, a, out):
    h0 = nc.dram_tensor("h0_rows", (NTOK, D), F32, kind="Internal").ap()
    tok_stage(nc, a, h0)
    stages = [lambda r: rel_attn_stage(nc, a, h0, r), lambda r: lstm_stage(nc, a, r), lambda r: thread_stage(nc, a, r), lambda r: expert_stage(nc, a, r)]
    with nc.sbuf_tensor("resid", [TP, TILES, D], F32) as resid:
        for n, f in enumerate(stages):
            f(resid)
            if n == 1 or n == 2:
                clear_semaphores(nc)
        dump_rows(nc, resid, out.rearrange("b t d -> (b t) d"), "out")


def kernel(**inputs):
    import concourse.bacc as _bacc
    from concourse.bass_utils import run_bass_kernel_spmd as _run

    nc = _bacc.Bacc("TRN2", target_bir_lowering=False, num_devices=1)
    arrays, args = {}, {}
    feeds = dict(inputs)
    feeds["consts"] = np.concatenate([np.pad(v, ((0, P - v.shape[0]), (0, 0))) for v in CONSTS.values()], 1)
    for name, value in feeds.items():
        v = np.ascontiguousarray(value)
        arrays[f"in_{name}_dram"] = v
        args[name] = nc.dram_tensor(f"in_{name}_dram", v.shape, mybir.dt.from_np(v.dtype), kind="ExternalInput").ap()
    out = nc.dram_tensor("out_0_dram", (IMGS, TOK, D), F32, kind="ExternalOutput").ap()
    vit_tower_kernel(nc, args, out)
    r = _run(nc, [arrays], core_ids=[0])
    return r.results[0]["out_0_dram"]
```

```python
from contextlib import ExitStack

import numpy as np

import concourse.bass as bass
from concourse import mybir

F32 = mybir.dt.float32
BF16 = mybir.dt.bfloat16
U32 = mybir.dt.uint32
ALU = mybir.AluOpType
ACT = mybir.ActivationFunctionType
AX_X = mybir.AxisListType.X

P = 128
D = 128
IMGS = 32
TOK = 37
GRID = 6
PATCH = 16
NTOK = IMGS * TOK
TP = 3 * TOK
TILES = -(-NTOK // TP)
LAST = NTOK - (TILES - 1) * TP
COLS = TILES * TP
EPS = 1e-5
HEADS, DH = 8, 16
EXPERTS = 8
THREADS = 4
CYCLES = (5, 6, 7, 8)


def shape_constants():
    c = {}
    c["ident"] = np.eye(P, dtype=np.float32)
    sel = np.zeros((5, P, P), np.float32)
    sel[0] = np.eye(P)
    for m in range(16):
        sel[1, 80 + m, 64 + m] = 1
        sel[2, 64 + m, 80 + m] = 1
        sel[3, 112 + m, 96 + m] = 1
        sel[4, 96 + m, 112 + m] = 1
    c["shift_sel"] = sel.transpose(1, 0, 2).reshape(P, 5 * P)
    pos = np.arange(IMGS - 1, -1, -1, dtype=np.float32)
    inv = (1.0 / 10000.0 ** (np.arange(0, D, 2, dtype=np.float32) / D)).astype(np.float32)
    s = pos[:, None] * inv[None, :]
    c["rel_pos_t"] = np.concatenate([np.sin(s), np.cos(s)], -1).astype(np.float32).T
    c["head_mask"] = (np.arange(P)[:, None] // DH == np.arange(HEADS)[None, :]).astype(np.float32)
    c["head_rows"] = (np.arange(P)[:, None] % HEADS == np.arange(P)[None, :] // DH).astype(np.float32)
    t = np.arange(TOK, dtype=np.float32)[:, None]
    div = np.exp(np.arange(0, D, 2, dtype=np.float32) * np.float32(-np.log(10000.0) / D))
    pe = np.zeros((TOK, D), np.float32)
    pe[:, 0::2] = np.sin(t * div)
    pe[:, 1::2] = np.cos(t * div)
    tala = np.zeros((TOK, D), np.float32)
    slots = D // THREADS
    half = slots // 2
    harm = np.arange(1, half + 1, dtype=np.float32)
    for k, cyc in enumerate(CYCLES):
        phase = t % cyc / cyc * 2.0 * np.pi
        tala[:, k * slots:k * slots + half] = np.sin(phase * harm)
        tala[:, k * slots + half:(k + 1) * slots] = np.cos(phase * harm)
    c["pos_code"] = np.concatenate([np.tile(0.5 * pe + 0.5 * tala, (3, 1)), np.zeros((P - TP, D))], 0).astype(np.float32)
    a = np.arange(TP)
    diff = a[:, None] - a[None, :]
    same = a[:, None] // TOK == a[None, :] // TOK
    win = np.full((P, THREADS, TP), -1e30, np.float32)
    for k, cyc in enumerate(CYCLES):
        win[:TP, k] = np.where(same & (diff >= 0) & (diff < cyc), 0.0, -1e30)
    c["window"] = win.reshape(P, THREADS * TP)
    r = np.zeros((P, 18, P), np.float32)
    for j in range(18):
        r[j, j, :] = 1
    c["row_sel"] = r.reshape(P, 18 * P)
    c["ident_rep"] = np.repeat(np.eye(P, dtype=np.float32), HEADS, axis=1)
    c["gate_half"] = np.where(np.arange(P) % 4 == 2, 1.0, 0.5).astype(np.float32)[:, None]
    c["gru_facts"] = np.stack([(np.arange(P) % 3 < 2), np.ones(P)], 1).astype(np.float32)
    c["iota8"] = np.tile(np.arange(8, dtype=np.float32), (P, 1))
    return c


CONSTS = shape_constants()
CONST_AT = {}
_at = 0
for _n, _a in CONSTS.items():
    CONST_AT[_n] = (_at, _a.shape[1])
    _at += _a.shape[1]
CONST_COLS = _at


class Counts:

    def __init__(self, eng):
        self.eng, self.n = eng, {}

    def chain(self, sem, ins):
        ins.then_inc(sem, 1)
        self.n[sem.name] = self.n.get(sem.name, 0) + 1
        self.eng.wait_ge(sem, self.n[sem.name])


SEMAPHORES = []


def clear_semaphores(nc):
    nc.clear_and_free_semaphores(list(SEMAPHORES))
    SEMAPHORES.clear()
    nc.all_engine_barrier()


class Stage:

    def __init__(self, nc, ctx, tag):
        self.nc, self.ctx, self.tag = nc, ctx, tag

    def sb(self, name, shape, dt=F32):
        return self.ctx.enter_context(self.nc.sbuf_tensor(f"{self.tag}_{name}", shape, dt))

    def ps(self, name, banks=8):
        return self.ctx.enter_context(self.nc.psum_tensor(f"{self.tag}_{name}", [P, banks, 512], F32))

    def sem(self, name):
        s = self.nc.alloc_semaphore(f"{self.tag}_{name}")
        SEMAPHORES.append(s)
        return s


def const(c_all, name, rows=P):
    at, n = CONST_AT[name]
    return c_all[0:rows, at:at + n]


def rows_view(dram):
    full = dram[0:(TILES - 1) * TP, :].rearrange("(t p) d -> p t d", p=TP)
    return full, dram[(TILES - 1) * TP:NTOK, :]


def row_stats(c, s_v, nc, src, stats, mv, tiles=range(TILES)):
    for t in tiles:
        ins = nc.vector.bn_stats(stats[:, t, :], src[:, t, :])
    c.chain(s_v, ins)
    for t in tiles:
        ins = nc.vector.bn_aggr(mv[:, t, :], stats[:, t, :])
    c.chain(s_v, ins)


def tok_stage(nc, a, h_dram):
    NQ = 6
    HALF = 3 * IMGS
    SIDE = GRID + 1
    CELL = SIDE * SIDE
    CELLS = IMGS * CELL
    GUARD = SIDE + 1
    GT = 14
    GP = CELLS // GT
    with ExitStack() as ctx:
        st = Stage(nc, ctx, "tok")
        ident = st.sb("ident", [P, P])
        sel = st.sb("sel", [P, 5, P])
        wn = st.sb("wn", [P, 3 * 256])
        wt = st.sb("wt", [P, NQ, P])
        img = st.sb("img", [HALF, 2, 3, PATCH * 96])
        pat = st.sb("pat", [HALF, 2, 3, GRID, PATCH * PATCH])
        xt = st.sb("xt", [P, NQ, 4, 3 * HALF])
        grid = st.sb("grid", [P, GUARD + CELLS + GUARD])
        bias = st.sb("bias", [P, D])
        gain = st.sb("gain", [P, D])
        beta = st.sb("beta", [P, D])
        tok = st.sb("tok", [GP, GT, D])
        outp = st.sb("outp", [GP, GT, D])
        stats = st.sb("stats", [GP, GT, 6])
        mv = st.sb("mv", [GP, GT, 2])
        std = st.sb("std", [GP, GT, 1])
        rstd = st.sb("rstd", [GP, GT, 1])
        cls = st.sb("cls", [IMGS, D])
        ps = st.ps("ps")
        s_const, s_w, s_row, s_cls = st.sem("const"), st.sem("w"), st.sem("row"), st.sem("cls")
        s_img = [st.sem(f"img{u}") for u in range(2)]
        s_zero, s_v, s_a = st.sem("zero"), st.sem("v"), st.sem("a")
        s_wtp, s_wt = st.sem("wtp"), st.sem("wt")
        s_tp, s_xt_v, s_xt_a = st.sem("tp"), st.sem("xt_v"), st.sem("xt_a")
        s_pr, s_grid = st.sem("pr"), st.sem("grid")
        s_sh, s_tok = st.sem("sh"), st.sem("tok")
        s_mv, s_std, s_outp, s_out = st.sem("mv"), st.sem("std"), st.sem("outp"), st.sem("out")
        s_pad, s_pat = st.sem("pad"), [st.sem(f"pat{u}") for u in range(2)]

        xi = a["x"].rearrange("b c (i p) w -> b c i (p w)", p=PATCH)
        padded = nc.dram_tensor("grid_rows", (CELLS, D), F32, kind="Internal").ap()

        block = ctx.enter_context(nc.Block())

        @block.sync
        def _(sp):
            for u in range(2):
                for k in range(3):
                    sp.dma_start(img[32 * k:32 * k + 32, u, :, :], xi[:, :, 3 * u + k, :]).then_inc(s_img[u], 16)
            sp.wait_ge(s_std, 1)
            sp.wait_ge(s_cls, 16)
            hv = h_dram.rearrange("(b t) d -> b t d", t=TOK)
            sp.dma_start(hv[:, 0, :], cls[:, :]).then_inc(s_out, 16)
            for n in range(2):
                sp.wait_ge(s_outp, n + 1)
                half = slice(n * GT // 2, (n + 1) * GT // 2)
                sp.dma_start(padded.rearrange("(t p) d -> p t d", p=GP)[:, half, :], outp[:, half, :]).then_inc(s_pad, 16)
            sp.wait_ge(s_pad, 32)
            pv = padded.rearrange("(b i j) d -> b i j d", i=SIDE, j=SIDE)
            for i in range(GRID):
                sp.dma_start(hv[:, 1 + GRID * i:1 + GRID * i + GRID, :], pv[:, i, 0:GRID, :]).then_inc(s_out, 16)
            sp.wait_ge(s_out, 16 * (1 + GRID))

        @block.scalar
        def _(act):
            act.dma_start(ident[:], const(a["consts"], "ident")).then_inc(s_const, 16)
            act.wait_ge(s_zero, 1)
            act.dma_start(wn[0:64, :], a["L0_tok_W_main"]).then_inc(s_w, 16)
            wx = a["L0_tok_W_sx"].rearrange("o (r j) -> o r j", j=PATCH)
            wnx = wn[:, :].rearrange("o (r j) -> o r j", j=PATCH)
            act.dma_start(wnx[64:80, :, 8:16], wx[:, :, 0:8]).then_inc(s_w, 16)
            act.dma_start(wnx[80:96, :, 0:8], wx[:, :, 8:16]).then_inc(s_w, 16)
            wy = a["L0_tok_W_sy"].rearrange("o (c h r) -> o c h r", c=3, h=2)
            wny = wn[:, :].rearrange("o (c h r) -> o c h r", c=3, h=2)
            act.dma_start(wny[96:112, :, 1, :], wy[:, :, 0, :]).then_inc(s_w, 16)
            act.dma_start(wny[112:128, :, 0, :], wy[:, :, 1, :]).then_inc(s_w, 16)
            act.dma_start(sel[:], const(a["consts"], "shift_sel").rearrange("p (s m) -> p s m", s=5)).then_inc(s_const, 16)
            at = 0
            for nm, w in (("L0_tok_b_main", 64), ("L0_tok_b_sx", 16), ("L0_tok_b_sx", 16), ("L0_tok_b_sy", 16), ("L0_tok_b_sy", 16)):
                act.dma_start(bias[:, at:at + w], a[nm].partition_broadcast(P)).then_inc(s_row, 16)
                at += w
            act.dma_start(gain[:], a["L0_tok_ln_g"].partition_broadcast(P)).then_inc(s_row, 16)
            act.dma_start(beta[:], a["L0_tok_ln_b"].partition_broadcast(P)).then_inc(s_row, 16)
            act.dma_start(cls[:], a["cls_tok"].rearrange("a b d -> (a b d)").partition_broadcast(IMGS)).then_inc(s_cls, 16)
            for u in range(2):
                act.wait_ge(s_img[u], 48)
                nc.scalar.copy(pat[:, u, 2, :, :].rearrange("p j (r e) -> p j r e", e=PATCH),
                               img[:, u, 2, :].rearrange("p (r j e) -> p j r e", r=PATCH, j=GRID)).then_inc(s_pat[u], 1)
            for n in range(1, 24, 2):
                act.wait_ge(s_tp, n + 1)
                nc.scalar.copy(xt[:, n % NQ, n // NQ, :], ps[:, n % 4, 0:3 * HALF]).then_inc(s_xt_a, 1)
            act.wait_ge(s_mv, 1)
            nc.scalar.activation(std[:, :, 0], mv[:, :, 1], ACT.Sqrt).then_inc(s_std, 1)

        @block.tensor
        def _(pe):
            pe.wait_ge(s_const, 32)
            pe.wait_ge(s_w, 80)
            for q in range(NQ):
                last = nc.tensor.transpose(ps[:, 4 + q // 4, (q % 4) * P:(q % 4) * P + P], wn[:, q * P:(q + 1) * P], ident[:])
            last.then_inc(s_wtp, 1)
            for n in range(24):
                u, jg, q = n // 12, (n // NQ) % 2, n % NQ
                if n % 12 == 0:
                    pe.wait_ge(s_pat[u], 3)
                if n >= 4:
                    if n % 2:
                        pe.wait_ge(s_xt_a, (n - 4) // 2 + 1)
                    else:
                        pe.wait_ge(s_xt_v, (n - 4) // 2 + 1)
                for k in range(3):
                    src = pat[:, u, q // 2, 3 * jg + k, P * (q % 2):P * (q % 2) + P]
                    last = nc.tensor.transpose(ps[:, n % 4, k * HALF:(k + 1) * HALF], src, ident[0:HALF, 0:HALF])
                last.then_inc(s_tp, 1)
            pe.wait_ge(s_wt, 2)
            for g in range(4):
                for q in range(NQ):
                    n = g * NQ + q
                    if n % 2:
                        pe.wait_ge(s_xt_a, n // 2 + 1)
                    else:
                        pe.wait_ge(s_xt_v, n // 2 + 1)
                    last = nc.tensor.matmul(ps[:, 4 + g, 0:3 * HALF], wt[:, q, :], xt[:, q, g, :], start=(q == 0), stop=(q == NQ - 1))
                last.then_inc(s_pr, 1)
            pe.wait_ge(s_grid, 4)
            for t in range(GT):
                if t >= 4:
                    pe.wait_ge(s_tok, t - 3)
                for k, step in enumerate((0, 1, -1, SIDE, -SIDE)):
                    at = GUARD + t * GP + step
                    last = nc.tensor.matmul(ps[0:GP, t % 4, 0:P], grid[:, at:at + GP], sel[:, k, :], start=(k == 0), stop=(k == 4))
                last.then_inc(s_sh, 1)

        @block.vector
        def _(v):
            c = Counts(v)
            nc.vector.memset(wn[:], 0.0).then_inc(s_zero, 1)
            c.chain(s_v, nc.vector.memset(grid[:], 0.0))
            for u in range(2):
                v.wait_ge(s_img[u], 48)
                for ch in range(2):
                    nc.vector.tensor_copy(pat[:, u, ch, :, :].rearrange("p j (r e) -> p j r e", e=PATCH),
                                          img[:, u, ch, :].rearrange("p (r j e) -> p j r e", r=PATCH, j=GRID)).then_inc(s_pat[u], 1)
            v.wait_ge(s_wtp, 1)
            nc.vector.tensor_copy(wt[:, 0:4, :].rearrange("p q m -> p (q m)"), ps[:, 4, 0:512]).then_inc(s_wt, 1)
            nc.vector.tensor_copy(wt[:, 4:6, :].rearrange("p q m -> p (q m)"), ps[:, 5, 0:256]).then_inc(s_wt, 1)
            for n in range(0, 24, 2):
                v.wait_ge(s_tp, n + 1)
                nc.vector.tensor_copy(xt[:, n % NQ, n // NQ, :], ps[:, n % 4, 0:3 * HALF]).then_inc(s_xt_v, 1)
            for g in range(4):
                u, jg = g // 2, g % 2
                v.wait_ge(s_pr, g + 1)
                for k in range(3):
                    cells = grid[:, GUARD:GUARD + CELLS].rearrange("p (b i j) -> p b i j", i=SIDE, j=SIDE)
                    dst = cells[:, :, 3 * u:3 * u + 3, 3 * jg + k].rearrange("p b i -> p i b")
                    ins = nc.vector.tensor_copy(dst, ps[:, 4 + g, k * HALF:(k + 1) * HALF].rearrange("p (i b) -> p i b", i=3))
                ins.then_inc(s_grid, 1)
            v.wait_ge(s_row, 16 * 7)
            for t in range(GT):
                v.wait_ge(s_sh, t + 1)
                c.chain(s_tok, nc.vector.tensor_tensor(tok[:, t, :], ps[0:GP, t % 4, 0:P], bias[0:GP, :], ALU.add))
            row_stats(c, s_v, nc, tok, stats, mv, range(GT))
            c.chain(s_v, nc.vector.tensor_scalar(mv[:, :, 1:2], mv[:, :, 1:2], EPS, None, ALU.add))
            c.chain(s_mv, nc.vector.tensor_copy(std[0:1, 0, :], mv[0:1, 0, 1:2]))
            v.wait_ge(s_std, 1)
            c.chain(s_v, nc.vector.reciprocal(rstd[:, :, 0], std[:, :, 0]))
            for t in range(GT):
                ins = nc.vector.tensor_scalar(outp[:, t, :], tok[:, t, :], mv[:, t, 0:1], rstd[:, t, :], ALU.subtract, ALU.mult)
            c.chain(s_v, ins)
            for n in range(2):
                half = slice(n * GT // 2, (n + 1) * GT // 2)
                c.chain(s_v, nc.vector.tensor_tensor(outp[:, half, :], outp[:, half, :], gain[0:GP, :].unsqueeze(1).to_broadcast([GP, GT // 2, D]), ALU.mult))
                c.chain(s_outp, nc.vector.tensor_tensor(outp[:, half, :], outp[:, half, :], beta[0:GP, :].unsqueeze(1).to_broadcast([GP, GT // 2, D]), ALU.add))


class Norm:

    def __init__(self, st, name, rows, tiles, on_scalar=False):
        self.rows, self.tiles = rows, tiles
        self.stats = st.sb(f"{name}_stats", [rows, tiles, 6])
        self.mv = st.sb(f"{name}_mv", [rows, tiles, 2])
        self.var = st.sb(f"{name}_var", [rows, tiles])
        self.std = st.sb(f"{name}_std", [rows, tiles])
        self.rstd = st.sb(f"{name}_rstd", [rows, tiles])
        self.s_var = st.sem(f"{name}_var_ready")
        self.s_std = st.sem(f"{name}_std_ready")
        if on_scalar:
            self.off = st.sb(f"{name}_off", [rows, tiles])
            self.s_off = st.sem(f"{name}_off_ready")

    def vector(self, nc, v, c, s_v, src, dst, s_dst=None, turn=1):
        norm_measure(self, nc, c, s_v, src, range(self.tiles))
        norm_apply(self, nc, v, c, s_v, src, dst, range(self.tiles), turn, s_dst)
        if s_dst is not None:
            v.wait_ge(s_dst, turn * self.tiles)

    def scalar(self, nc, act, turn=1):
        norm_root(self, nc, act, range(self.tiles), turn)


def norm_measure(ln, nc, c, s_v, src, tiles):
    at = slice(tiles.start, tiles.stop)
    row_stats(c, s_v, nc, src, ln.stats, ln.mv, tiles)
    c.chain(ln.s_var, nc.vector.tensor_scalar(ln.var[:, at], ln.mv[:, at, 1], EPS, None, ALU.add))


def norm_root(ln, nc, act, tiles, turn):
    at = slice(tiles.start, tiles.stop)
    act.wait_ge(ln.s_var, turn)
    nc.scalar.activation(ln.std[:, at], ln.var[:, at], ACT.Sqrt).then_inc(ln.s_std, 1)


def norm_rows(ln, nc, src, dst, tiles, s_dst=None):
    for t in tiles:
        ins = nc.vector.tensor_scalar(dst[:, t, :], src[:, t, :], ln.mv[:, t, 0:1], ln.rstd[:, t:t + 1],
                                      ALU.subtract, ALU.mult)
        if s_dst is not None:
            ins.then_inc(s_dst, 1)
    return ins


def norm_apply(ln, nc, v, c, s_v, src, dst, tiles, turn, s_dst=None):
    at = slice(tiles.start, tiles.stop)
    v.wait_ge(ln.s_std, turn)
    c.chain(s_v, nc.vector.reciprocal(ln.rstd[:, at], ln.std[:, at]))
    ins = norm_rows(ln, nc, src, dst, tiles, s_dst)
    if s_dst is None:
        c.chain(s_v, ins)


def norm_factors(ln, nc, v, c, s_v, tiles, turn):
    at = slice(tiles.start, tiles.stop)
    v.wait_ge(ln.s_std, turn)
    c.chain(s_v, nc.vector.reciprocal(ln.rstd[:, at], ln.std[:, at]))
    nc.vector.scalar_tensor_tensor(out=ln.off[:, at], in0=ln.mv[:, at, 0], scalar=-1.0, in1=ln.rstd[:, at],
                                   op0=ALU.mult, op1=ALU.mult).then_inc(ln.s_off, 1)


def norm_rows_scalar(ln, nc, act, src, dst, tiles, turn, s_dst):
    act.wait_ge(ln.s_off, turn)
    for t in tiles:
        nc.scalar.activation(dst[:, t, :], src[:, t, :], ACT.Identity, scale=ln.rstd[:, t:t + 1],
                             bias=ln.off[:, t:t + 1]).then_inc(s_dst, 1)


def load_rows(eng, dst, dram, sem):
    full, last = rows_view(dram)
    eng.dma_start(dst[:, 0:TILES - 1, :], full).then_inc(sem, 16)
    eng.dma_start(dst[0:LAST, TILES - 1, :], last).then_inc(sem, 16)


def rel_attn_stage(nc, a, h_dram, resid):
    NB = 40
    QT = NB // 4
    HJ = HEADS * IMGS
    PITCH = (IMGS + 1) * HEADS
    with ExitStack() as ctx:
        st = Stage(nc, ctx, "rel")
        ident = st.sb("ident", [P, P])
        rep = st.sb("rep", [P, P * HEADS])
        hmask = st.sb("hmask", [P, HEADS])
        hrows = st.sb("hrows", [P, P])
        post = st.sb("post", [P, IMGS])
        wnat = st.sb("wnat", [P, 5, P])
        wt = st.sb("wt", [P, 5, P])
        cols = st.sb("cols", [P, 4])
        w = st.sb("w", [TP, TILES, D])
        wn = st.sb("wn", [TP, TILES, D])
        wnt = st.sb("wnt", [P, NB, IMGS])
        qw = st.sb("qw", [P, NB * IMGS])
        qr = st.sb("qr", [P, NB * IMGS])
        kexp = st.sb("kexp", [P, NB * IMGS, HEADS])
        rk = st.sb("rk", [P, IMGS])
        rexp = st.sb("rexp", [P, IMGS, HEADS])
        bdp = st.sb("bdp", [P, QT, PITCH])
        bds = st.sb("bds", [P, QT, HJ])
        vrow = st.sb("vrow", [P, QT, P])
        vexp = st.sb("vexp", [P, NB * 2, P])
        sc = st.sb("sc", [P, 2, HJ])
        mx = st.sb("mx", [P, 2, HEADS])
        pr = st.sb("pr", [P, 2, HJ])
        den = st.sb("den", [P, 2, HEADS])
        rden = st.sb("rden", [P, 4, HEADS])
        pt = st.sb("pt", [P, 2, 2, P])
        av = st.sb("av", [P, 2, P])
        avt = st.sb("avt", [P, 2, P])
        ao = st.sb("ao", [P, QT, P])
        aor = st.sb("aor", [TP, TILES, D])
        ps = st.ps("ps")
        ln1, ln2 = Norm(st, "ln1", TP, TILES), Norm(st, "ln2", TP, TILES)
        names = ("const", "w", "h", "zero", "v", "wn", "wnt_tp", "wnt", "wt_tp", "wt", "rk", "rexp", "q", "qr", "k", "kx",
                 "v_mm", "v_sb", "vr", "vx", "bd", "bd_sb", "bd_out", "bd_in", "ac", "s", "sub", "e", "den", "pt", "pt_sb",
                 "pv", "av", "avt", "avt_sb", "wo", "ao", "ao_out", "ao_in")
        S = {n: st.sem(n) for n in names}
        bd_dram = nc.dram_tensor("rel_pos_scores", (NB, IMGS * PITCH), F32, kind="Internal").ap()
        ao_dram = nc.dram_tensor("rel_out_rows", (NTOK, D), F32, kind="Internal").ap()
        block = ctx.enter_context(nc.Block())

        @block.sync
        def _(sp):
            sp.wait_ge(S["zero"], 1)
            load_rows(sp, resid, h_dram, S["h"])
            sp.dma_start(ident[:], const(a["consts"], "ident")).then_inc(S["const"], 16)
            sp.dma_start(post[:], const(a["consts"], "rel_pos_t")).then_inc(S["const"], 16)
            sp.dma_start(hmask[:], const(a["consts"], "head_mask")).then_inc(S["const"], 16)
            sp.dma_start(hrows[:], const(a["consts"], "head_rows")).then_inc(S["const"], 16)
            sp.dma_start(rep[:], const(a["consts"], "ident_rep")).then_inc(S["const"], 16)
            sp.wait_ge(S["bd_sb"], QT // 2)
            sp.dma_start(bd_dram.rearrange("n (i c) -> (n i) c", i=IMGS).rearrange("(t p) c -> p t c", p=P), bdp[:]).then_inc(S["bd_out"], 16)
            sp.wait_ge(S["bd_out"], 16)
            shifted = bd_dram[:, HJ:HJ + IMGS * HJ].rearrange("(t b) (i c) -> b i t c", b=4, i=IMGS)
            for b in range(4):
                sp.dma_start(bds[32 * b:32 * b + 32, :, :], shifted[b]).then_inc(S["bd_in"], 16)
            sp.wait_ge(S["ao"], QT)
            dst = ao_dram.rearrange("(i n) d -> i n d", n=TOK)
            for b in range(4):
                n = QT if b == 0 else QT - 1
                sp.dma_start(dst[:, b:b + 4 * (n - 1) + 1:4, :], ao[32 * b:32 * b + 32, 0:n, :]).then_inc(S["ao_out"], 16)
            sp.wait_ge(S["ao_out"], 64)
            load_rows(sp, aor, ao_dram, S["ao_in"])

        @block.scalar
        def _(act):
            for k in range(3):
                act.dma_start(wnat[:, k, :], a["L0_attn_Wqkv"][k * D:(k + 1) * D, :]).then_inc(S["w"], 16)
            act.dma_start(wnat[:, 3, :], a["L0_attn_Wr"]).then_inc(S["w"], 16)
            act.dma_start(wnat[:, 4, :], a["L0_attn_Wo"]).then_inc(S["w"], 16)
            act.dma_start(cols[:, 0:1], a["L0_attn_ln_gamma"].rearrange("(d o) -> d o", o=1)).then_inc(S["w"], 16)
            act.dma_start(cols[:, 1:2], a["L0_attn_ln_beta"].rearrange("(d o) -> d o", o=1)).then_inc(S["w"], 16)
            act.dma_start(cols[:, 2:3], a["L0_attn_r_w_bias"].rearrange("n (d o) -> (n d) o", o=1)).then_inc(S["w"], 16)
            act.dma_start(cols[:, 3:4], a["L0_attn_r_r_bias"].rearrange("n (d o) -> (n d) o", o=1)).then_inc(S["w"], 16)
            ln1.scalar(nc, act)
            ln2.scalar(nc, act)
            act.wait_ge(S["w"], 16 * 9)
            for n in range(3):
                act.wait_ge(S["q"], n + 1)
                wd = min(512, NB * IMGS - 512 * n)
                nc.scalar.activation(qr[:, 512 * n:512 * n + wd], ps[:, n, 0:wd], ACT.Identity, bias=cols[:, 3:4]).then_inc(S["qr"], 1)
            for n in range(5):
                act.wait_ge(S["bd"], 2 * n + 2)
                nc.scalar.copy(bdp[:, 2 * n:2 * n + 2, HEADS:PITCH], ps[:, 4 + n % 2, :].rearrange("p (t c) -> p t c", t=2)).then_inc(S["bd_sb"], 1)
            for n in range(3):
                act.wait_ge(S["v_mm"], n + 1)
                wd = min(4, QT - 4 * n)
                nc.scalar.copy(vrow[:, 4 * n:4 * n + wd, :].rearrange("p t d -> p (t d)"), ps[:, 6 + n % 2, 0:wd * P]).then_inc(S["v_sb"], 1)
            for t in range(QT + 5):
                if t < QT:
                    act.wait_ge(S["sub"], t + 1)
                    if t >= 2:
                        act.wait_ge(S["pt"], t - 1)
                        act.wait_ge(S["den"], t - 1)
                    nc.scalar.activation(pr[:, t % 2, :], sc[:, t % 2, :], ACT.Exp, scale=float(DH) ** -0.5).then_inc(S["e"], 1)
                u = t - 1
                if 0 <= u < QT:
                    act.wait_ge(S["pt"], u + 1)
                    if u >= 2:
                        act.wait_ge(S["pv"], u - 1)
                    nc.scalar.copy(pt[:, u % 2, :, :].rearrange("p a b -> p (a b)"), ps[:, 2 + u % 2, 0:2 * P]).then_inc(S["pt_sb"], 1)
                u = t - 3
                if 0 <= u < QT:
                    act.wait_ge(S["avt"], u + 1)
                    if u >= 2:
                        act.wait_ge(S["wo"], u - 1)
                    nc.scalar.copy(avt[:, u % 2, :], ps[:, 6, 0:P]).then_inc(S["avt_sb"], 1)
                u = t - 4
                if 0 <= u < QT:
                    act.wait_ge(S["wo"], u + 1)
                    nc.scalar.copy(ao[:, u, :], ps[:, 7, 0:P]).then_inc(S["ao"], 1)

        @block.tensor
        def _(pe):
            pe.wait_ge(S["const"], 80)
            pe.wait_ge(S["w"], 16 * 9)
            for k in range(5):
                last = nc.tensor.transpose(ps[:, 6 + k // 4, (k % 4) * P:(k % 4) * P + P], wnat[:, k, :], ident[:])
            last.then_inc(S["wt_tp"], 1)
            for t in range(TILES):
                pe.wait_ge(S["wn"], t + 1)
                last = nc.tensor.transpose(ps[:, 3 + t // 4, (t % 4) * TP:(t % 4) * TP + TP], wn[:, t, :], ident[0:TP, 0:TP])
                if t % 4 == 3 or t == TILES - 1:
                    last.then_inc(S["wnt_tp"], 1)
            pe.wait_ge(S["wt"], 1)
            nc.tensor.matmul(ps[:, 7, 128:128 + IMGS], wt[:, 3, :], post[:], start=True, stop=True).then_inc(S["rk"], 1)
            flat = wnt[:].rearrange("p n i -> p (n i)")
            pe.wait_ge(S["wnt"], 3)
            for n in range(3):
                wd = min(512, NB * IMGS - 512 * n)
                nc.tensor.matmul(ps[:, n, 0:wd], wt[:, 0, :], flat[:, 512 * n:512 * n + wd], start=True, stop=True).then_inc(S["q"], 1)
            for n in range(3):
                wd = min(512, NB * IMGS - 512 * n)
                nc.tensor.matmul(ps[:, 3 + n, 0:wd], wt[:, 1, :], flat[:, 512 * n:512 * n + wd], start=True, stop=True).then_inc(S["k"], 1)
            pe.wait_ge(S["kx"], 3)
            pe.wait_ge(S["rexp"], 2)
            pe.wait_ge(S["qr"], 3)
            for t in range(QT):
                if t % 2 == 0 and t >= 4:
                    pe.wait_ge(S["bd_sb"], t // 2 - 1)
                nc.tensor.matmul(ps[:, 4 + (t // 2) % 2, (t % 2) * HJ:(t % 2) * HJ + HJ], qr[:, t * P:(t + 1) * P],
                                 rexp[:].rearrange("p j n -> p (j n)"), start=True, stop=True).then_inc(S["bd"], 1)
            for t in range(QT):
                if t == 8:
                    pe.wait_ge(S["v_sb"], 1)
                last = nc.tensor.matmul(ps[:, 6 + (t // 4) % 2, (t % 4) * P:(t % 4) * P + P], flat[:, t * P:(t + 1) * P], wt[:, 2, :], start=True, stop=True)
                if t % 4 == 3 or t == QT - 1:
                    last.then_inc(S["v_mm"], 1)
            pe.wait_ge(S["v_sb"], 3)
            pe.wait_ge(S["bd_sb"], 5)
            for n in range(2 * NB):
                t, b, half = n // 8, (n // 2) % 4, n % 2
                if n % 4 == 0 and n >= 8:
                    pe.wait_ge(S["vx"], n // 4 - 1)
                at = (32 * b + 16 * half) * HEADS
                last = nc.tensor.matmul(ps[:, 4 + (n // 4) % 2, (n % 4) * P:(n % 4) * P + P], rep[:, at:at + P], vrow[:, t, :], start=True, stop=True)
                if n % 4 == 3:
                    last.then_inc(S["vr"], 1)
            pe.wait_ge(S["vx"], 2 * NB // 4)
            for t in range(QT + 4):
                if t < QT:
                    if t >= 2:
                        pe.wait_ge(S["s"], t - 1)
                    for b in range(4):
                        tok = 4 * t + b
                        last = nc.tensor.matmul(ps[32 * b:32 * b + 32, t % 2, 0:HJ], qw[:, tok * IMGS:(tok + 1) * IMGS],
                                                kexp[:, tok * IMGS:(tok + 1) * IMGS, :].rearrange("p j n -> p (j n)"), start=True, stop=True)
                    last.then_inc(S["ac"], 1)
                u = t - 1
                if 0 <= u < QT:
                    pe.wait_ge(S["e"], u + 1)
                    if u >= 2:
                        pe.wait_ge(S["pt_sb"], u - 1)
                    for half in range(2):
                        last = nc.tensor.transpose(ps[:, 2 + u % 2, half * P:half * P + P], pr[:, u % 2, half * P:half * P + P], ident[:])
                    last.then_inc(S["pt"], 1)
                u = t - 2
                if 0 <= u < QT:
                    pe.wait_ge(S["pt_sb"], u + 1)
                    if u >= 2:
                        pe.wait_ge(S["av"], u - 1)
                    for b in range(4):
                        for half in range(2):
                            last = nc.tensor.matmul(ps[32 * b:32 * b + 32, 4 + u % 2, 0:P], pt[:, u % 2, half, 32 * b:32 * b + 32],
                                                    vexp[:, (4 * u + b) * 2 + half, :], start=(half == 0), stop=(half == 1))
                    last.then_inc(S["pv"], 1)
                u = t - 3
                if 0 <= u < QT:
                    pe.wait_ge(S["av"], u + 1)
                    if u >= 1:
                        pe.wait_ge(S["avt_sb"], u)
                    nc.tensor.transpose(ps[:, 6, 0:P], av[:, u % 2, :], ident[:]).then_inc(S["avt"], 1)
                u = t - 4
                if 0 <= u < QT:
                    pe.wait_ge(S["avt_sb"], u + 1)
                    if u >= 1:
                        pe.wait_ge(S["ao"], u)
                    nc.tensor.matmul(ps[:, 7, 0:P], avt[:, u % 2, :], wt[:, 4, :], start=True, stop=True).then_inc(S["wo"], 1)

        @block.vector
        def _(v):
            c = Counts(v)
            nc.vector.memset(resid[:, TILES - 1, :], 0.0).then_inc(S["zero"], 1)
            c.chain(S["v"], nc.vector.memset(wnt[:, TOK:NB, :], 0.0))
            c.chain(S["v"], nc.vector.memset(bdp[:, :, 0:HEADS], 0.0))
            v.wait_ge(S["h"], 32)
            ln1.vector(nc, v, c, S["v"], resid, w)
            ln2.vector(nc, v, c, S["v"], w, wn, S["wn"])
            c.chain(S["v"], nc.vector.tensor_tensor(resid[:], resid[:], w[:], ALU.add))
            v.wait_ge(S["wt_tp"], 1)
            c.chain(S["v"], nc.vector.tensor_copy(wt[:, 0:4, :].rearrange("p q m -> p (q m)"), ps[:, 6, :]))
            nc.vector.tensor_copy(wt[:, 4, :], ps[:, 7, 0:P]).then_inc(S["wt"], 1)
            v.wait_ge(S["w"], 16 * 9)
            for n in range(3):
                v.wait_ge(S["wnt_tp"], n + 1)
                m = min(12, IMGS - 12 * n)
                nc.vector.tensor_scalar(wnt[:, 0:TOK, 12 * n:12 * n + m].rearrange("p t i -> p i t"),
                                        ps[:, 3 + n, 0:m * TOK].rearrange("p (i t) -> p i t", t=TOK),
                                        cols[:, 0:1], cols[:, 1:2], ALU.mult, ALU.add).then_inc(S["wnt"], 1)
            v.wait_ge(S["rk"], 1)
            c.chain(S["rexp"], nc.vector.tensor_copy(rk[:], ps[:, 7, 128:128 + IMGS]))
            c.chain(S["rexp"], nc.vector.tensor_tensor(rexp[:], rk[:].unsqueeze(2).to_broadcast([P, IMGS, HEADS]),
                                                       hmask[:].unsqueeze(1).to_broadcast([P, IMGS, HEADS]), ALU.mult))
            for n in range(3):
                wd = min(512, NB * IMGS - 512 * n)
                v.wait_ge(S["qr"], n + 1)
                c.chain(S["v"], nc.vector.tensor_scalar(qw[:, 512 * n:512 * n + wd], ps[:, n, 0:wd], cols[:, 2:3], None, ALU.add))
            for n in range(3):
                wd = min(512, NB * IMGS - 512 * n)
                v.wait_ge(S["k"], n + 1)
                nc.vector.tensor_tensor(kexp[:, 512 * n:512 * n + wd, :], ps[:, 3 + n, 0:wd].unsqueeze(2).to_broadcast([P, wd, HEADS]),
                                        hmask[:].unsqueeze(1).to_broadcast([P, wd, HEADS]), ALU.mult).then_inc(S["kx"], 1)
            for n in range(2 * NB // 4):
                v.wait_ge(S["vr"], n + 1)
                nc.vector.tensor_tensor(vexp[:, 4 * n:4 * n + 4, :], ps[:, 4 + n % 2, :].rearrange("p (a d) -> p a d", a=4),
                                        hrows[:].unsqueeze(1).to_broadcast([P, 4, P]), ALU.mult).then_inc(S["vx"], 1)
            v.wait_ge(S["bd_in"], 64)
            for t in range(QT + 2):
                if t < QT:
                    v.wait_ge(S["ac"], t + 1)
                    if t >= 2:
                        v.wait_ge(S["e"], t - 1)
                    c.chain(S["s"], nc.vector.tensor_tensor(sc[:, t % 2, :], ps[:, t % 2, 0:HJ], bds[:, t, :], ALU.add))
                    sv = sc[:, t % 2, :].rearrange("p (j n) -> p j n", n=HEADS)
                    c.chain(S["v"], nc.vector.tensor_reduce(mx[:, t % 2, :], sv.rearrange("p j n -> p n j"), AX_X, ALU.max))
                    nc.vector.tensor_tensor(sv, sv, mx[:, t % 2, :].unsqueeze(1).to_broadcast([P, IMGS, HEADS]), ALU.subtract).then_inc(S["sub"], 1)
                u = t - 1
                if 0 <= u < QT:
                    v.wait_ge(S["e"], u + 1)
                    c.chain(S["den"], nc.vector.tensor_reduce(den[:, u % 2, :], pr[:, u % 2, :].rearrange("p (j n) -> p n j", n=HEADS), AX_X, ALU.add))
                    c.chain(S["v"], nc.vector.reciprocal(rden[:, u % 4, :], den[:, u % 2, :]))
                u = t - 2
                if 0 <= u < QT:
                    v.wait_ge(S["pv"], u + 1)
                    if u >= 2:
                        v.wait_ge(S["avt"], u - 1)
                    nc.vector.tensor_tensor(av[:, u % 2, :].rearrange("p (n d) -> p n d", n=HEADS),
                                            ps[:, 4 + u % 2, 0:P].rearrange("p (n d) -> p n d", n=HEADS),
                                            rden[:, u % 4, :].unsqueeze(2).to_broadcast([P, HEADS, DH]), ALU.mult).then_inc(S["av"], 1)
            v.wait_ge(S["ao_in"], 32)
            c.chain(S["v"], nc.vector.tensor_tensor(resid[:, 0:TILES - 1, :], resid[:, 0:TILES - 1, :], aor[:, 0:TILES - 1, :], ALU.add))
            c.chain(S["v"], nc.vector.tensor_tensor(resid[0:LAST, TILES - 1, :], resid[0:LAST, TILES - 1, :], aor[0:LAST, TILES - 1, :], ALU.add))


def transpose_rows(nc, pe, rows, ident, ps, bank0, s_rows, s_tp):
    for t in range(TILES):
        pe.wait_ge(s_rows, t + 1)
        last = nc.tensor.transpose(ps[:, bank0 + t // 4, (t % 4) * TP:(t % 4) * TP + TP], rows[:, t, :], ident[0:TP, 0:TP])
        if t % 4 == 3 or t == TILES - 1:
            last.then_inc(s_tp, 1)


SPANS = [(4 * n * TP, min(4, TILES - 4 * n) * TP) for n in range(3)]


def lstm_stage(nc, a, resid):
    F16 = mybir.dt.float16
    KE = 2 * EXPERTS
    G = 4
    EG = EXPERTS // 2
    N = 2 * TOK
    with ExitStack() as ctx:
        st = Stage(nc, ctx, "moe")
        gate_half = st.sb("gate_half", [P, 1])
        w_hi = [st.sb(f"w_hi{n}", [P, EXPERTS, G, P], F16) for n in range(2)]
        w_lo = [st.sb(f"w_lo{n}", [P, EXPERTS, G, P], F16) for n in range(2)]
        scale = st.sb("scale", [P, 6])
        sbits = st.sb("sbits", [P, 2], U32)
        brow = st.sb("brow", [P, 32, P], BF16)
        ones = st.sb("ones", [P, N], BF16)
        wo = st.sb("wo", [P, EXPERTS, P])
        bo = st.sb("bo", [EXPERTS, P])
        x_hi = st.sb("x_hi", [P, COLS], F16)
        x_lo = st.sb("x_lo", [P, COLS], F16)
        ct = st.sb("ct", [EXPERTS, COLS])
        mask = st.sb("mask", [P, KE, COLS], F16)
        rwt = st.sb("rwt", [P, 2, COLS])
        cell = st.sb("cell", [P, 2, EG, N])
        hs = st.sb("hs", [P, EXPERTS, COLS])
        ps = st.ps("ps")
        names = ("const", "w", "bias", "wo", "zero", "v", "pool", "xn", "xt_tp", "xt", "lg", "top", "e1", "pack", "mt_tp", "mt",
                 "bc", "bc_v", "bc_a", "amax", "allmax", "scale", "w_hi", "w_lo", "wf_used", "wf1", "bparts", "brow", "y", "y_sb",
                 "lv", "xm", "hm", "wst", "hs", "table")
        S = {n: st.sem(n) for n in names}
        s_gates = [st.sem(f"gates_mm{g}") for g in range(2)]
        s_tanh = [st.sem(f"gates_tanh{g}") for g in range(2)]
        s_cell = [st.sem(f"cell{g}") for g in range(2)]
        s_tc = [st.sem(f"cell_tanh{g}") for g in range(2)]
        s_h = [st.sem(f"state{g}") for g in range(2)]
        blocks = [(j, n) for j in range(18) for n in range(3)]

        def by_vector(b):
            return b % 2 == 0

        with ExitStack() as before:
            pre = Stage(nc, before, "moe")
            ident = pre.sb("ident", [P, P])
            iota = pre.sb("iota", [P, 8])
            row_sel = pre.sb("row_sel", [18, 18, P])
            row_sel16 = pre.sb("row_sel16", [18, KE, P], F16)
            rw = pre.sb("rw", [P, EXPERTS])
            rb = pre.sb("rb", [TP, EXPERTS])
            wf = pre.sb("wf", [P, EXPERTS, G, P])
            amax = pre.sb("amax", [P, 4])
            bf = pre.sb("bf", [32, P])
            bparts = pre.sb("bparts", [32, 3, P], BF16)
            brem = pre.sb("brem", [32, 2, P])
            xn = pre.sb("xn", [TP, TILES, D])
            xt = pre.sb("xt", [P, COLS])
            lg = pre.sb("lg", [TP, TILES, 8])
            top = pre.sb("top", [TP, TILES, 8])
            topi = pre.sb("topi", [TP, TILES, 8], U32)
            topf = pre.sb("topf", [TP, TILES, 2])
            pack = pre.sb("pack", [TP, TILES, 18])
            comb = pre.sb("comb", [TP, TILES, 2, 8])
            e1 = pre.sb("e1", [TP, TILES, 3])
            mt = pre.sb("mt", [18, COLS])
            mt16 = pre.sb("mt16", [18, COLS], F16)
            ln = Norm(pre, "ln", TP, TILES)
            with nc.Block() as block:
                @block.sync
                def _(sp):
                    sp.dma_start(ident[:], const(a["consts"], "ident")).then_inc(S["const"], 16)
                    sp.dma_start(rw[:], a["L0_ffn_router_w"]).then_inc(S["const"], 16)
                    sp.dma_start(rb[:], a["L0_ffn_router_b"].partition_broadcast(TP)).then_inc(S["const"], 16)
                    sp.dma_start(iota[:], const(a["consts"], "iota8")).then_inc(S["const"], 16)
                    sp.dma_start(gate_half[:], const(a["consts"], "gate_half"), allow_slow_non_contiguous=True).then_inc(S["const"], 16)
                    sp.dma_start(row_sel[:], const(a["consts"], "row_sel", 18).rearrange("p (j m) -> p j m", j=18)).then_inc(S["const"], 16)
                    sp.dma_start(bf[:], a["L0_ffn_b"].rearrange("e (g h) -> (e g) h", g=G)).then_inc(S["bias"], 16)
                    sp.dma_start(wo[:], a["L0_ffn_Wo"].rearrange("e h o -> h e o")).then_inc(S["wo"], 16)
                    sp.dma_start(bo[:], a["L0_ffn_bo"]).then_inc(S["wo"], 16)
                    sp.wait_ge(S["bparts"], 5)
                    sp.wait_ge(S["zero"], 2)
                    for k in range(3):
                        sp.dma_start(brow[k:k + 1, :, :], bparts[:, k, :]).then_inc(S["brow"], 16)
                    sp.wait_ge(S["brow"], 48)

                @block.scalar
                def _(act):
                    act.dma_start(wf[:], a["L0_ffn_Wi"].rearrange("e i (g h) -> i e g h", g=G)).then_inc(S["w"], 16)
                    act.dma_start(hs_as_w(hs), a["L0_ffn_Wh"].rearrange("e i (g h) -> i e g h", g=G)).then_inc(S["w"], 16)
                    ln.scalar(nc, act)
                    act.wait_ge(S["top"], 2)
                    nc.scalar.activation(e1[:, :, 1], e1[:, :, 0], ACT.Exp).then_inc(S["e1"], 1)
                    act.wait_ge(S["scale"], 6)
                    act.wait_ge(S["w"], 32)
                    for n, src in enumerate((wf[:], hs_as_w(hs))):
                        for g0, g1, col in ((0, 2, 1 + n), (2, 3, n), (3, 4, 1 + n)):
                            nc.scalar.activation(w_hi[n][:, :, g0:g1, :], src[:, :, g0:g1, :], ACT.Copy, scale=scale[:, col:col + 1]).then_inc(S["w_hi"], 1)
                    for b, (j, n) in enumerate(blocks):
                        if not by_vector(b):
                            act.wait_ge(S["bc"], b + 1)
                            at, wd = SPANS[n]
                            dst = mask[:, j, at:at + wd] if j < KE else rwt[:, j - KE, at:at + wd]
                            nc.scalar.copy(dst, ps[:, b % 6, 0:wd]).then_inc(S["bc_a"], 1)

                @block.gpsimd
                def _(pool):
                    nc.gpsimd.memset(ones[:], 1.0).then_inc(S["zero"], 1)
                    nc.gpsimd.memset(brow[:], 0.0).then_inc(S["zero"], 1)
                    for g in range(2):
                        nc.gpsimd.memset(cell[:, g, :, :], 0.0).then_inc(S["zero"], 1)
                    pool.wait_ge(S["amax"], 1)
                    nc.gpsimd.partition_all_reduce(amax[:, 3:4], amax[:, 2:3], P, bass.bass_isa.ReduceOp.max).then_inc(S["allmax"], 1)

                @block.tensor
                def _(pe):
                    pe.wait_ge(S["const"], 96)
                    transpose_rows(nc, pe, xn, ident, ps, 0, S["xn"], S["xt_tp"])
                    pe.wait_ge(S["xt"], 3)
                    for t in range(TILES):
                        last = nc.tensor.matmul(ps[0:TP, 3, 8 * t:8 * t + 8], xt[:, t * TP:(t + 1) * TP], rw[:], start=True, stop=True)
                    last.then_inc(S["lg"], 1)
                    pe.wait_ge(S["pack"], 1)
                    for t in range(TILES):
                        last = nc.tensor.transpose(ps[0:18, t // 4, (t % 4) * TP:(t % 4) * TP + TP], pack[:, t, :], ident[0:TP, 0:TP])
                    for t in range(TILES):
                        last = nc.tensor.transpose(ps[0:8, 3 + t // 4, (t % 4) * TP:(t % 4) * TP + TP], comb[:, t, 0, :], ident[0:TP, 0:TP])
                    last.then_inc(S["mt_tp"], 1)
                    pe.wait_ge(S["mt"], 10)
                    for b, (j, n) in enumerate(blocks):
                        at, wd = SPANS[n]
                        if b >= 6:
                            o = b - 6
                            pe.wait_ge(S["bc_v"] if by_vector(o) else S["bc_a"], o // 2 + 1)
                        lhs, rhs = (row_sel16, mt16) if j < KE else (row_sel, mt)
                        nc.tensor.matmul(ps[:, b % 6, 0:wd], lhs[:, j, :], rhs[:, at:at + wd], start=True, stop=True).then_inc(S["bc"], 1)

                @block.vector
                def _(v):
                    c = Counts(v)
                    ln.vector(nc, v, c, S["v"], resid, xn, S["xn"])
                    for n, (at, wd) in enumerate(SPANS):
                        v.wait_ge(S["xt_tp"], n + 1)
                        nc.vector.tensor_copy(xt[:, at:at + wd], ps[:, n, 0:wd]).then_inc(S["xt"], 1)
                    v.wait_ge(S["xt"], 3)
                    c.chain(S["v"], nc.vector.tensor_copy(x_hi[:], xt[:]))
                    c.chain(S["v"], nc.vector.tensor_tensor(x_lo[:], xt[:], x_hi[:], ALU.subtract))
                    v.wait_ge(S["lg"], 1)
                    v.wait_ge(S["const"], 96)
                    c.chain(S["v"], nc.vector.tensor_tensor(lg[:], ps[0:TP, 3, 0:8 * TILES].rearrange("p (t e) -> p t e", e=8),
                                                            rb[:].unsqueeze(1).to_broadcast([TP, TILES, 8]), ALU.add))
                    for t in range(TILES):
                        ins = nc.vector.max(top[:, t, :], lg[:, t, :])
                    c.chain(S["v"], ins)
                    for t in range(TILES):
                        ins = nc.vector.max_index(topi[:, t, :], top[:, t, :], lg[:, t, :])
                    c.chain(S["top"], ins)
                    c.chain(S["top"], nc.vector.tensor_tensor(e1[:, :, 0], top[:, :, 1], top[:, :, 0], ALU.subtract))
                    c.chain(S["v"], nc.vector.tensor_copy(topf[:], topi[:, :, 0:2]))
                    for k in range(2):
                        ins = nc.vector.tensor_tensor(pack[:, :, 8 * k:8 * k + 8], iota[0:TP, :].unsqueeze(1).to_broadcast([TP, TILES, 8]),
                                                      topf[:, :, k:k + 1].to_broadcast([TP, TILES, 8]), ALU.is_equal)
                    v.wait_ge(S["e1"], 1)
                    c.chain(S["v"], nc.vector.tensor_scalar(e1[:, :, 2], e1[:, :, 1], 1.0, None, ALU.add))
                    c.chain(S["v"], nc.vector.reciprocal(pack[:, :, 16], e1[:, :, 2]))
                    c.chain(S["v"], nc.vector.tensor_tensor(pack[:, :, 17], pack[:, :, 16], e1[:, :, 1], ALU.mult))
                    for k in range(2):
                        ins = nc.vector.tensor_tensor(comb[:, :, k, :], pack[:, :, 8 * k:8 * k + 8],
                                                      pack[:, :, 16 + k:17 + k].to_broadcast([TP, TILES, 8]), ALU.mult)
                    c.chain(S["v"], ins)
                    c.chain(S["pack"], nc.vector.tensor_tensor(comb[:, :, 0, :], comb[:, :, 0, :], comb[:, :, 1, :], ALU.add))
                    v.wait_ge(S["mt_tp"], 1)
                    nc.vector.tensor_copy(row_sel16[:], row_sel[:, 0:KE, :]).then_inc(S["mt"], 1)
                    for n, (at, wd) in enumerate(SPANS):
                        nc.vector.tensor_copy(mt[:, at:at + wd], ps[0:18, n, 0:wd]).then_inc(S["mt"], 1)
                        nc.vector.tensor_copy(mt16[:, at:at + wd], ps[0:18, n, 0:wd]).then_inc(S["mt"], 1)
                        nc.vector.tensor_scalar(ct[:, at:at + wd], ps[0:8, 3 + n, 0:wd], 2.0, None, ALU.mult).then_inc(S["mt"], 1)
                    v.wait_ge(S["w"], 32)
                    nc.vector.tensor_reduce(amax[:, 0:1], wf[:].rearrange("p e g h -> p (e g h)"), AX_X, ALU.max, apply_absolute_value=True)
                    c.chain(S["v"], nc.vector.tensor_reduce(amax[:, 1:2], hs_as_w(hs).rearrange("p e g h -> p (e g h)"), AX_X, ALU.max, apply_absolute_value=True))
                    c.chain(S["v"], nc.vector.tensor_tensor(amax[:, 2:3], amax[:, 0:1], amax[:, 1:2], ALU.max))
                    c.chain(S["amax"], nc.vector.tensor_copy(amax[:, 0:1], amax[:, 2:3]))
                    v.wait_ge(S["allmax"], 1)
                    c.chain(S["v"], nc.vector.tensor_scalar(amax[:, 3:4], amax[:, 3:4], 1e-25, None, ALU.max))
                    c.chain(S["v"], nc.vector.tensor_scalar(sbits[:, 0:1], amax[:, 3:4].bitcast(U32), 0x7F800000, None, ALU.bitwise_and))
                    c.chain(S["v"], nc.vector.tensor_scalar(sbits[:, 1:2], sbits[:, 0:1], -1.0, float(267 << 23), ALU.mult, ALU.add))
                    c.chain(S["scale"], nc.vector.tensor_copy(scale[:, 0:1], sbits[:, 1:2].bitcast(F32)))
                    c.chain(S["scale"], nc.vector.tensor_scalar(scale[:, 1:2], scale[:, 0:1], 0.5, None, ALU.mult))
                    c.chain(S["scale"], nc.vector.tensor_scalar(scale[:, 2:3], scale[:, 0:1], 0.25, None, ALU.mult))
                    c.chain(S["scale"], nc.vector.tensor_scalar(scale[:, 3:4], sbits[:, 0:1].bitcast(F32), 2.0 ** -13, None, ALU.mult))
                    c.chain(S["scale"], nc.vector.tensor_tensor(scale[:, 4:5], scale[:, 0:1], gate_half[:], ALU.mult))
                    c.chain(S["scale"], nc.vector.tensor_copy(scale[:, 5:6], scale[:, 0:1]))
                    v.wait_ge(S["bias"], 16)
                    c.chain(S["v"], nc.vector.tensor_scalar(brem[:, 0, :], bf[:], scale[0:32, 4:5], None, ALU.mult))
                    c.chain(S["bparts"], nc.vector.tensor_copy(bparts[:, 0, :], brem[:, 0, :]))
                    c.chain(S["bparts"], nc.vector.tensor_tensor(brem[:, 1, :], brem[:, 0, :], bparts[:, 0, :], ALU.subtract))
                    c.chain(S["bparts"], nc.vector.tensor_copy(bparts[:, 1, :], brem[:, 1, :]))
                    c.chain(S["bparts"], nc.vector.tensor_tensor(brem[:, 0, :], brem[:, 1, :], bparts[:, 1, :], ALU.subtract))
                    c.chain(S["bparts"], nc.vector.tensor_copy(bparts[:, 2, :], brem[:, 0, :]))
                    for n, src in enumerate((wf[:], hs_as_w(hs))):
                        for k, (g0, g1, col) in enumerate(((0, 2, 1 + n), (2, 3, n), (3, 4, 1 + n))):
                            v.wait_ge(S["w_hi"], 3 * n + k + 1)
                            for e in range(EXPERTS):
                                nc.vector.scalar_tensor_tensor(out=w_lo[n][:, e, g0:g1, :], in0=src[:, e, g0:g1, :], scalar=scale[:, col:col + 1],
                                                               in1=w_hi[n][:, e, g0:g1, :], op0=ALU.mult, op1=ALU.subtract).then_inc(S["w_lo"], 1)
                    for b, (j, n) in enumerate(blocks):
                        if by_vector(b):
                            v.wait_ge(S["bc"], b + 1)
                            at, wd = SPANS[n]
                            dst = mask[:, j, at:at + wd] if j < KE else rwt[:, j - KE, at:at + wd]
                            nc.vector.tensor_copy(dst, ps[:, b % 6, 0:wd]).then_inc(S["bc_v"], 1)


        STEPS = 2
        TURNS = IMGS // STEPS
        with ExitStack() as during:
            loop = Stage(nc, during, "moe")
            xm_hi = loop.sb("xm_hi", [P, 2, KE, TOK], F16)
            xm_lo = loop.sb("xm_lo", [P, 2, KE, TOK], F16)
            gates = loop.sb("gates", [P, 2, EG, G, N])
            fc = loop.sb("fc", [P, 2, EG, N])
            ig = loop.sb("ig", [P, 2, EG, N])
            tc = loop.sb("tc", [P, 2, EG, N])
            hf = loop.sb("hf", [P, 2, 2, EG, N])
            hm = loop.sb("hm", [P, 2, EXPERTS, N])
            h_hi = loop.sb("h_hi", [P, 2, EG, N], F16)
            h_lo = loop.sb("h_lo", [P, 2, EG, N], F16)
            wst = loop.sb("wst", [P, 2, 2, EXPERTS, TOK])
            with nc.Block() as block:
                @block.tensor
                def _(pe):
                    with pe.Fori(0, TURNS) as i:
                        for s in range(STEPS):
                            pe.wait_ge(S["xm"], i * (2 * STEPS) + (2 * s + 2))
                            for g in range(2):
                                pe.wait_ge(s_tanh[g], i * STEPS + (s + 1))
                                for e in range(EG):
                                    ex = g * EG + e
                                    rhs = [m[:, s, ex:KE:EXPERTS, :] for m in (xm_hi, xm_hi, xm_lo)]
                                    for q in range(G):
                                        dst = ps[:, g * EG + e, q * N:(q + 1) * N]
                                        nc.tensor.matmul(dst, brow[:, ex * G + q, :], ones[:], start=(q == 0), stop=False, skip_group_check=True)
                                        for k, wgt in enumerate((w_hi, w_lo, w_hi)):
                                            nc.tensor.matmul(dst, wgt[0][:, ex, q, :], rhs[k], start=False, stop=False, skip_group_check=True)
                                pe.wait_ge(s_h[g], i * STEPS + (s + 1))
                                for e in range(EG):
                                    ex = g * EG + e
                                    for q in range(G):
                                        dst = ps[:, g * EG + e, q * N:(q + 1) * N]
                                        for k, (wgt, h) in enumerate(((w_hi, h_hi), (w_lo, h_hi), (w_hi, h_lo))):
                                            last = nc.tensor.matmul(dst, wgt[1][:, ex, q, :], h[:, g, e, :], start=False, stop=(k == 2), skip_group_check=True)
                                last.then_inc(s_gates[g], 1)

                @block.scalar
                def _(act):
                    for g in range(2):
                        nc.scalar.activation(tc[:, g, 0, 0:1], cell[:, g, 0, 0:1], ACT.Tanh).then_inc(s_tanh[g], 1)
                        act.wait_ge(s_tanh[g], 1)
                    with act.Fori(0, TURNS) as i:
                        for s in range(STEPS):
                            for g in range(2):
                                act.wait_ge(s_gates[g], i * STEPS + (s + 1))
                                nc.scalar.activation(gates[:, g, :, :, :].rearrange("p e q n -> p e (q n)"), ps[:, g * EG:(g + 1) * EG, 0:G * N],
                                                     ACT.Tanh, scale=scale[:, 3:4]).then_inc(s_tanh[g], 1)
                                act.wait_ge(s_cell[g], i * STEPS + (s + 1))
                                nc.scalar.activation(tc[:, g, :, :], cell[:, g, :, :], ACT.Tanh, scale=0.5).then_inc(s_tc[g], 1)

                @block.vector
                def _(v):
                    LV = 2 * 3
                    def mask_inputs(s, cols):
                        for n, (x, m) in enumerate(((x_hi, xm_hi), (x_lo, xm_lo))):
                            nc.vector.tensor_tensor(m[:, s, :, :], x[:, cols].unsqueeze(1).to_broadcast([P, KE, TOK]),
                                                    mask[:, :, cols], ALU.mult).then_inc(S["xm"], 1)

                    def cell_step(i, s, g):
                        v.wait_ge(s_tanh[g], i * STEPS + (s + 2))
                        nc.vector.scalar_tensor_tensor(out=fc[:, g, :, :], in0=gates[:, g, :, 1, :], scalar=1.0, in1=cell[:, g, :, :], op0=ALU.add, op1=ALU.mult)
                        nc.vector.scalar_tensor_tensor(out=ig[:, g, :, :], in0=gates[:, g, :, 0, :], scalar=1.0, in1=gates[:, g, :, 2, :],
                                                       op0=ALU.add, op1=ALU.mult).then_inc(S["lv"], 1)
                        v.wait_ge(S["lv"], i * (LV * STEPS) + (LV * s + 3 * g + 1))
                        nc.vector.scalar_tensor_tensor(out=cell[:, g, :, :], in0=fc[:, g, :, :], scalar=0.5, in1=ig[:, g, :, :],
                                                       op0=ALU.mult, op1=ALU.add).then_inc(s_cell[g], 1)

                    def state_step(i, s, g):
                        v.wait_ge(s_tc[g], i * STEPS + (s + 1))
                        nc.vector.scalar_tensor_tensor(out=h_hi[:, g, :, :], in0=gates[:, g, :, 3, :], scalar=1.0, in1=tc[:, g, :, :], op0=ALU.add,
                                                       op1=ALU.mult).then_inc(S["lv"], 1)
                        nc.vector.scalar_tensor_tensor(out=hf[:, s, g, :, :], in0=gates[:, g, :, 3, :], scalar=1.0, in1=tc[:, g, :, :], op0=ALU.add,
                                                       op1=ALU.mult).then_inc(S["lv"], 1)
                        v.wait_ge(S["lv"], i * (LV * STEPS) + (LV * s + 3 * g + 3))
                        nc.vector.tensor_tensor(h_lo[:, g, :, :], hf[:, s, g, :, :], h_hi[:, g, :, :], ALU.subtract).then_inc(s_h[g], 1)

                    def pick(s, cols):
                        nc.vector.tensor_tensor(hs[:, :, cols], hm[:, s, :, 0:TOK], hm[:, s, :, TOK:N], ALU.add).then_inc(S["hs"], 1)

                    for g in range(2):
                        nc.vector.memset(h_hi[:, g, :, :], 0.0).then_inc(S["hs"], 1)
                        v.wait_ge(S["hs"], g + 1)
                        nc.vector.memset(h_lo[:, g, :, :], 0.0).then_inc(s_h[g], 1)
                    mask_inputs(0, slice(0, TOK))
                    with v.Fori(0, TURNS) as i:
                        for s in range(STEPS):
                            if s == 0:
                                mask_inputs(1, bass.ds(i * (STEPS * TOK) + TOK, TOK))
                            else:
                                mask_inputs(0, bass.ds(i * (STEPS * TOK) + (STEPS * TOK), TOK))
                            v.wait_ge(S["hm"], i * (2 * STEPS) + (2 * s + 2))
                            pick(1 - s, bass.ds(i * (STEPS * TOK) + s * TOK, TOK))
                            cell_step(i, s, 0)
                            state_step(i, s, 0)
                            cell_step(i, s, 1)
                            state_step(i, s, 1)
                    v.wait_ge(S["hm"], 2 * IMGS + 2)
                    pick(1, slice(NTOK, COLS))

                @block.gpsimd
                def _(pool):
                    for g in range(2):
                        nc.gpsimd.memset(hm[:, 1, g * EG:(g + 1) * EG, :], 0.0).then_inc(S["hm"], 1)
                    with pool.Fori(0, TURNS) as i:
                        for s in range(STEPS):
                            cols = bass.ds(i * (STEPS * TOK) + s * TOK, TOK)
                            nc.gpsimd.tensor_tensor(wst[:, s, :, :, :], mask[:, :, cols].rearrange("p (k e) n -> p k e n", k=2),
                                                    rwt[:, :, cols].unsqueeze(2).to_broadcast([P, 2, EXPERTS, TOK]), ALU.mult).then_inc(S["wst"], 1)
                            pool.wait_ge(S["wst"], i * STEPS + (s + 1))
                            for g in range(2):
                                pool.wait_ge(s_h[g], i * STEPS + (s + 2))
                                nc.gpsimd.tensor_tensor(hm[:, s, g * EG:(g + 1) * EG, :].rearrange("p e (k n) -> p e k n", k=2),
                                                        hf[:, s, g, :, :].rearrange("p e (k n) -> p e k n", k=2),
                                                        wst[:, s, :, g * EG:(g + 1) * EG, :].rearrange("p k e n -> p e k n"), ALU.mult).then_inc(S["hm"], 1)

        with nc.Block() as block:
            @block.tensor
            def _(pe):
                pe.wait_ge(S["wo"], 32)
                for t in range(TILES):
                    if t >= 4:
                        pe.wait_ge(S["y_sb"], t - 2)
                    n = TP if t < TILES - 1 else LAST
                    dst = ps[0:n, t % 4, 0:P]
                    nc.tensor.matmul(dst, ct[:, t * TP:t * TP + n], bo[:], start=True, stop=False)
                    for e in range(EXPERTS):
                        last = nc.tensor.matmul(dst, hs[:, e, TOK + t * TP:TOK + t * TP + n], wo[:, e, :], start=False, stop=(e == EXPERTS - 1))
                    last.then_inc(S["y"], 1)

            @block.vector
            def _(v):
                for t in range(TILES):
                    n = TP if t < TILES - 1 else LAST
                    v.wait_ge(S["y"], t + 1)
                    nc.vector.scalar_tensor_tensor(out=resid[0:n, t, :], in0=ps[0:n, t % 4, 0:P], scalar=0.5, in1=resid[0:n, t, :],
                                                   op0=ALU.mult, op1=ALU.add).then_inc(S["y_sb"], 1)


def hs_as_w(hs):
    return hs[:].rearrange("p e n -> p (e n)")[:, 0:4096].rearrange("p (e g h) -> p e g h", e=EXPERTS, g=4)


def power_of_two(nc, c, s_v, top, bits, scale, inverse):
    c.chain(s_v, nc.vector.tensor_scalar(top, top, 1e-25, None, ALU.max))
    c.chain(s_v, nc.vector.tensor_scalar(bits[:, 0:1], top.bitcast(U32), 0x7F800000, None, ALU.bitwise_and))
    c.chain(s_v, nc.vector.tensor_scalar(bits[:, 1:2], bits[:, 0:1], -1.0, float(267 << 23), ALU.mult, ALU.add))
    c.chain(s_v, nc.vector.tensor_copy(scale, bits[:, 1:2].bitcast(F32)))
    c.chain(s_v, nc.vector.tensor_scalar(inverse, bits[:, 0:1].bitcast(F32), 2.0 ** -13, None, ALU.mult))


def thread_stage(nc, a, resid):
    F16 = mybir.dt.float16
    K = THREADS
    B = IMGS
    KT = K * TILES
    WIH, WHH, WQ, WK, WV, WB, WM = 0, 12, 24, 28, 32, 36, 44
    NW = 48
    with ExitStack() as ctx:
        st = Stage(nc, ctx, "thr")
        ident = st.sb("ident", [P, P])
        x1 = st.sb("x1", [TP, TILES, D])
        x1s = st.sb("x1s", [TP, TILES, D])
        wt = st.sb("wt", [P, NW, P])

        scale = st.sb("scale", [P, 4])
        x_hi = st.sb("x_hi", [P, TOK, B], F16)
        x_lo = st.sb("x_lo", [P, TOK, B], F16)
        wi_hi = st.sb("wi_hi", [P, 12, P], F16)
        wi_lo = st.sb("wi_lo", [P, 12, P], F16)
        wh_hi = st.sb("wh_hi", [P, 12, P], F16)
        wh_lo = st.sb("wh_lo", [P, 12, P], F16)
        brow = st.sb("brow", [P, 12, P], BF16)
        ones = st.sb("ones", [P, B], BF16)
        ncols = st.sb("ncols", [P, 4 + 4])
        aot = st.sb("aot", [P, K, COLS])
        xn_in = st.sb("xn_in", [P, TOK, K, B])
        hist = st.sb("hist", [P, K, TOK + 1, B])
        bn_rows = st.sb("bn_rows", [TP, 2, D])
        ps = st.ps("ps")
        names = ("const", "pool", "w", "v", "xn", "xt_tp", "xt", "wtp", "wt_sb", "amax", "allmax", "whi", "wlo", "rows", "bparts", "brow", "col_tp", "cols",
                 "pj", "pj_sb", "zero", "sc", "sub", "e", "p", "pt", "pt_sb", "ao", "ao_sb", "gru_in", "lv", "table", "thn_a", "gbt", "beat",
                 "rden", "shift", "shift_mm", "x1s", "wt_act", "th", "tht", "tht_sb", "mix", "mix_sb", "thn", "xh")
        S = {n: st.sem(n) for n in names}
        s_r, s_z, s_n = st.sem("r_mm"), st.sem("z_mm"), st.sem("n_mm")
        s_tr, s_tz, s_tn, s_np, s_hi, s_lo = (st.sem(n) for n in ("r_tanh", "z_tanh", "n_tanh", "n_pre", "state_hi", "state_lo"))

        with ExitStack() as inner:
            sa = Stage(nc, inner, "thr")
            win = sa.sb("win", [TP, K, TP])
            qt = sa.sb("qt", [P, K, COLS])
            kt = sa.sb("kt", [P, K, COLS])
            vr = sa.sb("vr", [TP, TILES, K, P])
            with ExitStack() as first:
                sp_ = Stage(nc, first, "thr")
                xt = sp_.sb("xt", [P, COLS])
                pos = sp_.sb("pos", [TP, D])
                amax = sp_.sb("amax", [P, 2])
                sbits = sp_.sb("sbits", [P, 2], U32)
                rows = sp_.sb("rows", [12, 2, P])
                nrows = sp_.sb("nrows", [2 * K, P])
                facts = sp_.sb("facts", [12, 2])
                brem = sp_.sb("brem", [12, 2, P])
                bparts = sp_.sb("bparts", [12, 3, P], BF16)
                bcols = sp_.sb("bcols", [P, 12])
                shift = sp_.sb("shift", [P, K, TP])
                ln = Norm(sp_, "ln", TP, TILES)
                jobs = [("q", k, n) for k in range(K) for n in range(3)] + [("k", k, n) for k in range(K) for n in range(3)] \
                    + [("n", k, n) for k in range(K) for n in range(3)] + [("v", 0, t) for t in range(TILES)]
                with nc.Block() as block:
                    @block.sync
                    def _(sp):
                        sp.dma_start(wt[:, WHH:WHH + 12, :], a["L1_attn_gru_whh"].rearrange("k (g i) j -> i (k g) j", g=3)).then_inc(S["w"], 16)
                        sp.dma_start(ident[:], const(a["consts"], "ident")).then_inc(S["const"], 16)
                        for nm, at in (("L1_attn_wq", WQ), ("L1_attn_wk", WK), ("L1_attn_wv", WV)):
                            sp.dma_start(wt[:, at:at + K, :], a[nm].rearrange("k i j -> i k j")).then_inc(S["w"], 16)
                        for k in range(K):
                            sp.dma_start(wt[:, WB + 2 * k:WB + 2 * k + 2, :].rearrange("p a j -> p (a j)"), a["L1_attn_w_beat"][k]).then_inc(S["w"], 16)
                        sp.dma_start(wt[:, WM:WM + K, :].rearrange("p a j -> p (a j)"), a["L1_attn_w_mix"]).then_inc(S["w"], 16)
                        sp.dma_start(pos[:], const(a["consts"], "pos_code", TP)).then_inc(S["const"], 16)
                        sp.dma_start(win[:], const(a["consts"], "window", TP).rearrange("p (k s) -> p k s", k=K)).then_inc(S["const"], 16)
                        sp.dma_start(facts[:], const(a["consts"], "gru_facts", 12)).then_inc(S["const"], 16)
                        sp.dma_start(rows[:, 0, :], a["L1_attn_gru_bih"].rearrange("k (g i) -> (k g) i", g=3)).then_inc(S["rows"], 16)
                        sp.dma_start(rows[:, 1, :], a["L1_attn_gru_bhh"].rearrange("k (g i) -> (k g) i", g=3)).then_inc(S["rows"], 16)
                        sp.dma_start(nrows[0:K, :], a["L1_attn_norm_g"]).then_inc(S["rows"], 16)
                        sp.dma_start(nrows[K:2 * K, :], a["L1_attn_norm_b"]).then_inc(S["rows"], 16)
                        sp.dma_start(bn_rows[:, 0, :], a["L1_attn_bn_g"].partition_broadcast(TP)).then_inc(S["rows"], 16)
                        sp.dma_start(bn_rows[:, 1, :], a["L1_attn_bn_b"].partition_broadcast(TP)).then_inc(S["rows"], 16)
                        sp.wait_ge(S["bparts"], 5)
                        sp.wait_ge(S["pool"], 2)
                        for k in range(3):
                            sp.dma_start(brow[k:k + 1, :, :], bparts[:, k, :]).then_inc(S["brow"], 16)
                        sp.wait_ge(S["brow"], 48)

                    @block.scalar
                    def _(act):
                        act.dma_start(wt[:, WIH:WIH + 12, :], a["L1_attn_gru_wih"].rearrange("k (g i) j -> i (k g) j", g=3)).then_inc(S["w"], 16)
                        ln.scalar(nc, act)
                        for n in range(1, NW // 4, 2):
                            act.wait_ge(S["wtp"], n + 1)
                            nc.scalar.copy(wt[:, 4 * n:4 * n + 4, :].rearrange("p a j -> p (a j)"), ps[:, n % 4, :]).then_inc(S["wt_act"], 1)
                        for n, (kind, k, m) in enumerate(jobs):
                            act.wait_ge(S["pj"], n + 1)
                            if kind == "v":
                                ins = nc.scalar.copy(vr[:, m, :, :].rearrange("p k d -> p (k d)"), ps[0:TP, n % 8, :])
                            elif kind == "n":
                                t0, tn = 16 * m, min(16, TOK - 16 * m)
                                ins = nc.scalar.activation(xn_in[:, t0:t0 + tn, k, :], ps[:, n % 8, 0:tn * B].rearrange("p (t b) -> p t b", b=B),
                                                           ACT.Identity, bias=bcols[:, 3 * k + 2:3 * k + 3])
                            else:
                                at, wd = SPANS[m]
                                ins = nc.scalar.copy((qt if kind == "q" else kt)[:, k, at:at + wd], ps[:, n % 8, 0:wd])
                            ins.then_inc(S["pj_sb"], 1)

                    @block.gpsimd
                    def _(pool):
                        nc.gpsimd.memset(ones[:], 1.0).then_inc(S["pool"], 1)
                        nc.gpsimd.memset(brow[:], 0.0).then_inc(S["pool"], 1)
                        nc.gpsimd.memset(hist[:, :, 0, :], 0.0).then_inc(S["pool"], 1)
                        pool.wait_ge(S["amax"], 1)
                        nc.gpsimd.partition_all_reduce(amax[:, 1:2], amax[:, 0:1], P, bass.bass_isa.ReduceOp.max).then_inc(S["allmax"], 1)

                    @block.tensor
                    def _(pe):
                        pe.wait_ge(S["const"], 64)
                        pe.wait_ge(S["w"], 16 * 10)
                        for n in range(NW // 4):
                            if n >= 4:
                                pe.wait_ge(S["wt_act"] if n % 2 else S["wt_sb"], (n - 4) // 2 + 1)
                            for k in range(4):
                                last = nc.tensor.transpose(ps[:, n % 4, k * P:(k + 1) * P], wt[:, 4 * n + k, :], ident[:])
                            last.then_inc(S["wtp"], 1)
                        pe.wait_ge(S["rows"], 96)
                        nc.tensor.transpose(ps[:, 7, 0:12], rows[:, 0, :], ident[0:12, 0:12])
                        nc.tensor.transpose(ps[:, 7, 16:16 + 2 * K], nrows[:], ident[0:2 * K, 0:2 * K]).then_inc(S["col_tp"], 1)
                        transpose_rows(nc, pe, x1, ident, ps, 4, S["xn"], S["xt_tp"])
                        pe.wait_ge(S["cols"], 2)
                        pe.wait_ge(S["xt"], 3)
                        pe.wait_ge(S["wt_sb"], NW // 8)
                        pe.wait_ge(S["wt_act"], NW // 8)
                        pe.wait_ge(S["shift"], 1)
                        for k in range(K):
                            last = nc.tensor.matmul(ps[0:TP, 7, 0:P], shift[:, k, :], wt[:, WM + k, :], start=(k == 0), stop=(k == K - 1))
                        last.then_inc(S["shift_mm"], 1)
                        xtb = xt[:, 0:NTOK].rearrange("p (b t) -> p t b", t=TOK)
                        for n, (kind, k, m) in enumerate(jobs):
                            if n >= 8:
                                pe.wait_ge(S["pj_sb"], n - 7)
                            if n == 7:
                                pe.wait_ge(S["x1s"], 1)
                            if kind == "v":
                                mm = nc.tensor.matmul(ps[0:TP, n % 8, :], xt[:, m * TP:(m + 1) * TP], wt[:, WV:WV + K, :].rearrange("p k d -> p (k d)"), start=True, stop=True)
                            elif kind == "n":
                                t0, tn = 16 * m, min(16, TOK - 16 * m)
                                mm = nc.tensor.matmul(ps[:, n % 8, 0:tn * B], wt[:, WIH + 3 * k + 2, :], xtb[:, t0:t0 + tn, :], start=True, stop=True)
                            else:
                                at, wd = SPANS[m]
                                mm = nc.tensor.matmul(ps[:, n % 8, 0:wd], wt[:, (WQ if kind == "q" else WK) + k, :], xt[:, at:at + wd], start=True, stop=True)
                            mm.then_inc(S["pj"], 1)
                    @block.vector
                    def _(v):
                        c = Counts(v)
                        ln.vector(nc, v, c, S["v"], resid, x1)
                        v.wait_ge(S["const"], 64)
                        nc.vector.tensor_tensor(x1[:], x1[:], pos[:].unsqueeze(1).to_broadcast([TP, TILES, D]), ALU.add).then_inc(S["xn"], TILES)
                        v.wait_ge(S["w"], 16 * 10)
                        for n in range(0, NW // 4, 2):
                            v.wait_ge(S["wtp"], n + 1)
                            nc.vector.tensor_copy(wt[:, 4 * n:4 * n + 4, :].rearrange("p a j -> p (a j)"), ps[:, n % 4, :]).then_inc(S["wt_sb"], 1)
                        v.wait_ge(S["col_tp"], 1)
                        nc.vector.tensor_copy(bcols[:], ps[:, 7, 0:12]).then_inc(S["cols"], 1)
                        nc.vector.tensor_copy(ncols[:], ps[:, 7, 16:16 + 2 * K]).then_inc(S["cols"], 1)
                        v.wait_ge(S["cols"], 2)
                        nc.vector.tensor_copy(shift[:], ncols[:, K:2 * K].unsqueeze(2).to_broadcast([P, K, TP])).then_inc(S["shift"], 1)
                        for n, (at, wd) in enumerate(SPANS):
                            v.wait_ge(S["xt_tp"], n + 1)
                            nc.vector.tensor_copy(xt[:, at:at + wd], ps[:, 4 + n, 0:wd]).then_inc(S["xt"], 1)
                        v.wait_ge(S["shift_mm"], 1)
                        v.wait_ge(S["xn"], TILES)
                        nc.vector.tensor_tensor(x1s[:], x1[:], ps[0:TP, 7, 0:P].unsqueeze(1).to_broadcast([TP, TILES, D]), ALU.add).then_inc(S["x1s"], 1)
                        v.wait_ge(S["wt_sb"], NW // 8)
                        v.wait_ge(S["wt_act"], NW // 8)
                        c.chain(S["v"], nc.vector.tensor_reduce(amax[:, 0:1], wt[:, 0:24, :].rearrange("p a j -> p (a j)"), AX_X, ALU.max, apply_absolute_value=True))
                        c.chain(S["amax"], nc.vector.tensor_copy(scale[:, 3:4], amax[:, 0:1]))
                        v.wait_ge(S["xt"], 3)
                        xtb = xt[:, 0:NTOK].rearrange("p (b t) -> p t b", t=TOK)
                        c.chain(S["v"], nc.vector.tensor_copy(x_hi[:], xtb))
                        c.chain(S["v"], nc.vector.tensor_tensor(x_lo[:], xtb, x_hi[:], ALU.subtract))
                        v.wait_ge(S["allmax"], 1)
                        power_of_two(nc, c, S["v"], amax[:, 1:2], sbits, scale[:, 0:1], scale[:, 3:4])
                        c.chain(S["v"], nc.vector.tensor_scalar(scale[:, 1:2], scale[:, 0:1], 0.5, None, ALU.mult))
                        c.chain(S["v"], nc.vector.tensor_scalar(scale[:, 2:3], scale[:, 0:1], 0.25, None, ALU.mult))
                        v.wait_ge(S["rows"], 96)
                        c.chain(S["v"], nc.vector.scalar_tensor_tensor(out=brem[:, 0, :], in0=rows[:, 0, :], scalar=facts[:, 0:1], in1=rows[:, 1, :],
                                                                       op0=ALU.mult, op1=ALU.add))
                        c.chain(S["v"], nc.vector.tensor_scalar(brem[:, 0, :], brem[:, 0, :], scale[0:12, 1:2], None, ALU.mult))
                        c.chain(S["bparts"], nc.vector.tensor_copy(bparts[:, 0, :], brem[:, 0, :]))
                        c.chain(S["bparts"], nc.vector.tensor_tensor(brem[:, 1, :], brem[:, 0, :], bparts[:, 0, :], ALU.subtract))
                        c.chain(S["bparts"], nc.vector.tensor_copy(bparts[:, 1, :], brem[:, 1, :]))
                        c.chain(S["bparts"], nc.vector.tensor_tensor(brem[:, 0, :], brem[:, 1, :], bparts[:, 1, :], ALU.subtract))
                        c.chain(S["bparts"], nc.vector.tensor_copy(bparts[:, 2, :], brem[:, 0, :]))
                        for hi, lo, at, col in ((wi_hi, wi_lo, WIH, 1), (wh_hi, wh_lo, WHH, 2)):
                            src, sc_ = wt[:, at:at + 12, :].rearrange("p a j -> p (a j)"), scale[:, col:col + 1]
                            c.chain(S["whi"], nc.vector.tensor_scalar(hi[:].rearrange("p a j -> p (a j)"), src, sc_, None, ALU.mult))
                            c.chain(S["v"], nc.vector.scalar_tensor_tensor(out=lo[:].rearrange("p a j -> p (a j)"), in0=src, scalar=sc_,
                                                                           in1=hi[:].rearrange("p a j -> p (a j)"), op0=ALU.mult, op1=ALU.subtract))
                        for k in range(K):
                            nc.vector.tensor_scalar(wt[:, WB + 2 * k, :], wt[:, WB + 2 * k, :], 0.5, None, ALU.mult)
                            ins = nc.vector.tensor_scalar(wt[:, WM + k, :], wt[:, WM + k, :], ncols[:, k:k + 1], None, ALU.mult)
                        c.chain(S["v"], ins)

            sc = sa.sb("sc", [TP, 2, K, TP])
            mx = sa.sb("mx", [TP, 2, K])
            den = sa.sb("den", [TP, 2, K])
            rden = sa.sb("rden", [TP, 2, K])
            pr = sa.sb("pr", [TP, 2, K, TP])
            pn = sa.sb("pn", [TP, 2, K, TP])
            pt = sa.sb("pt", [TP, 2, K, TP])
            with nc.Block() as block:
                @block.tensor
                def _(pe):
                    for t in range(TILES + 3):
                        if t < TILES:
                            if t >= 2:
                                pe.wait_ge(S["sc"], t - 1)
                            for k in range(K):
                                cols = slice(t * TP, (t + 1) * TP)
                                last = nc.tensor.matmul(ps[0:TP, t % 2, k * TP:(k + 1) * TP], qt[:, k, cols], kt[:, k, cols], start=True, stop=True)
                            last.then_inc(S["th"], 1)
                        if 2 <= t < TILES + 2:
                            u = t - 2
                            pe.wait_ge(S["p"], u + 1)
                            if u >= 2:
                                pe.wait_ge(S["pt_sb"], u - 1)
                            for k in range(K):
                                last = nc.tensor.transpose(ps[0:TP, 2 + u % 2, k * TP:(k + 1) * TP], pn[:, u % 2, k, :], ident[0:TP, 0:TP])
                            last.then_inc(S["pt"], 1)
                        if t >= 3:
                            u = t - 3
                            pe.wait_ge(S["pt_sb"], u + 1)
                            if u >= 2:
                                pe.wait_ge(S["ao_sb"], u - 1)
                            for k in range(K):
                                last = nc.tensor.matmul(ps[:, 4 + u % 2, k * TP:(k + 1) * TP], vr[:, u, k, :], pt[:, u % 2, k, :], start=True, stop=True)
                            last.then_inc(S["ao"], 1)

                @block.scalar
                def _(act):
                    for t in range(TILES + 3):
                        if t < TILES:
                            act.wait_ge(S["sub"], t + 1)
                            if t >= 2:
                                act.wait_ge(S["p"], t - 1)
                            nc.scalar.activation(pr[:, t % 2, :, :], sc[:, t % 2, :, :], ACT.Exp, scale=float(D) ** -0.5).then_inc(S["e"], 1)
                        if 2 <= t < TILES + 2:
                            u = t - 2
                            act.wait_ge(S["pt"], u + 1)
                            if u >= 2:
                                act.wait_ge(S["ao"], u - 1)
                            nc.scalar.copy(pt[:, u % 2, :, :].rearrange("p k s -> p (k s)"), ps[0:TP, 2 + u % 2, 0:K * TP]).then_inc(S["pt_sb"], 1)
                        if t >= 3:
                            u = t - 3
                            act.wait_ge(S["ao"], u + 1)
                            nc.scalar.copy(aot[:, :, u * TP:(u + 1) * TP], ps[:, 4 + u % 2, 0:K * TP].rearrange("p (k s) -> p k s", k=K)).then_inc(S["ao_sb"], 1)

                @block.gpsimd
                def _(pool):
                    for t in range(TILES):
                        b = t % 2
                        pool.wait_ge(S["rden"], t + 1)
                        if t >= 2:
                            pool.wait_ge(S["pt"], t - 1)
                        nc.gpsimd.tensor_tensor(pn[:, b, :, :], pr[:, b, :, :], rden[:, b, :].unsqueeze(2).to_broadcast([TP, K, TP]), ALU.mult).then_inc(S["p"], 1)

                @block.vector
                def _(v):
                    c = Counts(v)
                    for t in range(TILES + 1):
                        if t < TILES:
                            b = t % 2
                            v.wait_ge(S["th"], t + 1)
                            if t >= 2:
                                v.wait_ge(S["e"], t - 1)
                            c.chain(S["sc"], nc.vector.tensor_tensor(sc[:, b, :, :], ps[0:TP, b, 0:K * TP].rearrange("p (k s) -> p k s", k=K), win[:], ALU.add))
                            c.chain(S["lv"], nc.vector.tensor_reduce(mx[:, b, :], sc[:, b, :, :], AX_X, ALU.max))
                            nc.vector.tensor_tensor(sc[:, b, :, :], sc[:, b, :, :], mx[:, b, :].unsqueeze(2).to_broadcast([TP, K, TP]), ALU.subtract).then_inc(S["sub"], 1)
                        if t >= 1:
                            u = t - 1
                            b = u % 2
                            v.wait_ge(S["e"], u + 1)
                            c.chain(S["lv"], nc.vector.tensor_reduce(den[:, b, :], pr[:, b, :, :], AX_X, ALU.add))
                            if u >= 2:
                                v.wait_ge(S["p"], u - 1)
                            nc.vector.reciprocal(rden[:, b, :], den[:, b, :]).then_inc(S["rden"], 1)

        TURNS = TOK // 2
        KB = K * B
        with ExitStack() as inner:
            sg = Stage(nc, inner, "gru")
            tr = sg.sb("tr", [P, KB])
            tz = sg.sb("tz", [P, K, B])
            rn = sg.sb("rn", [P, KB])
            npre = sg.sb("npre", [P, KB])
            tn = sg.sb("tn", [P, K, B])
            omz = sg.sb("omz", [P, K, B])
            zh = sg.sb("zh", [P, K, B])
            pz = sg.sb("pz", [P, K, B])
            h_hi = sg.sb("h_hi", [P, K, B], F16)
            h_lo = sg.sb("h_lo", [P, K, B], F16)
            gv = sg.sem("gv")
            with nc.Block() as block:
                @block.tensor
                def _(pe):
                    def inputs(s, t):
                        for gate in range(3):
                            for k in range(K):
                                dst = ps[:, 3 * s + gate, k * B:(k + 1) * B]
                                w = 3 * k + gate
                                nc.tensor.matmul(dst, brow[:, w, :], ones[:], start=(k == 0), stop=False, skip_group_check=True)
                                if gate < 2:
                                    for wgt, x in ((wi_hi, x_hi), (wi_lo, x_hi), (wi_hi, x_lo)):
                                        nc.tensor.matmul(dst, wgt[:, w, :], x[:, t, :], start=False, stop=False, skip_group_check=True)

                    def states(s, n):
                        pe.wait_ge(s_hi, n)
                        for gate in (0, 2, 1):
                            for k in range(K):
                                dst = ps[:, 3 * s + gate, k * B:(k + 1) * B]
                                for wgt in (wh_hi, wh_lo):
                                    nc.tensor.matmul(dst, wgt[:, 3 * k + gate, :], h_hi[:, k, :], start=False, stop=False, skip_group_check=True)
                        pe.wait_ge(s_lo, n)
                        for gate, done in ((0, s_r), (2, s_n), (1, s_z)):
                            for k in range(K):
                                dst = ps[:, 3 * s + gate, k * B:(k + 1) * B]
                                last = nc.tensor.matmul(dst, wh_hi[:, 3 * k + gate, :], h_lo[:, k, :], start=False, stop=True, skip_group_check=True)
                            last.then_inc(done, 1)

                    inputs(0, 0)
                    with pe.Fori(0, TURNS) as i:
                        for s in range(2):
                            states(s, i * 2 + (s + 1))
                            inputs(1 - s, i * 2 + (s + 1))
                    states(0, TOK)

                @block.scalar
                def _(act):
                    nc.scalar.activation(tr[:, 0:1], scale[:, 0:1], ACT.Tanh).then_inc(S["table"], 1)
                    act.wait_ge(S["table"], 1)

                    def step(s, n):
                        act.wait_ge(s_r, n)
                        nc.scalar.activation(tr[:], ps[:, 3 * s, 0:KB], ACT.Tanh, scale=scale[:, 3:4]).then_inc(s_tr, 1)
                        act.wait_ge(s_z, n)
                        nc.scalar.activation(tz[:].rearrange("p k b -> p (k b)"), ps[:, 3 * s + 1, 0:KB], ACT.Tanh, scale=scale[:, 3:4]).then_inc(s_tz, 1)
                        act.wait_ge(s_np, n)
                        nc.scalar.activation(tn[:].rearrange("p k b -> p (k b)"), npre[:], ACT.Tanh).then_inc(s_tn, 1)

                    with act.Fori(0, TURNS) as i:
                        for s in range(2):
                            step(s, i * 2 + (s + 1))
                    step(0, TOK)

                @block.vector
                def _(v):
                    nc.vector.memset(h_hi[:], 0.0).then_inc(s_hi, 1)
                    nc.vector.memset(h_lo[:], 0.0).then_inc(s_lo, 1)
                    GV = 6

                    def step(s, t, n, base):
                        before, after = hist[:, :, slot(t, 0), :], hist[:, :, slot(t, 1), :]
                        v.wait_ge(s_tr, n)
                        v.wait_ge(s_n, n)
                        nc.vector.scalar_tensor_tensor(out=rn[:], in0=tr[:], scalar=1.0, in1=ps[:, 3 * s + 2, 0:KB], op0=ALU.add, op1=ALU.mult).then_inc(gv, 1)
                        v.wait_ge(gv, base + 1)
                        nc.vector.scalar_tensor_tensor(out=npre[:], in0=rn[:], scalar=scale[:, 3:4], in1=xn_at(t), op0=ALU.mult, op1=ALU.add).then_inc(s_np, 1)
                        v.wait_ge(s_tz, n)
                        nc.vector.tensor_scalar(omz[:], tz[:], -1.0, 1.0, ALU.mult, ALU.add).then_inc(gv, 1)
                        nc.vector.scalar_tensor_tensor(out=zh[:], in0=tz[:], scalar=1.0, in1=before, op0=ALU.add, op1=ALU.mult).then_inc(gv, 1)
                        v.wait_ge(s_tn, n)
                        v.wait_ge(gv, base + 3)
                        nc.vector.tensor_tensor(pz[:], omz[:], tn[:], ALU.mult).then_inc(gv, 1)
                        v.wait_ge(gv, base + 4)
                        nc.vector.scalar_tensor_tensor(out=h_hi[:], in0=zh[:], scalar=0.5, in1=pz[:], op0=ALU.mult, op1=ALU.add).then_inc(s_hi, 1)
                        nc.vector.scalar_tensor_tensor(out=after, in0=zh[:], scalar=0.5, in1=pz[:], op0=ALU.mult, op1=ALU.add).then_inc(gv, 1)
                        v.wait_ge(gv, base + 5)
                        v.wait_ge(s_hi, n + 1)
                        nc.vector.tensor_tensor(h_lo[:], after, h_hi[:], ALU.subtract).then_inc(s_lo, 1)

                    def slot(t, d):
                        return t + d

                    def xn_at(t):
                        return xn_in[:, t, :, :].rearrange("p k b -> p (k b)")

                    with v.Fori(0, TURNS) as i:
                        for s in range(2):
                            step(s, i * 2 + s, i * 2 + (s + 1), i * (2 * 5) + 5 * s)
                    step(0, TOK - 1, TOK, 5 * (TOK - 1))

        with ExitStack() as inner:
            sf = Stage(nc, inner, "mix")
            gbt = sf.sb("gbt", [P, K, COLS])
            th = sf.sb("th", [TP, KT, P])
            tht = sf.sb("tht", [P, K, COLS])
            mixed = sf.sb("mixed", [TP, TILES, D])
            lt = Norm(sf, "lt", TP, KT, on_scalar=True)
            lm = Norm(sf, "lm", TP, TILES, on_scalar=True)
            s_mn, s_gain = sf.sem("mixed_norm"), sf.sem("gain")
            fv, s_thr = sf.sem("fv"), sf.sem("thr")
            groups = [range(0, 4), range(4, 8), range(8, TILES)]
            threads = [range(K * g.start, K * g.stop) for g in groups]

            def by_scalar(t):
                return t % 4 < 2

            def half(g, scalar):
                mine = [t for t in groups[g] if by_scalar(t) == scalar]
                return range(K * mine[0], K * (mine[-1] + 1))

            with nc.Block() as block:
                @block.tensor
                def _(pe):
                    def beat(g):
                        for t in groups[g]:
                            if t >= 4:
                                pe.wait_ge(s_thr, t - 3)
                            cols = slice(t * TP, (t + 1) * TP)
                            for k in range(K):
                                dst = ps[0:TP, t % 4, k * P:(k + 1) * P]
                                nc.tensor.matmul(dst, gbt[:, k, cols], wt[:, WB + 2 * k, :], start=True, stop=False)
                                last = nc.tensor.matmul(dst, aot[:, k, cols], wt[:, WB + 2 * k + 1, :], start=False, stop=True)
                            last.then_inc(S["beat"], 1)

                    def turned(g):
                        for t in groups[g]:
                            same = sum(by_scalar(u) == by_scalar(t) for u in range(t + 1))
                            pe.wait_ge(S["thn_a"] if by_scalar(t) else S["thn"], K * same)
                            if t >= 2:
                                pe.wait_ge(S["tht_sb"], t - 1)
                            for k in range(K):
                                last = nc.tensor.transpose(ps[:, 4 + t % 2, k * TP:(k + 1) * TP], th[:, K * t + k, :], ident[0:TP, 0:TP])
                            last.then_inc(S["tht"], 1)

                    def mix(g):
                        for t in groups[g]:
                            pe.wait_ge(S["tht_sb"], t + 1)
                            if t >= 2:
                                pe.wait_ge(S["mix_sb"], t - 1)
                            for k in range(K):
                                last = nc.tensor.matmul(ps[0:TP, 6 + t % 2, 0:P], tht[:, k, t * TP:(t + 1) * TP], wt[:, WM + k, :], start=(k == 0), stop=(k == K - 1))
                            last.then_inc(S["mix"], 1)

                    pe.wait_ge(S["gbt"], K + 1)
                    beat(0)
                    beat(1)
                    beat(2)
                    turned(0)
                    turned(1)
                    mix(0)
                    turned(2)
                    mix(1)
                    mix(2)

                @block.scalar
                def _(act):
                    def evacuate(g):
                        for t in groups[g]:
                            act.wait_ge(S["tht"], t + 1)
                            nc.scalar.copy(tht[:, :, t * TP:(t + 1) * TP], ps[:, 4 + t % 2, 0:K * TP].rearrange("p (k s) -> p k s", k=K)).then_inc(S["tht_sb"], 1)

                    for k in range(K // 2, K):
                        nc.scalar.copy(gbt[:, k, 0:NTOK].rearrange("p (b t) -> p b t", t=TOK),
                                       hist[:, k, 1:TOK + 1, :].rearrange("p t b -> p b t")).then_inc(S["gbt"], 1)
                    def normalise(g):
                        norm_rows_scalar(lt, nc, act, th, th, half(g, True), g + 1, S["thn_a"])

                    norm_root(lt, nc, act, threads[0], 1)
                    normalise(0)
                    norm_root(lt, nc, act, threads[1], 2)
                    evacuate(0)
                    normalise(1)
                    norm_root(lt, nc, act, threads[2], 3)
                    evacuate(1)
                    normalise(2)
                    norm_root(lm, nc, act, groups[0], 1)
                    norm_rows_scalar(lm, nc, act, mixed, mixed, groups[0], 1, s_mn)
                    evacuate(2)
                    norm_root(lm, nc, act, groups[1], 2)
                    norm_rows_scalar(lm, nc, act, mixed, mixed, groups[1], 2, s_mn)
                    norm_root(lm, nc, act, groups[2], 3)

                @block.gpsimd
                def _(pool):
                    c = Counts(pool)
                    for g in range(2):
                        at, n = slice(groups[g].start, groups[g].stop), len(groups[g])
                        pool.wait_ge(s_mn, groups[g].stop)
                        c.chain(s_gain, nc.gpsimd.tensor_tensor(mixed[:, at, :], mixed[:, at, :], bn_rows[:, 0, :].unsqueeze(1).to_broadcast([TP, n, D]), ALU.mult))
                        c.chain(s_gain, nc.gpsimd.tensor_tensor(mixed[:, at, :], mixed[:, at, :], bn_rows[:, 1, :].unsqueeze(1).to_broadcast([TP, n, D]), ALU.add))
                        c.chain(s_gain, nc.gpsimd.tensor_tensor(resid[:, at, :], resid[:, at, :], mixed[:, at, :], ALU.add))

                @block.vector
                def _(v):
                    c = Counts(v)

                    def add_and_measure(g):
                        for t in groups[g]:
                            v.wait_ge(S["beat"], t + 1)
                            ins = nc.vector.tensor_tensor(th[:, K * t:K * (t + 1), :], ps[0:TP, t % 4, :].rearrange("p (k d) -> p k d", k=K),
                                                          x1[:, t, :].unsqueeze(1).to_broadcast([TP, K, P]), ALU.add)
                            ins.then_inc(s_thr, 1)
                        v.wait_ge(s_thr, groups[g].stop)
                        norm_measure(lt, nc, c, fv, th, threads[g])

                    def normalise(g):
                        norm_factors(lt, nc, v, c, fv, threads[g], g + 1)
                        norm_rows(lt, nc, th, th, half(g, False), S["thn"])

                    def mixed_and_measure(g):
                        for t in groups[g]:
                            v.wait_ge(S["mix"], t + 1)
                            nc.vector.tensor_tensor(mixed[:, t, :], ps[0:TP, 6 + t % 2, 0:P], x1s[:, t, :], ALU.add).then_inc(S["mix_sb"], 1)
                        v.wait_ge(S["mix_sb"], groups[g].stop)
                        norm_measure(lm, nc, c, fv, mixed, groups[g])

                    def finish(g):
                        at, n = slice(groups[g].start, groups[g].stop), len(groups[g])
                        norm_apply(lm, nc, v, c, fv, mixed, mixed, groups[g], g + 1)
                        c.chain(fv, nc.vector.tensor_tensor(mixed[:, at, :], mixed[:, at, :], bn_rows[:, 0, :].unsqueeze(1).to_broadcast([TP, n, D]), ALU.mult))
                        c.chain(fv, nc.vector.tensor_tensor(mixed[:, at, :], mixed[:, at, :], bn_rows[:, 1, :].unsqueeze(1).to_broadcast([TP, n, D]), ALU.add))
                        c.chain(fv, nc.vector.tensor_tensor(resid[:, at, :], resid[:, at, :], mixed[:, at, :], ALU.add))

                    nc.vector.memset(gbt[:, :, NTOK:COLS], 0.0).then_inc(S["gbt"], 1)
                    for k in range(K // 2):
                        nc.vector.tensor_copy(gbt[:, k, 0:NTOK].rearrange("p (b t) -> p b t", t=TOK),
                                              hist[:, k, 1:TOK + 1, :].rearrange("p t b -> p b t")).then_inc(S["gbt"], 1)
                    add_and_measure(0)
                    normalise(0)
                    add_and_measure(1)
                    normalise(1)
                    add_and_measure(2)
                    normalise(2)
                    mixed_and_measure(0)
                    norm_factors(lm, nc, v, c, fv, groups[0], 1)
                    mixed_and_measure(1)
                    norm_factors(lm, nc, v, c, fv, groups[1], 2)
                    mixed_and_measure(2)
                    finish(2)


def expert_stage(nc, a, resid, dram):
    E, NE = EXPERTS, EXPERTS + 1
    with ExitStack() as ctx:
        st = Stage(nc, ctx, "ffn")
        ident = st.sb("ident", [P, P])
        iota = st.sb("iota", [P, 8])
        w1 = st.sb("w1", [P, NE, P])
        w2 = st.sb("w2", [P, NE, P])
        gw = st.sb("gw", [E, P])
        gwt = st.sb("gwt", [P, E])
        b1 = st.sb("b1", [NE, P])
        b1c = st.sb("b1c", [P, NE])
        b2 = st.sb("b2", [E, P])
        sb2 = st.sb("sb2", [TP, P])
        xn = st.sb("xn", [TP, TILES, D])
        xt = st.sb("xt", [P, COLS])
        lg = st.sb("lg", [TP, TILES, E])
        red = st.sb("red", [TP, TILES, 4])
        top = st.sb("top", [TP, TILES, 8])
        topi = st.sb("topi", [TP, TILES, 8], U32)
        topf = st.sb("topf", [TP, TILES, 2])
        hot = st.sb("hot", [TP, TILES, 2, E])
        comb = st.sb("comb", [TP, TILES, E])
        ct = st.sb("ct", [E, COLS])
        h1 = st.sb("h1", [P, NE, COLS])
        ps = st.ps("ps")
        ln = Norm(st, "ln", TP, TILES)
        names = ("const", "w", "v", "xn", "xt_tp", "xt", "wtp", "wts", "lg", "sub", "e", "comb", "ct_tp", "ct", "h1", "h1_sb", "y", "acc", "sb2", "out")
        S = {n: st.sem(n) for n in names}
        EARLY = 4
        firsts = [(e, n) for e in [E, *range(E)] for n in range(3)]
        BEFORE = 3 * (EARLY + 1)
        passes = [(half, t) for half in range(2) for t in range(TILES)]
        def base_bank(t):
            return (2, 7)[t // 2 % 2]

        sums, done = [], {}
        for half in range(2):
            for t0 in range(0, TILES, 2):
                pair = range(t0, min(t0 + 2, TILES))
                if half == 0:
                    sums.append((half, t0, None))
                for e in range(EARLY):
                    for t in pair:
                        sums.append((half, t, e))
                for t in pair:
                    done[half, t] = len(sums)

        block = ctx.enter_context(nc.Block())

        @block.sync
        def _(sp):
            sp.dma_start(ident[:], const(a["consts"], "ident")).then_inc(S["const"], 16)
            sp.dma_start(iota[:], const(a["consts"], "iota8")).then_inc(S["const"], 16)
            sp.dma_start(gw[:], a["L1_ffn_gate_w"]).then_inc(S["const"], 16)
            sp.dma_start(b1[0:E, :], a["L1_ffn_b1"]).then_inc(S["const"], 16)
            sp.dma_start(b1[E:NE, :], a["L1_ffn_sb1"].partition_broadcast(1)).then_inc(S["const"], 16)
            sp.dma_start(b2[:], a["L1_ffn_b2"]).then_inc(S["const"], 16)
            sp.dma_start(sb2[:], a["L1_ffn_sb2"].partition_broadcast(TP)).then_inc(S["const"], 16)
            full, last = rows_view(dram)
            for t0, t1 in ((0, 4), (4, 8), (8, TILES - 1)):
                sp.wait_ge(S["acc"], done[1, t1 - 1])
                sp.dma_start(full[:, t0:t1, :], resid[:, t0:t1, :]).then_inc(S["out"], 16)
            sp.wait_ge(S["acc"], done[1, TILES - 1])
            sp.dma_start(last, resid[0:LAST, TILES - 1, :]).then_inc(S["out"], 16)
            sp.wait_ge(S["out"], 64)

        @block.scalar
        def _(act):
            act.dma_start(w1[:, 0:E, :], a["L1_ffn_w1"].rearrange("e h f -> h e f")).then_inc(S["w"], 16)
            act.dma_start(w1[:, E, :], a["L1_ffn_sw1"]).then_inc(S["w"], 16)
            act.dma_start(w2[:, 0:E, :], a["L1_ffn_w2"].rearrange("e f h -> f e h")).then_inc(S["w"], 16)
            act.dma_start(w2[:, E, :], a["L1_ffn_sw2"]).then_inc(S["w"], 16)
            ln.scalar(nc, act)
            act.wait_ge(S["sub"], 1)
            nc.scalar.activation(lg[:], lg[:], ACT.Exp).then_inc(S["e"], 1)
            act.wait_ge(S["wts"], 2)
            for n, (e, m) in enumerate(firsts):
                at, wd = SPANS[m]
                act.wait_ge(S["h1"], n + 1)
                nc.scalar.activation(h1[:, e, at:at + wd], ps[:, n % 2, 0:wd], ACT.Relu, bias=b1c[:, e:e + 1]).then_inc(S["h1_sb"], 1)

        @block.gpsimd
        def _(pool):
            pool.wait_ge(S["xn"], TILES)
            pool.wait_ge(S["const"], 16 * 7)
            nc.gpsimd.tensor_tensor(resid[:], resid[:], sb2[:].unsqueeze(1).to_broadcast([TP, TILES, D]), ALU.add).then_inc(S["sb2"], 1)

        @block.tensor
        def _(pe):
            pe.wait_ge(S["const"], 16 * 7)
            nc.tensor.transpose(ps[:, 7, 0:E], gw[:], ident[0:E, 0:E])
            nc.tensor.transpose(ps[:, 7, 16:16 + NE], b1[:], ident[0:NE, 0:NE]).then_inc(S["wtp"], 1)
            transpose_rows(nc, pe, xn, ident, ps, 0, S["xn"], S["xt_tp"])
            pe.wait_ge(S["xt"], 3)
            pe.wait_ge(S["wts"], 2)
            for t in range(TILES):
                last = nc.tensor.matmul(ps[0:TP, 6, E * t:E * t + E], xt[:, t * TP:(t + 1) * TP], gwt[:], start=True, stop=True)
            last.then_inc(S["lg"], 1)
            pe.wait_ge(S["w"], 64)

            def first(n):
                e, m = firsts[n]
                at, wd = SPANS[m]
                if n >= 2:
                    pe.wait_ge(S["h1_sb"], n - 1)
                nc.tensor.matmul(ps[:, n % 2, 0:wd], w1[:, e, :], xt[:, at:at + wd], start=True, stop=True).then_inc(S["h1"], 1)

            for n in range(BEFORE):
                first(n)
            pe.wait_ge(S["comb"], 1)
            for t in range(TILES):
                last = nc.tensor.transpose(ps[0:E, 3 + t // 4, (t % 4) * TP:(t % 4) * TP + TP], comb[:, t, :], ident[0:TP, 0:TP])
            last.then_inc(S["ct_tp"], 1)
            for n in range(BEFORE, BEFORE + 3):
                first(n)
            pe.wait_ge(S["ct"], 3)
            for i, (half, t) in enumerate(passes):
                cols = slice(t * TP, (t + 1) * TP)
                if half == 0 and BEFORE + 3 + t < 3 * NE:
                    first(BEFORE + 3 + t)
                if i == 0:
                    pe.wait_ge(S["h1_sb"], 3 * (1 + EARLY))
                if i == TILES:
                    pe.wait_ge(S["h1_sb"], 3 * NE)
                if i >= 4:
                    pe.wait_ge(S["acc"], done[passes[i - 4]])
                if half == 0:
                    base = ps[0:TP, base_bank(t), (t % 2) * P:(t % 2) * P + P]
                    nc.tensor.matmul(base, ct[:, cols], b2[:], start=True, stop=False)
                    nc.tensor.matmul(base, h1[:, E, cols], w2[:, E, :], start=False, stop=True)
                for e in range(EARLY):
                    last = nc.tensor.matmul(ps[0:TP, 3 + i % 4, e * P:(e + 1) * P], h1[:, EARLY * half + e, cols], w2[:, EARLY * half + e, :], start=True, stop=True)
                last.then_inc(S["y"], 1)

        @block.vector
        def _(v):
            c = Counts(v)
            v.wait_ge(S["wtp"], 1)
            nc.vector.tensor_copy(gwt[:], ps[:, 7, 0:E]).then_inc(S["wts"], 1)
            nc.vector.tensor_copy(b1c[:], ps[:, 7, 16:16 + NE]).then_inc(S["wts"], 1)
            ln.vector(nc, v, c, S["v"], resid, xn, S["xn"])
            for n, (at, wd) in enumerate(SPANS):
                v.wait_ge(S["xt_tp"], n + 1)
                nc.vector.tensor_copy(xt[:, at:at + wd], ps[:, n, 0:wd]).then_inc(S["xt"], 1)
            v.wait_ge(S["lg"], 1)
            v.wait_ge(S["const"], 16 * 7)
            lgp = ps[0:TP, 6, 0:E * TILES].rearrange("p (t e) -> p t e", e=E)
            c.chain(S["v"], nc.vector.tensor_reduce(red[:, :, 0], lgp, AX_X, ALU.max))
            c.chain(S["sub"], nc.vector.tensor_tensor(lg[:], lgp, red[:, :, 0:1].to_broadcast([TP, TILES, E]), ALU.subtract))
            v.wait_ge(S["e"], 1)
            c.chain(S["v"], nc.vector.tensor_reduce(red[:, :, 1], lg[:], AX_X, ALU.add))
            c.chain(S["v"], nc.vector.reciprocal(red[:, :, 2], red[:, :, 1]))
            c.chain(S["v"], nc.vector.tensor_tensor(lg[:], lg[:], red[:, :, 2:3].to_broadcast([TP, TILES, E]), ALU.mult))
            for t in range(TILES):
                ins = nc.vector.max(top[:, t, :], lg[:, t, :])
            c.chain(S["v"], ins)
            for t in range(TILES):
                ins = nc.vector.max_index(topi[:, t, :], top[:, t, :], lg[:, t, :])
            c.chain(S["v"], ins)
            c.chain(S["v"], nc.vector.tensor_copy(topf[:], topi[:, :, 0:2]))
            c.chain(S["v"], nc.vector.tensor_tensor(red[:, :, 0], top[:, :, 0], top[:, :, 1], ALU.add))
            c.chain(S["v"], nc.vector.tensor_scalar(red[:, :, 0], red[:, :, 0], 1e-20, None, ALU.add))
            c.chain(S["v"], nc.vector.reciprocal(red[:, :, 1], red[:, :, 0]))
            c.chain(S["v"], nc.vector.tensor_tensor(red[:, :, 2:4], top[:, :, 0:2], red[:, :, 1:2].to_broadcast([TP, TILES, 2]), ALU.mult))
            for k in range(2):
                ins = nc.vector.tensor_tensor(hot[:, :, k, :], iota[0:TP, :].unsqueeze(1).to_broadcast([TP, TILES, E]),
                                              topf[:, :, k:k + 1].to_broadcast([TP, TILES, E]), ALU.is_equal)
            c.chain(S["v"], ins)
            for k in range(2):
                ins = nc.vector.tensor_tensor(hot[:, :, k, :], hot[:, :, k, :], red[:, :, 2 + k:3 + k].to_broadcast([TP, TILES, E]), ALU.mult)
            c.chain(S["v"], ins)
            c.chain(S["comb"], nc.vector.tensor_tensor(comb[:], hot[:, :, 0, :], hot[:, :, 1, :], ALU.add))
            v.wait_ge(S["ct_tp"], 1)
            for n, (at, wd) in enumerate(SPANS):
                nc.vector.tensor_copy(ct[:, at:at + wd], ps[0:E, 3 + n, 0:wd]).then_inc(S["ct"], 1)
            v.wait_ge(S["sb2"], 1)
            before, seen = {}, 0
            for n, (half, t, e) in enumerate(sums):
                i = passes.index((half, t))
                pair = range(t, min(t + 2, TILES))
                need = i + len(pair) if e is None else i + 1
                if need > seen:
                    v.wait_ge(S["y"], need)
                    seen = need
                if e is None:
                    nc.vector.tensor_tensor(resid[:, t:t + len(pair), :], ps[0:TP, base_bank(t), 0:len(pair) * P].rearrange("p (t d) -> p t d", d=P),
                                            resid[:, t:t + len(pair), :], ALU.add).then_inc(S["acc"], 1)
                    before.update({u: n + 1 for u in pair})
                else:
                    v.wait_ge(S["acc"], before[t])
                    nc.vector.scalar_tensor_tensor(out=resid[:, t, :], in0=ps[0:TP, 3 + i % 4, e * P:(e + 1) * P], scalar=comb[:, t, EARLY * half + e:EARLY * half + e + 1],
                                                   in1=resid[:, t, :], op0=ALU.mult, op1=ALU.add).then_inc(S["acc"], 1)
                    before[t] = n + 1


def vit_tower_kernel(nc, a, out):
    h0 = nc.dram_tensor("h0_rows", (NTOK, D), F32, kind="Internal").ap()
    tok_stage(nc, a, h0)
    stages = [lambda r: rel_attn_stage(nc, a, h0, r), lambda r: lstm_stage(nc, a, r), lambda r: thread_stage(nc, a, r), lambda r: expert_stage(nc, a, r, out.rearrange("b t d -> (b t) d"))]
    with nc.sbuf_tensor("resid", [TP, TILES, D], F32) as resid:
        for n, f in enumerate(stages):
            f(resid)
            if n == 1 or n == 2:
                clear_semaphores(nc)


def kernel(**inputs):
    import concourse.bacc as _bacc
    from concourse.bass_utils import run_bass_kernel_spmd as _run

    nc = _bacc.Bacc("TRN2", target_bir_lowering=False, num_devices=1)
    arrays, args = {}, {}
    feeds = dict(inputs)
    feeds["consts"] = np.concatenate([np.pad(v, ((0, P - v.shape[0]), (0, 0))) for v in CONSTS.values()], 1)
    for name, value in feeds.items():
        v = np.ascontiguousarray(value)
        arrays[f"in_{name}_dram"] = v
        args[name] = nc.dram_tensor(f"in_{name}_dram", v.shape, mybir.dt.from_np(v.dtype), kind="ExternalInput").ap()
    out = nc.dram_tensor("out_0_dram", (IMGS, TOK, D), F32, kind="ExternalOutput").ap()
    vit_tower_kernel(nc, args, out)
    r = _run(nc, [arrays], core_ids=[0])
    return r.results[0]["out_0_dram"]
```

```python
from contextlib import ExitStack

import numpy as np

import concourse.bass as bass
from concourse import mybir

F32 = mybir.dt.float32
BF16 = mybir.dt.bfloat16
U32 = mybir.dt.uint32
ALU = mybir.AluOpType
ACT = mybir.ActivationFunctionType
AX_X = mybir.AxisListType.X

P = 128
D = 128
IMGS = 32
TOK = 37
GRID = 6
PATCH = 16
NTOK = IMGS * TOK
TP = 3 * TOK
TILES = -(-NTOK // TP)
LAST = NTOK - (TILES - 1) * TP
COLS = TILES * TP
EPS = 1e-5
HEADS, DH = 8, 16
EXPERTS = 8
THREADS = 4
CYCLES = (5, 6, 7, 8)


def shape_constants():
    c = {}
    c["ident"] = np.eye(P, dtype=np.float32)
    sel = np.zeros((5, P, P), np.float32)
    sel[0] = np.eye(P)
    for m in range(16):
        sel[1, 80 + m, 64 + m] = 1
        sel[2, 64 + m, 80 + m] = 1
        sel[3, 112 + m, 96 + m] = 1
        sel[4, 96 + m, 112 + m] = 1
    c["shift_sel"] = sel.transpose(1, 0, 2).reshape(P, 5 * P)
    pos = np.arange(IMGS - 1, -1, -1, dtype=np.float32)
    inv = (1.0 / 10000.0 ** (np.arange(0, D, 2, dtype=np.float32) / D)).astype(np.float32)
    s = pos[:, None] * inv[None, :]
    c["rel_pos_t"] = np.concatenate([np.sin(s), np.cos(s)], -1).astype(np.float32).T
    c["head_mask"] = (np.arange(P)[:, None] // DH == np.arange(HEADS)[None, :]).astype(np.float32)
    c["head_rows"] = (np.arange(P)[:, None] % HEADS == np.arange(P)[None, :] // DH).astype(np.float32)
    t = np.arange(TOK, dtype=np.float32)[:, None]
    div = np.exp(np.arange(0, D, 2, dtype=np.float32) * np.float32(-np.log(10000.0) / D))
    pe = np.zeros((TOK, D), np.float32)
    pe[:, 0::2] = np.sin(t * div)
    pe[:, 1::2] = np.cos(t * div)
    tala = np.zeros((TOK, D), np.float32)
    slots = D // THREADS
    half = slots // 2
    harm = np.arange(1, half + 1, dtype=np.float32)
    for k, cyc in enumerate(CYCLES):
        phase = t % cyc / cyc * 2.0 * np.pi
        tala[:, k * slots:k * slots + half] = np.sin(phase * harm)
        tala[:, k * slots + half:(k + 1) * slots] = np.cos(phase * harm)
    c["pos_code"] = np.concatenate([np.tile(0.5 * pe + 0.5 * tala, (3, 1)), np.zeros((P - TP, D))], 0).astype(np.float32)
    a = np.arange(TP)
    diff = a[:, None] - a[None, :]
    same = a[:, None] // TOK == a[None, :] // TOK
    win = np.full((P, THREADS, TP), -1e30, np.float32)
    for k, cyc in enumerate(CYCLES):
        win[:TP, k] = np.where(same & (diff >= 0) & (diff < cyc), 0.0, -1e30)
    c["window"] = win.reshape(P, THREADS * TP)
    r = np.zeros((P, 18, P), np.float32)
    for j in range(18):
        r[j, j, :] = 1
    c["row_sel"] = r.reshape(P, 18 * P)
    c["ident_rep"] = np.repeat(np.eye(P, dtype=np.float32), HEADS, axis=1)
    c["gate_half"] = np.where(np.arange(P) % 4 == 2, 1.0, 0.5).astype(np.float32)[:, None]
    c["gru_facts"] = np.stack([(np.arange(P) % 3 < 2), np.ones(P)], 1).astype(np.float32)
    c["iota8"] = np.tile(np.arange(8, dtype=np.float32), (P, 1))
    return c


CONSTS = shape_constants()
CONST_AT = {}
_at = 0
for _n, _a in CONSTS.items():
    CONST_AT[_n] = (_at, _a.shape[1])
    _at += _a.shape[1]
CONST_COLS = _at


class Counts:

    def __init__(self, eng):
        self.eng, self.n = eng, {}

    def chain(self, sem, ins):
        ins.then_inc(sem, 1)
        self.n[sem.name] = self.n.get(sem.name, 0) + 1
        self.eng.wait_ge(sem, self.n[sem.name])


SEMAPHORES = []


def clear_semaphores(nc):
    nc.clear_and_free_semaphores(list(SEMAPHORES))
    SEMAPHORES.clear()
    nc.all_engine_barrier()


class Stage:

    def __init__(self, nc, ctx, tag):
        self.nc, self.ctx, self.tag = nc, ctx, tag

    def sb(self, name, shape, dt=F32):
        return self.ctx.enter_context(self.nc.sbuf_tensor(f"{self.tag}_{name}", shape, dt))

    def ps(self, name, banks=8):
        return self.ctx.enter_context(self.nc.psum_tensor(f"{self.tag}_{name}", [P, banks, 512], F32))

    def sem(self, name):
        s = self.nc.alloc_semaphore(f"{self.tag}_{name}")
        SEMAPHORES.append(s)
        return s


def const(c_all, name, rows=P):
    at, n = CONST_AT[name]
    return c_all[0:rows, at:at + n]


def rows_view(dram):
    full = dram[0:(TILES - 1) * TP, :].rearrange("(t p) d -> p t d", p=TP)
    return full, dram[(TILES - 1) * TP:NTOK, :]


def row_stats(c, s_v, nc, src, stats, mv, tiles=range(TILES)):
    if src is not None:
        for t in tiles:
            ins = nc.vector.bn_stats(stats[:, t, :], src[:, t, :])
        c.chain(s_v, ins)
    for t in tiles:
        ins = nc.vector.bn_aggr(mv[:, t, :], stats[:, t, :])
    c.chain(s_v, ins)


def tok_stage(nc, a, h_dram):
    NQ = 6
    HALF = 3 * IMGS
    SIDE = GRID + 1
    CELL = SIDE * SIDE
    CELLS = IMGS * CELL
    GUARD = SIDE + 1
    GT = 14
    HG = GT // 2
    GP = CELLS // GT
    with ExitStack() as ctx:
        st = Stage(nc, ctx, "tok")
        ident = st.sb("ident", [P, P])
        sel = st.sb("sel", [P, 5, P])
        wn = st.sb("wn", [P, 3 * 256])
        wt = st.sb("wt", [P, NQ, P])
        img = st.sb("img", [HALF, 2, 3, PATCH * 96])
        pat = st.sb("pat", [HALF, 2, 3, GRID, PATCH * PATCH])
        xt = st.sb("xt", [P, NQ, 4, 3 * HALF])
        grid = st.sb("grid", [P, GUARD + CELLS + GUARD])
        bias = st.sb("bias", [P, D])
        gain = st.sb("gain", [P, D])
        beta = st.sb("beta", [P, D])
        tok = st.sb("tok", [GP, GT, D])
        outp = st.sb("outp", [GP, GT, D])
        stats = st.sb("stats", [GP, GT, 6])
        mv = st.sb("mv", [GP, GT, 2])
        std = st.sb("std", [GP, GT, 1])
        rstd = st.sb("rstd", [GP, GT, 1])
        cls = st.sb("cls", [IMGS, D])
        ps = st.ps("ps")
        s_const, s_w, s_row, s_cls = st.sem("const"), st.sem("w"), st.sem("row"), st.sem("cls")
        s_img = [st.sem(f"img{u}") for u in range(2)]
        s_zero, s_v, s_a = st.sem("zero"), st.sem("v"), st.sem("a")
        s_wtp, s_wt = st.sem("wtp"), st.sem("wt")
        s_tp, s_xt_v, s_xt_a = st.sem("tp"), st.sem("xt_v"), st.sem("xt_a")
        s_pr, s_grid = st.sem("pr"), st.sem("grid")
        s_sh, s_tok = st.sem("sh"), st.sem("tok")
        s_mv, s_std, s_outp, s_out = st.sem("mv"), st.sem("std"), st.sem("outp"), st.sem("out")
        s_norm, s_gain, s_outp0 = st.sem("norm"), st.sem("gain"), st.sem("outp0")
        s_pad, s_pat = st.sem("pad"), [st.sem(f"pat{u}") for u in range(2)]

        xi = a["x"].rearrange("b c (i p) w -> b c i (p w)", p=PATCH)
        padded = nc.dram_tensor("grid_rows", (CELLS, D), F32, kind="Internal").ap()

        block = ctx.enter_context(nc.Block())

        @block.sync
        def _(sp):
            for u in range(2):
                for k in range(3):
                    sp.dma_start(img[32 * k:32 * k + 32, u, :, :], xi[:, :, 3 * u + k, :]).then_inc(s_img[u], 16)
            sp.wait_ge(s_std, 1)
            sp.wait_ge(s_cls, 16)
            hv = h_dram.rearrange("(b t) d -> b t d", t=TOK)
            sp.dma_start(hv[:, 0, :], cls[:, :]).then_inc(s_out, 16)
            for n in range(2):
                sp.wait_ge(s_outp if n else s_outp0, 1)
                half = slice(n * HG, (n + 1) * HG)
                sp.dma_start(padded.rearrange("(t p) d -> p t d", p=GP)[:, half, :], outp[:, half, :]).then_inc(s_pad, 16)
            sp.wait_ge(s_pad, 32)
            pv = padded.rearrange("(b i j) d -> b i j d", i=SIDE, j=SIDE)
            for i in range(GRID):
                sp.dma_start(hv[:, 1 + GRID * i:1 + GRID * i + GRID, :], pv[:, i, 0:GRID, :]).then_inc(s_out, 16)
            sp.wait_ge(s_out, 16 * (1 + GRID))

        @block.scalar
        def _(act):
            act.dma_start(ident[:], const(a["consts"], "ident")).then_inc(s_const, 16)
            act.wait_ge(s_zero, 1)
            act.dma_start(wn[0:64, :], a["L0_tok_W_main"]).then_inc(s_w, 16)
            wx = a["L0_tok_W_sx"].rearrange("o (r j) -> o r j", j=PATCH)
            wnx = wn[:, :].rearrange("o (r j) -> o r j", j=PATCH)
            act.dma_start(wnx[64:80, :, 8:16], wx[:, :, 0:8]).then_inc(s_w, 16)
            act.dma_start(wnx[80:96, :, 0:8], wx[:, :, 8:16]).then_inc(s_w, 16)
            wy = a["L0_tok_W_sy"].rearrange("o (c h r) -> o c h r", c=3, h=2)
            wny = wn[:, :].rearrange("o (c h r) -> o c h r", c=3, h=2)
            act.dma_start(wny[96:112, :, 1, :], wy[:, :, 0, :]).then_inc(s_w, 16)
            act.dma_start(wny[112:128, :, 0, :], wy[:, :, 1, :]).then_inc(s_w, 16)
            act.dma_start(sel[:], const(a["consts"], "shift_sel").rearrange("p (s m) -> p s m", s=5)).then_inc(s_const, 16)
            at = 0
            for nm, w in (("L0_tok_b_main", 64), ("L0_tok_b_sx", 16), ("L0_tok_b_sx", 16), ("L0_tok_b_sy", 16), ("L0_tok_b_sy", 16)):
                act.dma_start(bias[:, at:at + w], a[nm].partition_broadcast(P)).then_inc(s_row, 16)
                at += w
            act.dma_start(gain[:], a["L0_tok_ln_g"].partition_broadcast(P)).then_inc(s_row, 16)
            act.dma_start(beta[:], a["L0_tok_ln_b"].partition_broadcast(P)).then_inc(s_row, 16)
            act.dma_start(cls[:], a["cls_tok"].rearrange("a b d -> (a b d)").partition_broadcast(IMGS)).then_inc(s_cls, 16)
            for u in range(2):
                act.wait_ge(s_img[u], 48)
                nc.scalar.copy(pat[:, u, 2, :, :].rearrange("p j (r e) -> p j r e", e=PATCH),
                               img[:, u, 2, :].rearrange("p (r j e) -> p j r e", r=PATCH, j=GRID)).then_inc(s_pat[u], 1)
            for n in range(1, 24, 2):
                act.wait_ge(s_tp, n + 1)
                nc.scalar.copy(xt[:, n % NQ, n // NQ, :], ps[:, n % 4, 0:3 * HALF]).then_inc(s_xt_a, 1)
            for n in range(2):
                act.wait_ge(s_mv, n + 1)
                nc.scalar.activation(std[:, n * HG:(n + 1) * HG, 0], mv[:, n * HG:(n + 1) * HG, 1], ACT.Sqrt).then_inc(s_std, 1)

        @block.gpsimd
        def _(pool):
            c = Counts(pool)
            pool.wait_ge(s_row, 16 * 7)
            pool.wait_ge(s_norm, HG)
            c.chain(s_gain, nc.gpsimd.tensor_tensor(outp[:, 0:HG, :], outp[:, 0:HG, :], gain[0:GP, :].unsqueeze(1).to_broadcast([GP, HG, D]), ALU.mult))
            nc.gpsimd.tensor_tensor(outp[:, 0:HG, :], outp[:, 0:HG, :], beta[0:GP, :].unsqueeze(1).to_broadcast([GP, HG, D]), ALU.add).then_inc(s_outp0, 1)

        @block.tensor
        def _(pe):
            pe.wait_ge(s_const, 32)
            pe.wait_ge(s_w, 80)
            for q in range(NQ):
                last = nc.tensor.transpose(ps[:, 4 + q // 4, (q % 4) * P:(q % 4) * P + P], wn[:, q * P:(q + 1) * P], ident[:])
            last.then_inc(s_wtp, 1)
            for n in range(24):
                u, jg, q = n // 12, (n // NQ) % 2, n % NQ
                if n % 12 == 0:
                    pe.wait_ge(s_pat[u], 3)
                if n >= 4:
                    if n % 2:
                        pe.wait_ge(s_xt_a, (n - 4) // 2 + 1)
                    else:
                        pe.wait_ge(s_xt_v, (n - 4) // 2 + 1)
                for k in range(3):
                    src = pat[:, u, q // 2, 3 * jg + k, P * (q % 2):P * (q % 2) + P]
                    last = nc.tensor.transpose(ps[:, n % 4, k * HALF:(k + 1) * HALF], src, ident[0:HALF, 0:HALF])
                last.then_inc(s_tp, 1)
            pe.wait_ge(s_wt, 2)
            for g in range(4):
                for q in range(NQ):
                    n = g * NQ + q
                    if n % 2:
                        pe.wait_ge(s_xt_a, n // 2 + 1)
                    else:
                        pe.wait_ge(s_xt_v, n // 2 + 1)
                    last = nc.tensor.matmul(ps[:, 4 + g, 0:3 * HALF], wt[:, q, :], xt[:, q, g, :], start=(q == 0), stop=(q == NQ - 1))
                last.then_inc(s_pr, 1)
            pe.wait_ge(s_grid, 4)
            for t in range(GT):
                if t >= 4:
                    pe.wait_ge(s_tok, t - 3)
                for k, step in enumerate((0, 1, -1, SIDE, -SIDE)):
                    at = GUARD + t * GP + step
                    last = nc.tensor.matmul(ps[0:GP, t % 4, 0:P], grid[:, at:at + GP], sel[:, k, :], start=(k == 0), stop=(k == 4))
                last.then_inc(s_sh, 1)

        @block.vector
        def _(v):
            c = Counts(v)
            nc.vector.memset(wn[:], 0.0).then_inc(s_zero, 1)
            c.chain(s_v, nc.vector.memset(grid[:], 0.0))
            for u in range(2):
                v.wait_ge(s_img[u], 48)
                for ch in range(2):
                    nc.vector.tensor_copy(pat[:, u, ch, :, :].rearrange("p j (r e) -> p j r e", e=PATCH),
                                          img[:, u, ch, :].rearrange("p (r j e) -> p j r e", r=PATCH, j=GRID)).then_inc(s_pat[u], 1)
            v.wait_ge(s_wtp, 1)
            nc.vector.tensor_copy(wt[:, 0:4, :].rearrange("p q m -> p (q m)"), ps[:, 4, 0:512]).then_inc(s_wt, 1)
            nc.vector.tensor_copy(wt[:, 4:6, :].rearrange("p q m -> p (q m)"), ps[:, 5, 0:256]).then_inc(s_wt, 1)
            for n in range(0, 24, 2):
                v.wait_ge(s_tp, n + 1)
                nc.vector.tensor_copy(xt[:, n % NQ, n // NQ, :], ps[:, n % 4, 0:3 * HALF]).then_inc(s_xt_v, 1)
            for g in range(4):
                u, jg = g // 2, g % 2
                v.wait_ge(s_pr, g + 1)
                for k in range(3):
                    cells = grid[:, GUARD:GUARD + CELLS].rearrange("p (b i j) -> p b i j", i=SIDE, j=SIDE)
                    dst = cells[:, :, 3 * u:3 * u + 3, 3 * jg + k].rearrange("p b i -> p i b")
                    ins = nc.vector.tensor_copy(dst, ps[:, 4 + g, k * HALF:(k + 1) * HALF].rearrange("p (i b) -> p i b", i=3))
                ins.then_inc(s_grid, 1)
            v.wait_ge(s_row, 16 * 7)

            def normalise(t):
                nc.vector.tensor_scalar(outp[:, t, :], tok[:, t, :], mv[:, t, 0:1], rstd[:, t, :], ALU.subtract, ALU.mult).then_inc(s_norm, 1)

            for n in range(2):
                half = slice(n * HG, (n + 1) * HG)
                for t in range(n * HG, (n + 1) * HG):
                    v.wait_ge(s_sh, t + 1)
                    c.chain(s_tok, nc.vector.tensor_tensor(tok[:, t, :], ps[0:GP, t % 4, 0:P], bias[0:GP, :], ALU.add))
                    ins = nc.vector.bn_stats(stats[:, t, :], tok[:, t, :])
                    if t == HG:
                        v.wait_ge(s_std, 1)
                        c.chain(s_v, nc.vector.reciprocal(rstd[:, 0:HG, 0], std[:, 0:HG, 0]))
                    if t >= HG:
                        normalise(t - HG)
                c.chain(s_v, ins)
                for t in range(n * HG, (n + 1) * HG):
                    ins = nc.vector.bn_aggr(mv[:, t, :], stats[:, t, :])
                c.chain(s_v, ins)
                nc.vector.tensor_scalar(mv[:, half, 1:2], mv[:, half, 1:2], EPS, None, ALU.add).then_inc(s_mv, 1)
            v.wait_ge(s_std, 2)
            c.chain(s_v, nc.vector.reciprocal(rstd[:, half, 0], std[:, half, 0]))
            for t in range(HG, GT):
                normalise(t)
            v.wait_ge(s_norm, GT)
            c.chain(s_v, nc.vector.tensor_tensor(outp[:, half, :], outp[:, half, :], gain[0:GP, :].unsqueeze(1).to_broadcast([GP, HG, D]), ALU.mult))
            nc.vector.tensor_tensor(outp[:, half, :], outp[:, half, :], beta[0:GP, :].unsqueeze(1).to_broadcast([GP, HG, D]), ALU.add).then_inc(s_outp, 1)


class Norm:

    def __init__(self, st, name, rows, tiles, on_scalar=False, stats=None):
        self.rows, self.tiles = rows, tiles
        self.summed = stats is not None
        self.stats = stats if self.summed else st.sb(f"{name}_stats", [rows, tiles, 6])
        self.mv = st.sb(f"{name}_mv", [rows, tiles, 2])
        self.var = st.sb(f"{name}_var", [rows, tiles])
        self.std = st.sb(f"{name}_std", [rows, tiles])
        self.rstd = st.sb(f"{name}_rstd", [rows, tiles])
        self.s_var = st.sem(f"{name}_var_ready")
        self.s_std = st.sem(f"{name}_std_ready")
        if on_scalar:
            self.off = st.sb(f"{name}_off", [rows, tiles])
            self.s_off = st.sem(f"{name}_off_ready")

    def vector(self, nc, v, c, s_v, src, dst, s_dst=None, turn=1):
        norm_measure(self, nc, c, s_v, src, range(self.tiles))
        norm_apply(self, nc, v, c, s_v, src, dst, range(self.tiles), turn, s_dst)
        if s_dst is not None:
            v.wait_ge(s_dst, turn * self.tiles)

    def scalar(self, nc, act, turn=1):
        norm_root(self, nc, act, range(self.tiles), turn)


def norm_measure(ln, nc, c, s_v, src, tiles):
    at = slice(tiles.start, tiles.stop)
    row_stats(c, s_v, nc, None if ln.summed else src, ln.stats, ln.mv, tiles)
    c.chain(ln.s_var, nc.vector.tensor_scalar(ln.var[:, at], ln.mv[:, at, 1], EPS, None, ALU.add))


def norm_root(ln, nc, act, tiles, turn):
    at = slice(tiles.start, tiles.stop)
    act.wait_ge(ln.s_var, turn)
    nc.scalar.activation(ln.std[:, at], ln.var[:, at], ACT.Sqrt).then_inc(ln.s_std, 1)


def norm_rows(ln, nc, src, dst, tiles, s_dst=None):
    for t in tiles:
        ins = nc.vector.tensor_scalar(dst[:, t, :], src[:, t, :], ln.mv[:, t, 0:1], ln.rstd[:, t:t + 1],
                                      ALU.subtract, ALU.mult)
        if s_dst is not None:
            ins.then_inc(s_dst, 1)
    return ins


def norm_apply(ln, nc, v, c, s_v, src, dst, tiles, turn, s_dst=None):
    at = slice(tiles.start, tiles.stop)
    v.wait_ge(ln.s_std, turn)
    c.chain(s_v, nc.vector.reciprocal(ln.rstd[:, at], ln.std[:, at]))
    ins = norm_rows(ln, nc, src, dst, tiles, s_dst)
    if s_dst is None:
        c.chain(s_v, ins)


def norm_factors(ln, nc, v, c, s_v, tiles, turn):
    at = slice(tiles.start, tiles.stop)
    v.wait_ge(ln.s_std, turn)
    c.chain(s_v, nc.vector.reciprocal(ln.rstd[:, at], ln.std[:, at]))
    nc.vector.scalar_tensor_tensor(out=ln.off[:, at], in0=ln.mv[:, at, 0], scalar=-1.0, in1=ln.rstd[:, at],
                                   op0=ALU.mult, op1=ALU.mult).then_inc(ln.s_off, 1)


def norm_rows_scalar(ln, nc, act, src, dst, tiles, turn, s_dst):
    act.wait_ge(ln.s_off, turn)
    for t in tiles:
        nc.scalar.activation(dst[:, t, :], src[:, t, :], ACT.Identity, scale=ln.rstd[:, t:t + 1],
                             bias=ln.off[:, t:t + 1]).then_inc(s_dst, 1)


def load_rows(eng, dst, dram, sem):
    full, last = rows_view(dram)
    eng.dma_start(dst[:, 0:TILES - 1, :], full).then_inc(sem, 16)
    eng.dma_start(dst[0:LAST, TILES - 1, :], last).then_inc(sem, 16)


def rel_attn_stage(nc, a, h_dram, resid, ident, hs, s_weights, weight_max):
    NB = 40
    QT = NB // 4
    HJ = HEADS * IMGS
    PITCH = (IMGS + 1) * HEADS
    with ExitStack() as ctx:
        st = Stage(nc, ctx, "rel")
        rep = st.sb("rep", [P, P * HEADS])
        hmask = st.sb("hmask", [P, HEADS])
        hrows = st.sb("hrows", [P, P])
        post = st.sb("post", [P, IMGS])
        wnat = st.sb("wnat", [P, 5, P])
        wt = st.sb("wt", [P, 5, P])
        cols = st.sb("cols", [P, 4])
        w = st.sb("w", [TP, TILES, D])
        wn = st.sb("wn", [TP, TILES, D])
        wnt = st.sb("wnt", [P, NB, IMGS])
        qw = st.sb("qw", [P, NB * IMGS])
        qr = st.sb("qr", [P, NB * IMGS])
        kexp = st.sb("kexp", [P, NB * IMGS, HEADS])
        rk = st.sb("rk", [P, IMGS])
        rexp = st.sb("rexp", [P, IMGS, HEADS])
        bdp = st.sb("bdp", [P, QT, PITCH])
        bds = st.sb("bds", [P, QT, HJ])
        vrow = st.sb("vrow", [P, QT, P])
        vexp = st.sb("vexp", [P, NB * 2, P])
        sc = st.sb("sc", [P, 2, HJ])
        mx = st.sb("mx", [P, 2, HEADS])
        pr = st.sb("pr", [P, 2, HJ])
        den = st.sb("den", [P, 2, HEADS])
        rden = st.sb("rden", [P, 4, HEADS])
        pt = st.sb("pt", [P, 2, 2, P])
        av = st.sb("av", [P, 2, P])
        avt = st.sb("avt", [P, 2, P])
        ao = st.sb("ao", [P, QT, P])
        aor = wn
        ps = st.ps("ps")
        ln1, ln2 = Norm(st, "ln1", TP, TILES), Norm(st, "ln2", TP, TILES)
        names = ("const", "w", "h", "zero", "v", "wn", "wnt_tp", "wnt", "wt_tp", "wt", "rk", "rexp", "q", "qr", "k", "kx",
                 "v_mm", "v_sb", "vr", "vx", "bd", "bd_sb", "bd_out", "bd_in", "ac", "s", "sub", "e", "den", "pt", "pt_sb",
                 "pv", "av", "avt", "avt_sb", "wo", "ao", "ao_out", "ao_in", "w_rows", "h_plus_w", "qw", "kx_a")
        S = {n: st.sem(n) for n in names}
        bd_dram = nc.dram_tensor("rel_pos_scores", (NB, IMGS * PITCH), F32, kind="Internal").ap()
        ao_dram = nc.dram_tensor("rel_out_rows", (NTOK, D), F32, kind="Internal").ap()
        block = ctx.enter_context(nc.Block())

        @block.sync
        def _(sp):
            sp.wait_ge(S["zero"], 1)
            load_rows(sp, resid, h_dram, S["h"])
            sp.dma_start(ident[:], const(a["consts"], "ident")).then_inc(S["const"], 16)
            sp.dma_start(post[:], const(a["consts"], "rel_pos_t")).then_inc(S["const"], 16)
            sp.dma_start(hmask[:], const(a["consts"], "head_mask")).then_inc(S["const"], 16)
            sp.dma_start(hrows[:], const(a["consts"], "head_rows")).then_inc(S["const"], 16)
            sp.dma_start(rep[:], const(a["consts"], "ident_rep")).then_inc(S["const"], 16)
            for n, name in enumerate(("L0_ffn_Wi", "L0_ffn_Wh")):
                sp.dma_start(gate_weights(hs, n), a[name].rearrange("e i (g h) -> i e g h", g=4)).then_inc(s_weights, 16)
            sp.wait_ge(S["bd_sb"], QT // 2)
            sp.dma_start(bd_dram.rearrange("n (i c) -> (n i) c", i=IMGS).rearrange("(t p) c -> p t c", p=P), bdp[:]).then_inc(S["bd_out"], 16)
            sp.wait_ge(S["bd_out"], 16)
            shifted = bd_dram[:, HJ:HJ + IMGS * HJ].rearrange("(t b) (i c) -> b i t c", b=4, i=IMGS)
            for b in range(4):
                sp.dma_start(bds[32 * b:32 * b + 32, :, :], shifted[b]).then_inc(S["bd_in"], 16)
            sp.wait_ge(S["ao"], QT)
            dst = ao_dram.rearrange("(i n) d -> i n d", n=TOK)
            for b in range(4):
                n = QT if b == 0 else QT - 1
                sp.dma_start(dst[:, b:b + 4 * (n - 1) + 1:4, :], ao[32 * b:32 * b + 32, 0:n, :]).then_inc(S["ao_out"], 16)
            sp.wait_ge(S["ao_out"], 64)
            load_rows(sp, aor, ao_dram, S["ao_in"])

        @block.scalar
        def _(act):
            for k in range(3):
                act.dma_start(wnat[:, k, :], a["L0_attn_Wqkv"][k * D:(k + 1) * D, :]).then_inc(S["w"], 16)
            act.dma_start(wnat[:, 3, :], a["L0_attn_Wr"]).then_inc(S["w"], 16)
            act.dma_start(wnat[:, 4, :], a["L0_attn_Wo"]).then_inc(S["w"], 16)
            act.dma_start(cols[:, 0:1], a["L0_attn_ln_gamma"].rearrange("(d o) -> d o", o=1)).then_inc(S["w"], 16)
            act.dma_start(cols[:, 1:2], a["L0_attn_ln_beta"].rearrange("(d o) -> d o", o=1)).then_inc(S["w"], 16)
            act.dma_start(cols[:, 2:3], a["L0_attn_r_w_bias"].rearrange("n (d o) -> (n d) o", o=1)).then_inc(S["w"], 16)
            act.dma_start(cols[:, 3:4], a["L0_attn_r_r_bias"].rearrange("n (d o) -> (n d) o", o=1)).then_inc(S["w"], 16)
            ln1.scalar(nc, act)
            ln2.scalar(nc, act)
            act.wait_ge(S["w"], 16 * 9)
            for n in range(3):
                act.wait_ge(S["q"], n + 1)
                wd = min(512, NB * IMGS - 512 * n)
                nc.scalar.activation(qr[:, 512 * n:512 * n + wd], ps[:, n, 0:wd], ACT.Identity, bias=cols[:, 3:4]).then_inc(S["qr"], 1)
            for n in range(5):
                act.wait_ge(S["bd"], 2 * n + 2)
                nc.scalar.copy(bdp[:, 2 * n:2 * n + 2, HEADS:PITCH], ps[:, 6 + n % 2, :].rearrange("p (t c) -> p t c", t=2)).then_inc(S["bd_sb"], 1)
            for n in range(3):
                act.wait_ge(S["v_mm"], n + 1)
                wd = min(4, QT - 4 * n)
                nc.scalar.copy(vrow[:, 4 * n:4 * n + wd, :].rearrange("p t d -> p (t d)"), ps[:, n % 2, 0:wd * P]).then_inc(S["v_sb"], 1)
            for h in range(HEADS):
                last = nc.scalar.activation(kexp[:, 512:1024, h], ps[:, 4, :], ACT.Copy, scale=hmask[:, h:h + 1])
            last.then_inc(S["kx_a"], 1)
            for t in range(QT + 5):
                if t < QT:
                    act.wait_ge(S["sub"], t + 1)
                    if t >= 2:
                        act.wait_ge(S["pt"], t - 1)
                        act.wait_ge(S["den"], t - 1)
                    nc.scalar.activation(pr[:, t % 2, :], sc[:, t % 2, :], ACT.Exp, scale=float(DH) ** -0.5).then_inc(S["e"], 1)
                u = t - 1
                if 0 <= u < QT:
                    act.wait_ge(S["pt"], u + 1)
                    if u >= 2:
                        act.wait_ge(S["pv"], u - 1)
                    nc.scalar.copy(pt[:, u % 2, :, :].rearrange("p a b -> p (a b)"), ps[:, 2 + u % 2, 0:2 * P]).then_inc(S["pt_sb"], 1)
                u = t - 3
                if 0 <= u < QT:
                    act.wait_ge(S["avt"], u + 1)
                    if u >= 2:
                        act.wait_ge(S["wo"], u - 1)
                    nc.scalar.copy(avt[:, u % 2, :], ps[:, 6, 0:P]).then_inc(S["avt_sb"], 1)
                u = t - 4
                if 0 <= u < QT:
                    act.wait_ge(S["wo"], u + 1)
                    nc.scalar.copy(ao[:, u, :], ps[:, 7, 0:P]).then_inc(S["ao"], 1)

        @block.tensor
        def _(pe):
            pe.wait_ge(S["const"], 80)
            pe.wait_ge(S["w"], 16 * 9)
            for k in range(5):
                last = nc.tensor.transpose(ps[:, 6 + k // 4, (k % 4) * P:(k % 4) * P + P], wnat[:, k, :], ident[:])
            last.then_inc(S["wt_tp"], 1)
            for t in range(TILES):
                pe.wait_ge(S["wn"], t + 1)
                last = nc.tensor.transpose(ps[:, 3 + t // 4, (t % 4) * TP:(t % 4) * TP + TP], wn[:, t, :], ident[0:TP, 0:TP])
                if t % 4 == 3 or t == TILES - 1:
                    last.then_inc(S["wnt_tp"], 1)
            pe.wait_ge(S["wt"], 1)
            nc.tensor.matmul(ps[:, 7, 128:128 + IMGS], wt[:, 3, :], post[:], start=True, stop=True).then_inc(S["rk"], 1)
            flat = wnt[:].rearrange("p n i -> p (n i)")
            pe.wait_ge(S["wnt"], 3)
            for n in range(3):
                wd = min(512, NB * IMGS - 512 * n)
                nc.tensor.matmul(ps[:, n, 0:wd], wt[:, 0, :], flat[:, 512 * n:512 * n + wd], start=True, stop=True).then_inc(S["q"], 1)
            for n in range(3):
                wd = min(512, NB * IMGS - 512 * n)
                nc.tensor.matmul(ps[:, 3 + n, 0:wd], wt[:, 1, :], flat[:, 512 * n:512 * n + wd], start=True, stop=True).then_inc(S["k"], 1)
            pe.wait_ge(S["rexp"], 2)
            pe.wait_ge(S["qr"], 3)
            for t in range(QT):
                if t % 2 == 0 and t >= 4:
                    pe.wait_ge(S["bd_sb"], t // 2 - 1)
                nc.tensor.matmul(ps[:, 6 + (t // 2) % 2, (t % 2) * HJ:(t % 2) * HJ + HJ], qr[:, t * P:(t + 1) * P],
                                 rexp[:].rearrange("p j n -> p (j n)"), start=True, stop=True).then_inc(S["bd"], 1)
            pe.wait_ge(S["qw"], 3)
            for t in range(QT):
                if t == 8:
                    pe.wait_ge(S["v_sb"], 1)
                last = nc.tensor.matmul(ps[:, (t // 4) % 2, (t % 4) * P:(t % 4) * P + P], flat[:, t * P:(t + 1) * P], wt[:, 2, :], start=True, stop=True)
                if t % 4 == 3 or t == QT - 1:
                    last.then_inc(S["v_mm"], 1)
            pe.wait_ge(S["v_sb"], 3)
            pe.wait_ge(S["bd_sb"], 5)
            for n in range(2 * NB):
                t, b, half = n // 8, (n // 2) % 4, n % 2
                if n % 4 == 0 and n >= 8:
                    pe.wait_ge(S["vx"], n // 4 - 1)
                at = (32 * b + 16 * half) * HEADS
                last = nc.tensor.matmul(ps[:, 6 + (n // 4) % 2, (n % 4) * P:(n % 4) * P + P], rep[:, at:at + P], vrow[:, t, :], start=True, stop=True)
                if n % 4 == 3:
                    last.then_inc(S["vr"], 1)
            pe.wait_ge(S["vx"], 2 * NB // 4)
            pe.wait_ge(S["kx"], 2)
            pe.wait_ge(S["kx_a"], 1)
            for t in range(QT + 4):
                if t < QT:
                    if t >= 2:
                        pe.wait_ge(S["s"], t - 1)
                    for b in range(4):
                        tok = 4 * t + b
                        last = nc.tensor.matmul(ps[32 * b:32 * b + 32, t % 2, 0:HJ], qw[:, tok * IMGS:(tok + 1) * IMGS],
                                                kexp[:, tok * IMGS:(tok + 1) * IMGS, :].rearrange("p j n -> p (j n)"), start=True, stop=True)
                    last.then_inc(S["ac"], 1)
                u = t - 1
                if 0 <= u < QT:
                    pe.wait_ge(S["e"], u + 1)
                    if u >= 2:
                        pe.wait_ge(S["pt_sb"], u - 1)
                    for half in range(2):
                        last = nc.tensor.transpose(ps[:, 2 + u % 2, half * P:half * P + P], pr[:, u % 2, half * P:half * P + P], ident[:])
                    last.then_inc(S["pt"], 1)
                u = t - 2
                if 0 <= u < QT:
                    pe.wait_ge(S["pt_sb"], u + 1)
                    if u >= 2:
                        pe.wait_ge(S["av"], u - 1)
                    for b in range(4):
                        for half in range(2):
                            last = nc.tensor.matmul(ps[32 * b:32 * b + 32, 4 + u % 2, 0:P], pt[:, u % 2, half, 32 * b:32 * b + 32],
                                                    vexp[:, (4 * u + b) * 2 + half, :], start=(half == 0), stop=(half == 1))
                    last.then_inc(S["pv"], 1)
                u = t - 3
                if 0 <= u < QT:
                    pe.wait_ge(S["av"], u + 1)
                    if u >= 1:
                        pe.wait_ge(S["avt_sb"], u)
                    nc.tensor.transpose(ps[:, 6, 0:P], av[:, u % 2, :], ident[:]).then_inc(S["avt"], 1)
                u = t - 4
                if 0 <= u < QT:
                    pe.wait_ge(S["avt_sb"], u + 1)
                    if u >= 1:
                        pe.wait_ge(S["ao"], u)
                    nc.tensor.matmul(ps[:, 7, 0:P], avt[:, u % 2, :], wt[:, 4, :], start=True, stop=True).then_inc(S["wo"], 1)

        @block.gpsimd
        def _(pool):
            pool.wait_ge(S["w_rows"], TILES)
            nc.gpsimd.tensor_tensor(resid[:], resid[:], w[:], ALU.add).then_inc(S["h_plus_w"], 1)

        @block.vector
        def _(v):
            c = Counts(v)
            nc.vector.memset(resid[:, TILES - 1, :], 0.0).then_inc(S["zero"], 1)
            c.chain(S["v"], nc.vector.memset(wnt[:, TOK:NB, :], 0.0))
            c.chain(S["v"], nc.vector.memset(bdp[:, :, 0:HEADS], 0.0))
            v.wait_ge(S["h"], 32)
            ln1.vector(nc, v, c, S["v"], resid, w, S["w_rows"])
            ln2.vector(nc, v, c, S["v"], w, wn, S["wn"])
            v.wait_ge(S["wt_tp"], 1)
            c.chain(S["v"], nc.vector.tensor_copy(wt[:, 0:4, :].rearrange("p q m -> p (q m)"), ps[:, 6, :]))
            nc.vector.tensor_copy(wt[:, 4, :], ps[:, 7, 0:P]).then_inc(S["wt"], 1)
            v.wait_ge(S["w"], 16 * 9)
            for n in range(3):
                v.wait_ge(S["wnt_tp"], n + 1)
                m = min(12, IMGS - 12 * n)
                nc.vector.tensor_scalar(wnt[:, 0:TOK, 12 * n:12 * n + m].rearrange("p t i -> p i t"),
                                        ps[:, 3 + n, 0:m * TOK].rearrange("p (i t) -> p i t", t=TOK),
                                        cols[:, 0:1], cols[:, 1:2], ALU.mult, ALU.add).then_inc(S["wnt"], 1)
            v.wait_ge(S["rk"], 1)
            c.chain(S["rexp"], nc.vector.tensor_copy(rk[:], ps[:, 7, 128:128 + IMGS]))
            c.chain(S["rexp"], nc.vector.tensor_tensor(rexp[:], rk[:].unsqueeze(2).to_broadcast([P, IMGS, HEADS]),
                                                       hmask[:].unsqueeze(1).to_broadcast([P, IMGS, HEADS]), ALU.mult))
            for n in range(3):
                wd = min(512, NB * IMGS - 512 * n)
                v.wait_ge(S["qr"], n + 1)
                c.chain(S["qw"], nc.vector.tensor_scalar(qw[:, 512 * n:512 * n + wd], ps[:, n, 0:wd], cols[:, 2:3], None, ALU.add))
            for n in (0, 2):
                wd = min(512, NB * IMGS - 512 * n)
                v.wait_ge(S["k"], n + 1)
                nc.vector.tensor_tensor(kexp[:, 512 * n:512 * n + wd, :], ps[:, 3 + n, 0:wd].unsqueeze(2).to_broadcast([P, wd, HEADS]),
                                        hmask[:].unsqueeze(1).to_broadcast([P, wd, HEADS]), ALU.mult).then_inc(S["kx"], 1)
            for n in range(2 * NB // 4):
                v.wait_ge(S["vr"], n + 1)
                nc.vector.tensor_tensor(vexp[:, 4 * n:4 * n + 4, :], ps[:, 6 + n % 2, :].rearrange("p (a d) -> p a d", a=4),
                                        hrows[:].unsqueeze(1).to_broadcast([P, 4, P]), ALU.mult).then_inc(S["vx"], 1)
            v.wait_ge(S["bd_in"], 64)
            for t in range(QT + 2):
                if t < QT:
                    v.wait_ge(S["ac"], t + 1)
                    if t >= 2:
                        v.wait_ge(S["e"], t - 1)
                    c.chain(S["s"], nc.vector.tensor_tensor(sc[:, t % 2, :], ps[:, t % 2, 0:HJ], bds[:, t, :], ALU.add))
                    sv = sc[:, t % 2, :].rearrange("p (j n) -> p j n", n=HEADS)
                    c.chain(S["v"], nc.vector.tensor_reduce(mx[:, t % 2, :], sv.rearrange("p j n -> p n j"), AX_X, ALU.max))
                    nc.vector.tensor_tensor(sv, sv, mx[:, t % 2, :].unsqueeze(1).to_broadcast([P, IMGS, HEADS]), ALU.subtract).then_inc(S["sub"], 1)
                u = t - 1
                if 0 <= u < QT:
                    v.wait_ge(S["e"], u + 1)
                    c.chain(S["den"], nc.vector.tensor_reduce(den[:, u % 2, :], pr[:, u % 2, :].rearrange("p (j n) -> p n j", n=HEADS), AX_X, ALU.add))
                    c.chain(S["v"], nc.vector.reciprocal(rden[:, u % 4, :], den[:, u % 2, :]))
                u = t - 2
                if 0 <= u < QT:
                    v.wait_ge(S["pv"], u + 1)
                    if u >= 2:
                        v.wait_ge(S["avt"], u - 1)
                    nc.vector.tensor_tensor(av[:, u % 2, :].rearrange("p (n d) -> p n d", n=HEADS),
                                            ps[:, 4 + u % 2, 0:P].rearrange("p (n d) -> p n d", n=HEADS),
                                            rden[:, u % 4, :].unsqueeze(2).to_broadcast([P, HEADS, DH]), ALU.mult).then_inc(S["av"], 1)
            v.wait_ge(s_weights, 32)
            for n in range(2):
                nc.vector.tensor_reduce(weight_max[:, n:n + 1], gate_weights(hs, n).rearrange("p e g h -> p (e g h)"), AX_X, ALU.max, apply_absolute_value=True)
            v.wait_ge(S["ao_in"], 32)
            v.wait_ge(S["h_plus_w"], 1)
            c.chain(S["v"], nc.vector.tensor_tensor(resid[:, 0:TILES - 1, :], resid[:, 0:TILES - 1, :], aor[:, 0:TILES - 1, :], ALU.add))
            c.chain(S["v"], nc.vector.tensor_tensor(resid[0:LAST, TILES - 1, :], resid[0:LAST, TILES - 1, :], aor[0:LAST, TILES - 1, :], ALU.add))


def transpose_rows(nc, pe, rows, ident, ps, bank0, s_rows, s_tp):
    for t in range(TILES):
        pe.wait_ge(s_rows, t + 1)
        last = nc.tensor.transpose(ps[:, bank0 + t // 4, (t % 4) * TP:(t % 4) * TP + TP], rows[:, t, :], ident[0:TP, 0:TP])
        if t % 4 == 3 or t == TILES - 1:
            last.then_inc(s_tp, 1)


SPANS = [(4 * n * TP, min(4, TILES - 4 * n) * TP) for n in range(3)]


def lstm_stage(nc, a, resid, ident, hs, s_weights, weight_max, gru_w, row_sums):
    F16 = mybir.dt.float16
    KE = 2 * EXPERTS
    G = 4
    EG = EXPERTS // 2
    N = 2 * TOK
    with ExitStack() as ctx:
        st = Stage(nc, ctx, "moe")
        gate_half = st.sb("gate_half", [P, 1])
        w_hi = [st.sb(f"w_hi{n}", [P, EXPERTS, G, P], F16) for n in range(2)]
        w_lo = [st.sb(f"w_lo{n}", [P, EXPERTS, G, P], F16) for n in range(2)]
        scale = st.sb("scale", [P, 6])
        sbits = st.sb("sbits", [P, 2], U32)
        bias = st.sb("bias", [P, EXPERTS, G])
        wo = st.sb("wo", [P, EXPERTS, P])
        bo = st.sb("bo", [EXPERTS, P])
        x_hi = st.sb("x_hi", [P, COLS], F16)
        x_lo = st.sb("x_lo", [P, COLS], F16)
        ct = st.sb("ct", [EXPERTS, COLS])
        mask = st.sb("mask", [P, KE, COLS], F16)
        rwt = st.sb("rwt", [P, 2, COLS])
        cell = st.sb("cell", [P, 2, EG, N])
        ps = st.ps("ps")
        names = ("const", "w", "bias", "wo", "zero", "v", "pool", "xn", "xt_tp", "xt", "lg", "top", "e1", "pack", "mt_tp", "mt",
                 "bc", "bc_v", "bc_a", "x_hi", "x_lo", "w_scaled", "gru_w", "amax", "allmax", "scale", "w_hi", "w_lo", "wf_used", "wf1", "brem", "bias_tp", "bias_sb", "primed", "y", "y_sb",
                 "lv", "xm", "hm", "wst", "hs", "table")
        S = {n: st.sem(n) for n in names}
        s_gates = [st.sem(f"gates_mm{g}") for g in range(2)]
        s_tanh = [st.sem(f"gates_tanh{g}") for g in range(2)]
        s_bias = [st.sem(f"gates_bias{g}") for g in range(2)]
        s_cell = [st.sem(f"cell{g}") for g in range(2)]
        s_tc = [st.sem(f"cell_tanh{g}") for g in range(2)]
        s_h = [st.sem(f"state{g}") for g in range(2)]
        blocks = [(j, n) for j in (KE, KE + 1, *range(KE)) for n in range(3)]

        def by_vector(b):
            return b >= 8 and b % 2 == 0

        def read(b):
            same = sum(by_vector(o) == by_vector(b) for o in range(b + 1))
            return S["bc_v"] if by_vector(b) else S["bc_a"], same

        with ExitStack() as before:
            pre = Stage(nc, before, "moe")
            iota = pre.sb("iota", [P, 8])
            row_sel = pre.sb("row_sel", [18, 18, P])
            row_sel16 = pre.sb("row_sel16", [18, KE, P], F16)
            rw = pre.sb("rw", [P, EXPERTS])
            rb = pre.sb("rb", [TP, EXPERTS])
            amax = pre.sb("amax", [P, 4])
            bf = pre.sb("bf", [32, P])
            brem = pre.sb("brem", [32, P])
            xn = pre.sb("xn", [TP, TILES, D])
            xt = pre.sb("xt", [P, COLS])
            lg = pre.sb("lg", [TP, TILES, 8])
            top = pre.sb("top", [TP, TILES, 8])
            topi = pre.sb("topi", [TP, TILES, 8], U32)
            topf = pre.sb("topf", [TP, TILES, 2])
            pack = pre.sb("pack", [TP, TILES, 18])
            comb = pre.sb("comb", [TP, TILES, 2, 8])
            e1 = pre.sb("e1", [TP, TILES, 3])
            mt = pre.sb("mt", [18, COLS])
            mt16 = pre.sb("mt16", [18, COLS], F16)
            ln = Norm(pre, "ln", TP, TILES)
            with nc.Block() as block:
                @block.sync
                def _(sp):
                    sp.dma_start(rw[:], a["L0_ffn_router_w"]).then_inc(S["const"], 16)
                    sp.dma_start(rb[:], a["L0_ffn_router_b"].partition_broadcast(TP)).then_inc(S["const"], 16)
                    sp.dma_start(iota[:], const(a["consts"], "iota8")).then_inc(S["const"], 16)
                    sp.dma_start(gate_half[:], const(a["consts"], "gate_half"), allow_slow_non_contiguous=True).then_inc(S["const"], 16)
                    sp.dma_start(row_sel[:], const(a["consts"], "row_sel", 18).rearrange("p (j m) -> p j m", j=18)).then_inc(S["const"], 16)
                    sp.dma_start(bf[:], a["L0_ffn_b"].rearrange("e (g h) -> (e g) h", g=G)).then_inc(S["bias"], 16)
                    sp.dma_start(wo[:], a["L0_ffn_Wo"].rearrange("e h o -> h e o")).then_inc(S["wo"], 16)
                    sp.dma_start(bo[:], a["L0_ffn_bo"]).then_inc(S["wo"], 16)
                    for n, name in enumerate(("L1_attn_gru_wih", "L1_attn_gru_whh")):
                        sp.dma_start(gru_w[:, 12 * n:12 * n + 12, :], a[name].rearrange("k (g i) j -> i (k g) j", g=3)).then_inc(S["gru_w"], 16)

                @block.scalar
                def _(act):
                    ln.scalar(nc, act)
                    act.wait_ge(S["xt"], 3)
                    nc.scalar.copy(x_hi[:], xt[:]).then_inc(S["x_hi"], 1)
                    act.wait_ge(S["top"], 2)
                    nc.scalar.activation(e1[:, :, 1], e1[:, :, 0], ACT.Exp).then_inc(S["e1"], 1)
                    act.wait_ge(S["scale"], 6)
                    for n in range(2):
                        src = gate_weights(hs, n)
                        for g0, g1, col in ((0, 2, 1 + n), (2, 3, n), (3, 4, 1 + n)):
                            nc.scalar.activation(w_hi[n][:, :, g0:g1, :], src[:, :, g0:g1, :], ACT.Copy, scale=scale[:, col:col + 1]).then_inc(S["w_hi"], 1)
                        if n == 0:
                            act.wait_ge(S["mt_tp"], 1)
                            for m, (at, wd) in enumerate(SPANS):
                                nc.scalar.activation(ct[:, at:at + wd], ps[0:8, 3 + m, 0:wd], ACT.Copy, scale=2.0).then_inc(S["mt"], 1)
                    for b, (j, n) in enumerate(blocks):
                        if not by_vector(b):
                            act.wait_ge(S["bc"], b + 1)
                            at, wd = SPANS[n]
                            dst = mask[:, j, at:at + wd] if j < KE else rwt[:, j - KE, at:at + wd]
                            nc.scalar.copy(dst, ps[:, b % 6, 0:wd]).then_inc(S["bc_a"], 1)

                @block.gpsimd
                def _(pool):
                    for g in range(2):
                        nc.gpsimd.memset(cell[:, g, :, :], 0.0).then_inc(S["zero"], 1)
                    pool.wait_ge(S["amax"], 1)
                    nc.gpsimd.partition_all_reduce(amax[:, 3:4], amax[:, 2:3], P, bass.bass_isa.ReduceOp.max).then_inc(S["allmax"], 1)
                    pool.wait_ge(S["const"], 80)
                    nc.gpsimd.tensor_copy(row_sel16[:], row_sel[:, 0:KE, :]).then_inc(S["mt"], 1)
                    pool.wait_ge(S["x_hi"], 1)
                    nc.gpsimd.tensor_tensor(x_lo[:], xt[:], x_hi[:], ALU.subtract).then_inc(S["x_lo"], 1)
                    src = gate_weights(hs, 1)
                    for k, (g0, g1, col) in enumerate(((0, 2, 2), (2, 3, 1), (3, 4, 2))):
                        pool.wait_ge(S["w_hi"], 3 + k + 1)
                        nc.gpsimd.tensor_scalar(src[:, :, g0:g1, :], src[:, :, g0:g1, :], scale[:, col:col + 1], None, ALU.mult).then_inc(S["w_scaled"], 1)
                        pool.wait_ge(S["w_scaled"], k + 1)
                        nc.gpsimd.tensor_tensor(w_lo[1][:, :, g0:g1, :], src[:, :, g0:g1, :], w_hi[1][:, :, g0:g1, :], ALU.subtract).then_inc(S["w_lo"], 1)

                @block.tensor
                def _(pe):
                    transpose_rows(nc, pe, xn, ident, ps, 0, S["xn"], S["xt_tp"])
                    pe.wait_ge(S["xt"], 3)
                    pe.wait_ge(S["const"], 80)
                    for t in range(TILES):
                        last = nc.tensor.matmul(ps[0:TP, 3, 8 * t:8 * t + 8], xt[:, t * TP:(t + 1) * TP], rw[:], start=True, stop=True)
                    last.then_inc(S["lg"], 1)
                    pe.wait_ge(S["pack"], 1)
                    for t in range(TILES):
                        last = nc.tensor.transpose(ps[0:18, t // 4, (t % 4) * TP:(t % 4) * TP + TP], pack[:, t, :], ident[0:TP, 0:TP])
                    for t in range(TILES):
                        last = nc.tensor.transpose(ps[0:8, 3 + t // 4, (t % 4) * TP:(t % 4) * TP + TP], comb[:, t, 0, :], ident[0:TP, 0:TP])
                    last.then_inc(S["mt_tp"], 1)
                    pe.wait_ge(S["mt"], 10)
                    pe.wait_ge(S["brem"], 1)
                    nc.tensor.transpose(ps[:, 7, 0:32], brem[:], ident[0:32, 0:32]).then_inc(S["bias_tp"], 1)
                    for b, (j, n) in enumerate(blocks):
                        at, wd = SPANS[n]
                        if b >= 6:
                            pe.wait_ge(*read(b - 6))
                        lhs, rhs = (row_sel16, mt16) if j < KE else (row_sel, mt)
                        nc.tensor.matmul(ps[:, b % 6, 0:wd], lhs[:, j, :], rhs[:, at:at + wd], start=True, stop=True).then_inc(S["bc"], 1)

                @block.vector
                def _(v):
                    c = Counts(v)
                    ln.vector(nc, v, c, S["v"], resid, xn, S["xn"])
                    for n, (at, wd) in enumerate(SPANS):
                        v.wait_ge(S["xt_tp"], n + 1)
                        nc.vector.tensor_copy(xt[:, at:at + wd], ps[:, n, 0:wd]).then_inc(S["xt"], 1)
                    v.wait_ge(s_weights, 32)
                    c.chain(S["v"], nc.vector.tensor_tensor(amax[:, 2:3], weight_max[:, 0:1], weight_max[:, 1:2], ALU.max))
                    c.chain(S["amax"], nc.vector.tensor_copy(amax[:, 0:1], amax[:, 2:3]))
                    v.wait_ge(S["lg"], 1)
                    v.wait_ge(S["const"], 80)
                    c.chain(S["v"], nc.vector.tensor_tensor(lg[:], ps[0:TP, 3, 0:8 * TILES].rearrange("p (t e) -> p t e", e=8),
                                                            rb[:].unsqueeze(1).to_broadcast([TP, TILES, 8]), ALU.add))
                    for t in range(TILES):
                        ins = nc.vector.max(top[:, t, :], lg[:, t, :])
                    c.chain(S["v"], ins)
                    for t in range(TILES):
                        ins = nc.vector.max_index(topi[:, t, :], top[:, t, :], lg[:, t, :])
                    c.chain(S["top"], ins)
                    c.chain(S["top"], nc.vector.tensor_tensor(e1[:, :, 0], top[:, :, 1], top[:, :, 0], ALU.subtract))
                    c.chain(S["v"], nc.vector.tensor_copy(topf[:], topi[:, :, 0:2]))
                    for k in range(2):
                        ins = nc.vector.tensor_tensor(pack[:, :, 8 * k:8 * k + 8], iota[0:TP, :].unsqueeze(1).to_broadcast([TP, TILES, 8]),
                                                      topf[:, :, k:k + 1].to_broadcast([TP, TILES, 8]), ALU.is_equal)
                    v.wait_ge(S["e1"], 1)
                    c.chain(S["v"], nc.vector.tensor_scalar(e1[:, :, 2], e1[:, :, 1], 1.0, None, ALU.add))
                    c.chain(S["v"], nc.vector.reciprocal(pack[:, :, 16], e1[:, :, 2]))
                    c.chain(S["v"], nc.vector.tensor_tensor(pack[:, :, 17], pack[:, :, 16], e1[:, :, 1], ALU.mult))
                    for k in range(2):
                        ins = nc.vector.tensor_tensor(comb[:, :, k, :], pack[:, :, 8 * k:8 * k + 8],
                                                      pack[:, :, 16 + k:17 + k].to_broadcast([TP, TILES, 8]), ALU.mult)
                    c.chain(S["v"], ins)
                    c.chain(S["pack"], nc.vector.tensor_tensor(comb[:, :, 0, :], comb[:, :, 0, :], comb[:, :, 1, :], ALU.add))
                    v.wait_ge(S["allmax"], 1)
                    c.chain(S["v"], nc.vector.tensor_scalar(amax[:, 3:4], amax[:, 3:4], 1e-25, None, ALU.max))
                    c.chain(S["v"], nc.vector.tensor_scalar(sbits[:, 0:1], amax[:, 3:4].bitcast(U32), 0x7F800000, None, ALU.bitwise_and))
                    c.chain(S["v"], nc.vector.tensor_scalar(sbits[:, 1:2], sbits[:, 0:1], -1.0, float(267 << 23), ALU.mult, ALU.add))
                    c.chain(S["scale"], nc.vector.tensor_copy(scale[:, 0:1], sbits[:, 1:2].bitcast(F32)))
                    c.chain(S["scale"], nc.vector.tensor_scalar(scale[:, 1:2], scale[:, 0:1], 0.5, None, ALU.mult))
                    c.chain(S["scale"], nc.vector.tensor_scalar(scale[:, 2:3], scale[:, 0:1], 0.25, None, ALU.mult))
                    c.chain(S["scale"], nc.vector.tensor_scalar(scale[:, 3:4], sbits[:, 0:1].bitcast(F32), 2.0 ** -13, None, ALU.mult))
                    c.chain(S["scale"], nc.vector.tensor_tensor(scale[:, 4:5], scale[:, 0:1], gate_half[:], ALU.mult))
                    c.chain(S["scale"], nc.vector.tensor_copy(scale[:, 5:6], scale[:, 0:1]))
                    v.wait_ge(S["mt_tp"], 1)
                    for n, (at, wd) in enumerate(SPANS):
                        nc.vector.tensor_copy(mt[:, at:at + wd], ps[0:18, n, 0:wd]).then_inc(S["mt"], 1)
                        nc.vector.tensor_copy(mt16[:, at:at + wd], ps[0:18, n, 0:wd]).then_inc(S["mt"], 1)
                    v.wait_ge(S["bias"], 16)
                    nc.vector.tensor_scalar(brem[:], bf[:], scale[0:32, 4:5], None, ALU.mult).then_inc(S["brem"], 1)
                    v.wait_ge(S["bias_tp"], 1)
                    nc.vector.tensor_copy(bias[:].rearrange("p e g -> p (e g)"), ps[:, 7, 0:32]).then_inc(S["bias_sb"], 1)
                    src = gate_weights(hs, 0)
                    for k, (g0, g1, col) in enumerate(((0, 2, 1), (2, 3, 0), (3, 4, 1))):
                        v.wait_ge(S["w_hi"], k + 1)
                        for e in range(EXPERTS):
                            nc.vector.scalar_tensor_tensor(out=w_lo[0][:, e, g0:g1, :], in0=src[:, e, g0:g1, :], scalar=scale[:, col:col + 1],
                                                           in1=w_hi[0][:, e, g0:g1, :], op0=ALU.mult, op1=ALU.subtract).then_inc(S["w_lo"], 1)
                    for b, (j, n) in enumerate(blocks):
                        if by_vector(b):
                            v.wait_ge(S["bc"], b + 1)
                            at, wd = SPANS[n]
                            dst = mask[:, j, at:at + wd] if j < KE else rwt[:, j - KE, at:at + wd]
                            nc.vector.tensor_copy(dst, ps[:, b % 6, 0:wd]).then_inc(S["bc_v"], 1)


        STEPS = 2
        TURNS = IMGS // STEPS
        with ExitStack() as during:
            loop = Stage(nc, during, "moe")
            xm_hi = loop.sb("xm_hi", [P, 2, KE, TOK], F16)
            xm_lo = loop.sb("xm_lo", [P, 2, KE, TOK], F16)
            gates = loop.sb("gates", [P, 2, EG, G, N])
            fc = loop.sb("fc", [P, 2, EG, N])
            ig = loop.sb("ig", [P, 2, EG, N])
            tc = loop.sb("tc", [P, 2, EG, N])
            hf = loop.sb("hf", [P, 2, 2, EG, N])
            hm = loop.sb("hm", [P, 2, EXPERTS, N])
            h_hi = loop.sb("h_hi", [P, 2, EG, N], F16)
            h_lo = loop.sb("h_lo", [P, 2, EG, N], F16)
            wst = loop.sb("wst", [P, 2, 2, EXPERTS, TOK])
            with nc.Block() as block:
                @block.tensor
                def _(pe):
                    for ex in range(EXPERTS):
                        for q in range(G):
                            last = nc.tensor.matmul(ps[:, ex, q * N:(q + 1) * N], w_hi[0][:, ex, q, :], x_hi[:, 0:N], start=(q == 0), stop=False, skip_group_check=True)
                    last.then_inc(S["primed"], 1)
                    with pe.Fori(0, TURNS) as i:
                        for s in range(STEPS):
                            pe.wait_ge(S["xm"], i * (2 * STEPS) + (2 * s + 2))
                            for g in range(2):
                                pe.wait_ge(s_bias[g], i * STEPS + (s + 1))
                                for e in range(EG):
                                    ex = g * EG + e
                                    rhs = [m[:, s, ex:KE:EXPERTS, :] for m in (xm_hi, xm_hi, xm_lo)]
                                    for q in range(G):
                                        dst = ps[:, g * EG + e, q * N:(q + 1) * N]
                                        for k, wgt in enumerate((w_hi, w_lo, w_hi)):
                                            nc.tensor.matmul(dst, wgt[0][:, ex, q, :], rhs[k], start=False, stop=False, skip_group_check=True)
                                pe.wait_ge(s_h[g], i * STEPS + (s + 1))
                                for e in range(EG):
                                    ex = g * EG + e
                                    for q in range(G):
                                        dst = ps[:, g * EG + e, q * N:(q + 1) * N]
                                        for k, (wgt, h) in enumerate(((w_hi, h_hi), (w_lo, h_hi), (w_hi, h_lo))):
                                            last = nc.tensor.matmul(dst, wgt[1][:, ex, q, :], h[:, g, e, :], start=False, stop=False, skip_group_check=True)
                                last.then_inc(s_gates[g], 1)

                @block.scalar
                def _(act):
                    def put_biases(g):
                        nc.scalar.copy(ps[:, g * EG:(g + 1) * EG, 0:G * N].rearrange("p e (q n) -> p e q n", q=G),
                                       bias[:, g * EG:(g + 1) * EG, :].unsqueeze(3).to_broadcast([P, EG, G, N])).then_inc(s_bias[g], 1)

                    for g in range(2):
                        nc.scalar.activation(tc[:, g, 0, 0:1], cell[:, g, 0, 0:1], ACT.Tanh).then_inc(s_tanh[g], 1)
                        act.wait_ge(s_tanh[g], 1)
                    act.wait_ge(S["primed"], 1)
                    for g in range(2):
                        put_biases(g)
                    with act.Fori(0, TURNS) as i:
                        for s in range(STEPS):
                            for g in range(2):
                                act.wait_ge(s_gates[g], i * STEPS + (s + 1))
                                nc.scalar.activation(gates[:, g, :, :, :].rearrange("p e q n -> p e (q n)"), ps[:, g * EG:(g + 1) * EG, 0:G * N],
                                                     ACT.Tanh, scale=scale[:, 3:4]).then_inc(s_tanh[g], 1)
                                act.wait_ge(s_tanh[g], i * STEPS + (s + 2))
                                put_biases(g)
                                act.wait_ge(s_cell[g], i * STEPS + (s + 1))
                                nc.scalar.activation(tc[:, g, :, :], cell[:, g, :, :], ACT.Tanh, scale=0.5).then_inc(s_tc[g], 1)

                @block.vector
                def _(v):
                    LV = 2 * 3
                    def mask_inputs(n, s, cols):
                        x, m = ((x_hi, xm_hi), (x_lo, xm_lo))[n]
                        nc.vector.tensor_tensor(m[:, s, :, :], x[:, cols].unsqueeze(1).to_broadcast([P, KE, TOK]),
                                                mask[:, :, cols], ALU.mult).then_inc(S["xm"], 1)

                    def cell_step(i, s, g):
                        v.wait_ge(s_tanh[g], i * STEPS + (s + 2))
                        nc.vector.scalar_tensor_tensor(out=fc[:, g, :, :], in0=gates[:, g, :, 1, :], scalar=1.0, in1=cell[:, g, :, :], op0=ALU.add, op1=ALU.mult)
                        nc.vector.scalar_tensor_tensor(out=ig[:, g, :, :], in0=gates[:, g, :, 0, :], scalar=1.0, in1=gates[:, g, :, 2, :],
                                                       op0=ALU.add, op1=ALU.mult).then_inc(S["lv"], 1)
                        v.wait_ge(S["lv"], i * (LV * STEPS) + (LV * s + 3 * g + 1))
                        nc.vector.scalar_tensor_tensor(out=cell[:, g, :, :], in0=fc[:, g, :, :], scalar=0.5, in1=ig[:, g, :, :],
                                                       op0=ALU.mult, op1=ALU.add).then_inc(s_cell[g], 1)

                    def state_step(i, s, g):
                        v.wait_ge(s_tc[g], i * STEPS + (s + 1))
                        nc.vector.scalar_tensor_tensor(out=h_hi[:, g, :, :], in0=gates[:, g, :, 3, :], scalar=1.0, in1=tc[:, g, :, :], op0=ALU.add,
                                                       op1=ALU.mult).then_inc(S["lv"], 1)
                        nc.vector.scalar_tensor_tensor(out=hf[:, s, g, :, :], in0=gates[:, g, :, 3, :], scalar=1.0, in1=tc[:, g, :, :], op0=ALU.add,
                                                       op1=ALU.mult).then_inc(S["lv"], 1)
                        v.wait_ge(S["lv"], i * (LV * STEPS) + (LV * s + 3 * g + 3))
                        nc.vector.tensor_tensor(h_lo[:, g, :, :], hf[:, s, g, :, :], h_hi[:, g, :, :], ALU.subtract).then_inc(s_h[g], 1)

                    def pick(s, cols):
                        nc.vector.tensor_tensor(hs[:, :, cols], hm[:, s, :, 0:TOK], hm[:, s, :, TOK:N], ALU.add).then_inc(S["hs"], 1)

                    for g in range(2):
                        nc.vector.memset(h_hi[:, g, :, :], 0.0).then_inc(S["hs"], 1)
                        v.wait_ge(S["hs"], g + 1)
                        nc.vector.memset(h_lo[:, g, :, :], 0.0).then_inc(s_h[g], 1)
                    for n in range(2):
                        mask_inputs(n, 0, slice(0, TOK))
                    with v.Fori(0, TURNS) as i:
                        for s in range(STEPS):
                            mask_inputs(0, 1 - s, bass.ds(i * (STEPS * TOK) + (s + 1) * TOK, TOK))
                            cell_step(i, s, 0)
                            mask_inputs(1, 1 - s, bass.ds(i * (STEPS * TOK) + (s + 1) * TOK, TOK))
                            state_step(i, s, 0)
                            cell_step(i, s, 1)
                            v.wait_ge(S["hm"], i * (2 * STEPS) + (2 * s + 2))
                            pick(1 - s, bass.ds(i * (STEPS * TOK) + s * TOK, TOK))
                            state_step(i, s, 1)
                    v.wait_ge(S["hm"], 2 * IMGS + 2)
                    pick(1, slice(NTOK, COLS))

                @block.gpsimd
                def _(pool):
                    for g in range(2):
                        nc.gpsimd.memset(hm[:, 1, g * EG:(g + 1) * EG, :], 0.0).then_inc(S["hm"], 1)
                    with pool.Fori(0, TURNS) as i:
                        for s in range(STEPS):
                            cols = bass.ds(i * (STEPS * TOK) + s * TOK, TOK)
                            nc.gpsimd.tensor_tensor(wst[:, s, :, :, :], mask[:, :, cols].rearrange("p (k e) n -> p k e n", k=2),
                                                    rwt[:, :, cols].unsqueeze(2).to_broadcast([P, 2, EXPERTS, TOK]), ALU.mult).then_inc(S["wst"], 1)
                            pool.wait_ge(S["wst"], i * STEPS + (s + 1))
                            for g in range(2):
                                pool.wait_ge(s_h[g], i * STEPS + (s + 2))
                                nc.gpsimd.tensor_tensor(hm[:, s, g * EG:(g + 1) * EG, :].rearrange("p e (k n) -> p e k n", k=2),
                                                        hf[:, s, g, :, :].rearrange("p e (k n) -> p e k n", k=2),
                                                        wst[:, s, :, g * EG:(g + 1) * EG, :].rearrange("p k e n -> p e k n"), ALU.mult).then_inc(S["hm"], 1)

        with nc.Block() as block:
            @block.tensor
            def _(pe):
                pe.wait_ge(S["wo"], 32)
                for t in range(TILES):
                    if t >= 4:
                        pe.wait_ge(S["y_sb"], t - 2)
                    n = TP if t < TILES - 1 else LAST
                    dst = ps[0:n, t % 4, 0:P]
                    nc.tensor.matmul(dst, ct[:, t * TP:t * TP + n], bo[:], start=True, stop=False)
                    for e in range(EXPERTS):
                        last = nc.tensor.matmul(dst, hs[:, e, TOK + t * TP:TOK + t * TP + n], wo[:, e, :], start=False, stop=(e == EXPERTS - 1))
                    last.then_inc(S["y"], 1)

            @block.vector
            def _(v):
                for t in range(TILES):
                    n = TP if t < TILES - 1 else LAST
                    v.wait_ge(S["y"], t + 1)
                    nc.vector.scalar_tensor_tensor(out=resid[0:n, t, :], in0=ps[0:n, t % 4, 0:P], scalar=0.5, in1=resid[0:n, t, :],
                                                   op0=ALU.mult, op1=ALU.add).then_inc(S["y_sb"], 1)
                    v.wait_ge(S["y_sb"], t + 1)
                    nc.vector.bn_stats(row_sums[:, t, :], resid[:, t, :])

            @block.sync
            def _(sp):
                sp.wait_ge(S["gru_w"], 32)


def gate_weights(hs, n):
    return hs[:].rearrange("p e n -> p (e n)")[:, 4096 * n:4096 * (n + 1)].rearrange("p (e g h) -> p e g h", e=EXPERTS, g=4)


def power_of_two(nc, c, s_v, top, bits, scale, inverse):
    c.chain(s_v, nc.vector.tensor_scalar(top, top, 1e-25, None, ALU.max))
    c.chain(s_v, nc.vector.tensor_scalar(bits[:, 0:1], top.bitcast(U32), 0x7F800000, None, ALU.bitwise_and))
    c.chain(s_v, nc.vector.tensor_scalar(bits[:, 1:2], bits[:, 0:1], -1.0, float(267 << 23), ALU.mult, ALU.add))
    c.chain(s_v, nc.vector.tensor_copy(scale, bits[:, 1:2].bitcast(F32)))
    c.chain(s_v, nc.vector.tensor_scalar(inverse, bits[:, 0:1].bitcast(F32), 2.0 ** -13, None, ALU.mult))


def thread_stage(nc, a, resid, ident, hs, gru_w, row_sums):
    F16 = mybir.dt.float16
    K = THREADS
    B = IMGS
    KT = K * TILES
    WIH, WHH = 0, 12
    WQ, WK, WV, WB, WM = 0, 4, 8, 12, 20
    NW = 48
    with ExitStack() as ctx:
        st = Stage(nc, ctx, "thr")
        x1 = st.sb("x1", [TP, TILES, D])
        x1s = st.sb("x1s", [TP, TILES, D])
        wt = st.sb("wt", [P, NW // 2, P])

        def by_scalar(n):
            return n < NW // 8 or n % 2 == 1

        def copied(n):
            return S["wt_act"] if by_scalar(n) else S["wt_sb"], sum(by_scalar(m) == by_scalar(n) for m in range(n + 1))

        def quad(n):
            return gru_w[:, 4 * n:4 * n + 4, :] if n < NW // 8 else wt[:, 4 * n - NW // 2:4 * n - NW // 2 + 4, :]

        scale = st.sb("scale", [P, 4])
        x_hi = st.sb("x_hi", [P, TOK, B], F16)
        x_lo = st.sb("x_lo", [P, TOK, B], F16)
        wi_hi = st.sb("wi_hi", [P, 12, P], F16)
        wi_lo = st.sb("wi_lo", [P, 12, P], F16)
        wh_hi = st.sb("wh_hi", [P, 12, P], F16)
        wh_lo = st.sb("wh_lo", [P, 12, P], F16)
        brow = st.sb("brow", [P, 12, P], BF16)
        ones = st.sb("ones", [P, B], BF16)
        ncols = st.sb("ncols", [P, 4 + 4])
        aot = st.sb("aot", [P, K, COLS])
        xn_in = st.sb("xn_in", [P, TOK, K, B])
        gbt = hs[:, 0:K, :]
        steps = gbt[:, :, 0:NTOK].rearrange("p k (b t) -> p k b t", t=TOK)
        bn_rows = st.sb("bn_rows", [TP, 2, D])
        ps = st.ps("ps")
        names = ("const", "pool", "w", "v", "xn", "xt_tp", "xt", "wtp", "wt_sb", "amax", "allmax", "whi", "wlo", "rows", "bparts", "brow", "col_tp", "cols",
                 "pj", "pj_sb", "zero", "sc", "sub", "e", "p", "pt", "pt_sb", "ao", "ao_sb", "gru_in", "lv", "table", "thn_a", "beat",
                 "rden", "shift", "shift_mm", "x1s", "wt_act", "th", "tht", "tht_sb", "mix", "mix_sb", "thn", "xh")
        S = {n: st.sem(n) for n in names}
        s_r, s_z, s_n = st.sem("r_mm"), st.sem("z_mm"), st.sem("n_mm")
        s_tr, s_tz, s_tn, s_np, s_hi, s_lo = (st.sem(n) for n in ("r_tanh", "z_tanh", "n_tanh", "n_pre", "state_hi", "state_lo"))

        with ExitStack() as inner:
            sa = Stage(nc, inner, "thr")
            win = sa.sb("win", [TP, K, TP])
            qt, kt = hs[:, 0:K, :], hs[:, K:2 * K, :]
            vr = sa.sb("vr", [TP, TILES, K, P])
            with ExitStack() as first:
                sp_ = Stage(nc, first, "thr")
                xt = sp_.sb("xt", [P, COLS])
                pos = sp_.sb("pos", [TP, D])
                amax = sp_.sb("amax", [P, 2])
                sbits = sp_.sb("sbits", [P, 2], U32)
                rows = sp_.sb("rows", [12, 2, P])
                nrows = sp_.sb("nrows", [2 * K, P])
                facts = sp_.sb("facts", [12, 2])
                brem = sp_.sb("brem", [12, 2, P])
                bparts = sp_.sb("bparts", [12, 3, P], BF16)
                bcols = sp_.sb("bcols", [P, 12])
                shift = sp_.sb("shift", [P, K, TP])
                ln = Norm(sp_, "ln", TP, TILES, stats=row_sums)
                jobs = [("q", k, n) for k in range(K) for n in range(3)] + [("k", k, n) for k in range(K) for n in range(3)] \
                    + [("n", k, n) for k in range(K) for n in range(3)] + [("v", 0, t) for t in range(TILES)]
                with nc.Block() as block:
                    @block.sync
                    def _(sp):
                        sp.dma_start(pos[:], const(a["consts"], "pos_code", TP)).then_inc(S["const"], 16)
                        for nm, at in (("L1_attn_wq", WQ), ("L1_attn_wk", WK), ("L1_attn_wv", WV)):
                            sp.dma_start(wt[:, at:at + K, :], a[nm].rearrange("k i j -> i k j")).then_inc(S["w"], 16)
                        for k in range(K):
                            sp.dma_start(wt[:, WB + 2 * k:WB + 2 * k + 2, :].rearrange("p a j -> p (a j)"), a["L1_attn_w_beat"][k]).then_inc(S["w"], 16)
                        sp.dma_start(wt[:, WM:WM + K, :].rearrange("p a j -> p (a j)"), a["L1_attn_w_mix"]).then_inc(S["w"], 16)
                        sp.dma_start(win[:], const(a["consts"], "window", TP).rearrange("p (k s) -> p k s", k=K)).then_inc(S["const"], 16)
                        sp.dma_start(facts[:], const(a["consts"], "gru_facts", 12)).then_inc(S["const"], 16)
                        sp.dma_start(rows[:, 0, :], a["L1_attn_gru_bih"].rearrange("k (g i) -> (k g) i", g=3)).then_inc(S["rows"], 16)
                        sp.dma_start(rows[:, 1, :], a["L1_attn_gru_bhh"].rearrange("k (g i) -> (k g) i", g=3)).then_inc(S["rows"], 16)
                        sp.dma_start(nrows[0:K, :], a["L1_attn_norm_g"]).then_inc(S["rows"], 16)
                        sp.dma_start(nrows[K:2 * K, :], a["L1_attn_norm_b"]).then_inc(S["rows"], 16)
                        sp.dma_start(bn_rows[:, 0, :], a["L1_attn_bn_g"].partition_broadcast(TP)).then_inc(S["rows"], 16)
                        sp.dma_start(bn_rows[:, 1, :], a["L1_attn_bn_b"].partition_broadcast(TP)).then_inc(S["rows"], 16)
                        sp.wait_ge(S["bparts"], 5)
                        sp.wait_ge(S["pool"], 2)
                        for k in range(3):
                            sp.dma_start(brow[k:k + 1, :, :], bparts[:, k, :]).then_inc(S["brow"], 16)
                        sp.wait_ge(S["brow"], 48)

                    @block.scalar
                    def _(act):
                        ln.scalar(nc, act)
                        for n in filter(by_scalar, range(NW // 4)):
                            act.wait_ge(S["wtp"], n + 1)
                            nc.scalar.copy(quad(n).rearrange("p a j -> p (a j)"), ps[:, n % 4, :]).then_inc(S["wt_act"], 1)
                        for n, (kind, k, m) in enumerate(jobs):
                            act.wait_ge(S["pj"], n + 1)
                            if kind == "v":
                                ins = nc.scalar.copy(vr[:, m, :, :].rearrange("p k d -> p (k d)"), ps[0:TP, n % 8, :])
                            elif kind == "n":
                                t0, tn = 16 * m, min(16, TOK - 16 * m)
                                ins = nc.scalar.activation(xn_in[:, t0:t0 + tn, k, :], ps[:, n % 8, 0:tn * B].rearrange("p (t b) -> p t b", b=B),
                                                           ACT.Identity, bias=bcols[:, 3 * k + 2:3 * k + 3])
                            else:
                                at, wd = SPANS[m]
                                ins = nc.scalar.copy((qt if kind == "q" else kt)[:, k, at:at + wd], ps[:, n % 8, 0:wd])
                            ins.then_inc(S["pj_sb"], 1)

                    @block.gpsimd
                    def _(pool):
                        nc.gpsimd.memset(ones[:], 1.0).then_inc(S["pool"], 1)
                        nc.gpsimd.memset(brow[:], 0.0).then_inc(S["pool"], 1)
                        pool.wait_ge(S["amax"], 1)
                        nc.gpsimd.partition_all_reduce(amax[:, 1:2], amax[:, 0:1], P, bass.bass_isa.ReduceOp.max).then_inc(S["allmax"], 1)

                    @block.tensor
                    def _(pe):
                        for n in range(NW // 4):
                            if n == NW // 8:
                                pe.wait_ge(S["w"], 16 * 8)
                            if n >= 4:
                                pe.wait_ge(*copied(n - 4))
                            for k in range(4):
                                last = nc.tensor.transpose(ps[:, n % 4, k * P:(k + 1) * P], quad(n)[:, k, :], ident[:])
                            last.then_inc(S["wtp"], 1)
                        pe.wait_ge(S["rows"], 96)
                        nc.tensor.transpose(ps[:, 7, 0:12], rows[:, 0, :], ident[0:12, 0:12])
                        nc.tensor.transpose(ps[:, 7, 16:16 + 2 * K], nrows[:], ident[0:2 * K, 0:2 * K]).then_inc(S["col_tp"], 1)
                        transpose_rows(nc, pe, x1, ident, ps, 4, S["xn"], S["xt_tp"])
                        pe.wait_ge(S["cols"], 2)
                        pe.wait_ge(S["xt"], 3)
                        pe.wait_ge(*copied(NW // 4 - 2))
                        pe.wait_ge(*copied(NW // 4 - 1))
                        pe.wait_ge(S["shift"], 1)
                        for k in range(K):
                            last = nc.tensor.matmul(ps[0:TP, 7, 0:P], shift[:, k, :], wt[:, WM + k, :], start=(k == 0), stop=(k == K - 1))
                        last.then_inc(S["shift_mm"], 1)
                        xtb = xt[:, 0:NTOK].rearrange("p (b t) -> p t b", t=TOK)
                        for n, (kind, k, m) in enumerate(jobs):
                            if n >= 8:
                                pe.wait_ge(S["pj_sb"], n - 7)
                            if n == 7:
                                pe.wait_ge(S["x1s"], 1)
                            if kind == "v":
                                mm = nc.tensor.matmul(ps[0:TP, n % 8, :], xt[:, m * TP:(m + 1) * TP], wt[:, WV:WV + K, :].rearrange("p k d -> p (k d)"), start=True, stop=True)
                            elif kind == "n":
                                t0, tn = 16 * m, min(16, TOK - 16 * m)
                                mm = nc.tensor.matmul(ps[:, n % 8, 0:tn * B], gru_w[:, WIH + 3 * k + 2, :], xtb[:, t0:t0 + tn, :], start=True, stop=True)
                            else:
                                at, wd = SPANS[m]
                                mm = nc.tensor.matmul(ps[:, n % 8, 0:wd], wt[:, (WQ if kind == "q" else WK) + k, :], xt[:, at:at + wd], start=True, stop=True)
                            mm.then_inc(S["pj"], 1)
                    @block.vector
                    def _(v):
                        c = Counts(v)
                        ln.vector(nc, v, c, S["v"], resid, x1)
                        v.wait_ge(S["const"], 48)
                        nc.vector.tensor_tensor(x1[:], x1[:], pos[:].unsqueeze(1).to_broadcast([TP, TILES, D]), ALU.add).then_inc(S["xn"], TILES)
                        v.wait_ge(S["w"], 16 * 8)
                        for n in range(NW // 8, NW // 4, 2):
                            v.wait_ge(S["wtp"], n + 1)
                            nc.vector.tensor_copy(quad(n).rearrange("p a j -> p (a j)"), ps[:, n % 4, :]).then_inc(S["wt_sb"], 1)
                        v.wait_ge(S["col_tp"], 1)
                        nc.vector.tensor_copy(bcols[:], ps[:, 7, 0:12]).then_inc(S["cols"], 1)
                        nc.vector.tensor_copy(ncols[:], ps[:, 7, 16:16 + 2 * K]).then_inc(S["cols"], 1)
                        v.wait_ge(S["cols"], 2)
                        nc.vector.tensor_copy(shift[:], ncols[:, K:2 * K].unsqueeze(2).to_broadcast([P, K, TP])).then_inc(S["shift"], 1)
                        for n, (at, wd) in enumerate(SPANS):
                            v.wait_ge(S["xt_tp"], n + 1)
                            nc.vector.tensor_copy(xt[:, at:at + wd], ps[:, 4 + n, 0:wd]).then_inc(S["xt"], 1)
                        v.wait_ge(S["shift_mm"], 1)
                        v.wait_ge(S["xn"], TILES)
                        nc.vector.tensor_tensor(x1s[:], x1[:], ps[0:TP, 7, 0:P].unsqueeze(1).to_broadcast([TP, TILES, D]), ALU.add).then_inc(S["x1s"], 1)
                        v.wait_ge(*copied(NW // 4 - 2))
                        v.wait_ge(*copied(NW // 4 - 1))
                        c.chain(S["v"], nc.vector.tensor_reduce(amax[:, 0:1], gru_w[:].rearrange("p a j -> p (a j)"), AX_X, ALU.max, apply_absolute_value=True))
                        c.chain(S["amax"], nc.vector.tensor_copy(scale[:, 3:4], amax[:, 0:1]))
                        v.wait_ge(S["xt"], 3)
                        xtb = xt[:, 0:NTOK].rearrange("p (b t) -> p t b", t=TOK)
                        c.chain(S["v"], nc.vector.tensor_copy(x_hi[:], xtb))
                        c.chain(S["v"], nc.vector.tensor_tensor(x_lo[:], xtb, x_hi[:], ALU.subtract))
                        v.wait_ge(S["allmax"], 1)
                        power_of_two(nc, c, S["v"], amax[:, 1:2], sbits, scale[:, 0:1], scale[:, 3:4])
                        c.chain(S["v"], nc.vector.tensor_scalar(scale[:, 1:2], scale[:, 0:1], 0.5, None, ALU.mult))
                        c.chain(S["v"], nc.vector.tensor_scalar(scale[:, 2:3], scale[:, 0:1], 0.25, None, ALU.mult))
                        v.wait_ge(S["rows"], 96)
                        c.chain(S["v"], nc.vector.scalar_tensor_tensor(out=brem[:, 0, :], in0=rows[:, 0, :], scalar=facts[:, 0:1], in1=rows[:, 1, :],
                                                                       op0=ALU.mult, op1=ALU.add))
                        c.chain(S["v"], nc.vector.tensor_scalar(brem[:, 0, :], brem[:, 0, :], scale[0:12, 1:2], None, ALU.mult))
                        c.chain(S["bparts"], nc.vector.tensor_copy(bparts[:, 0, :], brem[:, 0, :]))
                        c.chain(S["bparts"], nc.vector.tensor_tensor(brem[:, 1, :], brem[:, 0, :], bparts[:, 0, :], ALU.subtract))
                        c.chain(S["bparts"], nc.vector.tensor_copy(bparts[:, 1, :], brem[:, 1, :]))
                        c.chain(S["bparts"], nc.vector.tensor_tensor(brem[:, 0, :], brem[:, 1, :], bparts[:, 1, :], ALU.subtract))
                        c.chain(S["bparts"], nc.vector.tensor_copy(bparts[:, 2, :], brem[:, 0, :]))
                        for hi, lo, at, col in ((wi_hi, wi_lo, WIH, 1), (wh_hi, wh_lo, WHH, 2)):
                            src, sc_ = gru_w[:, at:at + 12, :].rearrange("p a j -> p (a j)"), scale[:, col:col + 1]
                            c.chain(S["whi"], nc.vector.tensor_scalar(hi[:].rearrange("p a j -> p (a j)"), src, sc_, None, ALU.mult))
                            c.chain(S["v"], nc.vector.scalar_tensor_tensor(out=lo[:].rearrange("p a j -> p (a j)"), in0=src, scalar=sc_,
                                                                           in1=hi[:].rearrange("p a j -> p (a j)"), op0=ALU.mult, op1=ALU.subtract))
                        for k in range(K):
                            nc.vector.tensor_scalar(wt[:, WB + 2 * k, :], wt[:, WB + 2 * k, :], 0.5, None, ALU.mult)
                            ins = nc.vector.tensor_scalar(wt[:, WM + k, :], wt[:, WM + k, :], ncols[:, k:k + 1], None, ALU.mult)
                        c.chain(S["v"], ins)

            sc = sa.sb("sc", [TP, 2, K, TP])
            mx = sa.sb("mx", [TP, 2, K])
            den = sa.sb("den", [TP, 2, K])
            rden = sa.sb("rden", [TP, 2, K])
            pr = sa.sb("pr", [TP, 2, K, TP])
            pn = sa.sb("pn", [TP, 2, K, TP])
            pt = sa.sb("pt", [TP, 2, K, TP])
            with nc.Block() as block:
                @block.tensor
                def _(pe):
                    for t in range(TILES + 3):
                        if t < TILES:
                            if t >= 2:
                                pe.wait_ge(S["sc"], t - 1)
                            for k in range(K):
                                cols = slice(t * TP, (t + 1) * TP)
                                last = nc.tensor.matmul(ps[0:TP, t % 2, k * TP:(k + 1) * TP], qt[:, k, cols], kt[:, k, cols], start=True, stop=True)
                            last.then_inc(S["th"], 1)
                        if 2 <= t < TILES + 2:
                            u = t - 2
                            pe.wait_ge(S["p"], u + 1)
                            if u >= 2:
                                pe.wait_ge(S["pt_sb"], u - 1)
                            for k in range(K):
                                last = nc.tensor.transpose(ps[0:TP, 2 + u % 2, k * TP:(k + 1) * TP], pn[:, u % 2, k, :], ident[0:TP, 0:TP])
                            last.then_inc(S["pt"], 1)
                        if t >= 3:
                            u = t - 3
                            pe.wait_ge(S["pt_sb"], u + 1)
                            if u >= 2:
                                pe.wait_ge(S["ao_sb"], u - 1)
                            for k in range(K):
                                last = nc.tensor.matmul(ps[:, 4 + u % 2, k * TP:(k + 1) * TP], vr[:, u, k, :], pt[:, u % 2, k, :], start=True, stop=True)
                            last.then_inc(S["ao"], 1)

                @block.scalar
                def _(act):
                    for t in range(TILES + 3):
                        if t < TILES:
                            act.wait_ge(S["sub"], t + 1)
                            if t >= 2:
                                act.wait_ge(S["p"], t - 1)
                                act.wait_ge(S["rden"], t - 1)
                            for k in range(K):
                                last = nc.scalar.activation(pr[:, t % 2, k, :], sc[:, t % 2, k, :], ACT.Exp, scale=float(D) ** -0.5,
                                                            bias=mx[:, t % 2, k:k + 1], accum_out=den[:, t % 2, k:k + 1])
                            last.then_inc(S["e"], 1)
                        if 2 <= t < TILES + 2:
                            u = t - 2
                            act.wait_ge(S["pt"], u + 1)
                            if u >= 2:
                                act.wait_ge(S["ao"], u - 1)
                            nc.scalar.copy(pt[:, u % 2, :, :].rearrange("p k s -> p (k s)"), ps[0:TP, 2 + u % 2, 0:K * TP]).then_inc(S["pt_sb"], 1)
                        if t >= 3:
                            u = t - 3
                            act.wait_ge(S["ao"], u + 1)
                            nc.scalar.copy(aot[:, :, u * TP:(u + 1) * TP], ps[:, 4 + u % 2, 0:K * TP].rearrange("p (k s) -> p k s", k=K)).then_inc(S["ao_sb"], 1)

                @block.gpsimd
                def _(pool):
                    for t in range(TILES):
                        b = t % 2
                        pool.wait_ge(S["rden"], t + 1)
                        if t >= 2:
                            pool.wait_ge(S["pt"], t - 1)
                        nc.gpsimd.tensor_tensor(pn[:, b, :, :], pr[:, b, :, :], rden[:, b, :].unsqueeze(2).to_broadcast([TP, K, TP]), ALU.mult).then_inc(S["p"], 1)

                @block.vector
                def _(v):
                    c = Counts(v)
                    for t in range(TILES + 1):
                        if t < TILES:
                            b = t % 2
                            v.wait_ge(S["th"], t + 1)
                            if t >= 2:
                                v.wait_ge(S["e"], t - 1)
                            c.chain(S["sc"], nc.vector.tensor_tensor(sc[:, b, :, :], ps[0:TP, b, 0:K * TP].rearrange("p (k s) -> p k s", k=K), win[:], ALU.add))
                            c.chain(S["lv"], nc.vector.tensor_reduce(mx[:, b, :], sc[:, b, :, :], AX_X, ALU.max))
                            nc.vector.tensor_scalar(mx[:, b, :], mx[:, b, :], -float(D) ** -0.5, None, ALU.mult).then_inc(S["sub"], 1)
                        if t >= 1:
                            u = t - 1
                            b = u % 2
                            v.wait_ge(S["e"], u + 1)
                            if u >= 2:
                                v.wait_ge(S["p"], u - 1)
                            nc.vector.reciprocal(rden[:, b, :], den[:, b, :]).then_inc(S["rden"], 1)

        TURNS = TOK // 2
        KB = K * B
        with ExitStack() as inner:
            sg = Stage(nc, inner, "gru")
            tr = sg.sb("tr", [P, KB])
            tz = sg.sb("tz", [P, K, B])
            rn = sg.sb("rn", [P, KB])
            npre = sg.sb("npre", [P, KB])
            tn = sg.sb("tn", [P, K, B])
            zh = sg.sb("zh", [P, K, B])
            pz = sg.sb("pz", [P, K, B])
            h_now = sg.sb("h_now", [P, K, B])
            xn_now = sg.sb("xn_now", [P, K, B])
            h_hi = sg.sb("h_hi", [P, K, B], F16)
            h_lo = sg.sb("h_lo", [P, K, B], F16)
            gv = sg.sem("gv")
            with nc.Block() as block:
                @block.tensor
                def _(pe):
                    def inputs(s, t):
                        for gate in range(3):
                            for k in range(K):
                                dst = ps[:, 3 * s + gate, k * B:(k + 1) * B]
                                w = 3 * k + gate
                                nc.tensor.matmul(dst, brow[:, w, :], ones[:], start=(k == 0), stop=False, skip_group_check=True)
                                if gate < 2:
                                    for wgt, x in ((wi_hi, x_hi), (wi_lo, x_hi), (wi_hi, x_lo)):
                                        nc.tensor.matmul(dst, wgt[:, w, :], x[:, t, :], start=False, stop=False, skip_group_check=True)

                    def states(s, n):
                        def high(gate):
                            for k in range(K):
                                dst = ps[:, 3 * s + gate, k * B:(k + 1) * B]
                                for wgt in (wh_hi, wh_lo):
                                    nc.tensor.matmul(dst, wgt[:, 3 * k + gate, :], h_hi[:, k, :], start=False, stop=False, skip_group_check=True)

                        def low(gate, done):
                            for k in range(K):
                                dst = ps[:, 3 * s + gate, k * B:(k + 1) * B]
                                last = nc.tensor.matmul(dst, wh_hi[:, 3 * k + gate, :], h_lo[:, k, :], start=False, stop=True, skip_group_check=True)
                            last.then_inc(done, 1)

                        pe.wait_ge(s_hi, n)
                        high(0)
                        high(2)
                        pe.wait_ge(s_lo, n)
                        low(0, s_r)
                        low(2, s_n)
                        high(1)
                        low(1, s_z)

                    inputs(0, 0)
                    with pe.Fori(0, TURNS) as i:
                        for s in range(2):
                            states(s, i * 2 + (s + 1))
                            inputs(1 - s, i * 2 + (s + 1))
                    states(0, TOK)

                @block.scalar
                def _(act):
                    nc.scalar.activation(tr[:, 0:1], scale[:, 0:1], ACT.Tanh).then_inc(S["table"], 1)
                    act.wait_ge(S["table"], 1)

                    def step(s, n):
                        act.wait_ge(s_r, n)
                        nc.scalar.activation(tr[:], ps[:, 3 * s, 0:KB], ACT.Tanh, scale=scale[:, 3:4]).then_inc(s_tr, 1)
                        act.wait_ge(s_z, n)
                        nc.scalar.activation(tz[:].rearrange("p k b -> p (k b)"), ps[:, 3 * s + 1, 0:KB], ACT.Tanh, scale=scale[:, 3:4]).then_inc(s_tz, 1)
                        act.wait_ge(s_np, n)
                        nc.scalar.activation(tn[:].rearrange("p k b -> p (k b)"), npre[:], ACT.Tanh).then_inc(s_tn, 1)

                    with act.Fori(0, TURNS) as i:
                        for s in range(2):
                            step(s, i * 2 + (s + 1))
                    step(0, TOK)

                @block.vector
                def _(v):
                    nc.vector.memset(h_hi[:], 0.0).then_inc(s_hi, 1)
                    nc.vector.memset(h_lo[:], 0.0).then_inc(s_lo, 1)
                    nc.vector.memset(gbt[:, :, NTOK:COLS], 0.0)
                    nc.vector.memset(h_now[:], 0.0).then_inc(gv, 1)
                    nc.vector.tensor_copy(xn_now[:], xn_in[:, 0, :, :]).then_inc(gv, 1)
                    GV = 6

                    def step(s, n, base):
                        v.wait_ge(s_tr, n)
                        v.wait_ge(s_n, n)
                        nc.vector.scalar_tensor_tensor(out=rn[:], in0=tr[:], scalar=1.0, in1=ps[:, 3 * s + 2, 0:KB], op0=ALU.add, op1=ALU.mult).then_inc(gv, 1)
                        v.wait_ge(gv, base + 1)
                        nc.vector.scalar_tensor_tensor(out=npre[:], in0=rn[:], scalar=scale[:, 3:4], in1=xn_now[:].rearrange("p k b -> p (k b)"),
                                                       op0=ALU.mult, op1=ALU.add).then_inc(s_np, 1)
                        v.wait_ge(s_tz, n)
                        nc.vector.scalar_tensor_tensor(out=zh[:], in0=tz[:], scalar=1.0, in1=h_now[:], op0=ALU.add, op1=ALU.mult).then_inc(gv, 1)
                        v.wait_ge(s_tn, n)
                        nc.vector.scalar_tensor_tensor(out=pz[:], in0=tz[:], scalar=1.0, in1=tn[:], op0=ALU.subtract, op1=ALU.mult).then_inc(gv, 1)
                        v.wait_ge(gv, base + 3)
                        nc.vector.scalar_tensor_tensor(out=h_hi[:], in0=zh[:], scalar=0.5, in1=pz[:], op0=ALU.mult, op1=ALU.subtract).then_inc(s_hi, 1)
                        nc.vector.scalar_tensor_tensor(out=h_now[:], in0=zh[:], scalar=0.5, in1=pz[:], op0=ALU.mult, op1=ALU.subtract).then_inc(gv, 1)
                        v.wait_ge(s_hi, n + 1)
                        v.wait_ge(gv, base + 4)
                        nc.vector.tensor_tensor(h_lo[:], h_now[:], h_hi[:], ALU.subtract).then_inc(s_lo, 1)

                    with v.Fori(0, TURNS) as i:
                        for s in range(2):
                            step(s, i * 2 + (s + 1), i * (2 * GV) + (GV * s + 2))
                            nc.vector.tensor_copy(steps[:, :, :, i * 2 + s], h_now[:]).then_inc(gv, 1)
                            nc.vector.tensor_copy(xn_now[:], xn_in[:, i * 2 + (s + 1), :, :]).then_inc(gv, 1)
                    step(0, TOK, GV * (TOK - 1) + 2)
                    nc.vector.tensor_copy(steps[:, :, :, TOK - 1], h_now[:]).then_inc(gv, 1)

        with ExitStack() as inner:
            sf = Stage(nc, inner, "mix")
            tht = hs[:, K:2 * K, :]
            th = sf.sb("th", [TP, KT, P])
            mixed = sf.sb("mixed", [TP, TILES, D])
            lt = Norm(sf, "lt", TP, KT, on_scalar=True, stats=sf.sb("lt_stats", [TP, KT, 6]))
            lm = Norm(sf, "lm", TP, TILES, on_scalar=True, stats=sf.sb("lm_stats", [TP, TILES, 6]))
            s_mn, s_gain = sf.sem("mixed_norm"), sf.sem("gain")
            fv, s_thr = sf.sem("fv"), sf.sem("thr")
            groups = [range(0, 4), range(4, 8), range(8, TILES)]
            threads = [range(K * g.start, K * g.stop) for g in groups]

            def by_scalar(t):
                return t % 4 < (3 if t < 8 else 2)

            def half(g, scalar):
                mine = [t for t in groups[g] if by_scalar(t) == scalar]
                return range(K * mine[0], K * (mine[-1] + 1))

            with nc.Block() as block:
                @block.tensor
                def _(pe):
                    def beat(g):
                        for t in groups[g]:
                            if t >= 4:
                                pe.wait_ge(s_thr, t - 3)
                            cols = slice(t * TP, (t + 1) * TP)
                            for k in range(K):
                                dst = ps[0:TP, t % 4, k * P:(k + 1) * P]
                                nc.tensor.matmul(dst, gbt[:, k, cols], wt[:, WB + 2 * k, :], start=True, stop=False)
                                last = nc.tensor.matmul(dst, aot[:, k, cols], wt[:, WB + 2 * k + 1, :], start=False, stop=True)
                            last.then_inc(S["beat"], 1)

                    def turned(g):
                        for t in groups[g]:
                            same = sum(by_scalar(u) == by_scalar(t) for u in range(t + 1))
                            pe.wait_ge(S["thn_a"] if by_scalar(t) else S["thn"], K * same)
                            if t >= 2:
                                pe.wait_ge(S["tht_sb"], t - 1)
                            for k in range(K):
                                last = nc.tensor.transpose(ps[:, 4 + t % 2, k * TP:(k + 1) * TP], th[:, K * t + k, :], ident[0:TP, 0:TP])
                            last.then_inc(S["tht"], 1)

                    def mix(g):
                        for t in groups[g]:
                            pe.wait_ge(S["tht_sb"], t + 1)
                            if t >= 2:
                                pe.wait_ge(S["mix_sb"], t - 1)
                            for k in range(K):
                                last = nc.tensor.matmul(ps[0:TP, 6 + t % 2, 0:P], tht[:, k, t * TP:(t + 1) * TP], wt[:, WM + k, :], start=(k == 0), stop=(k == K - 1))
                            last.then_inc(S["mix"], 1)

                    beat(0)
                    beat(1)
                    beat(2)
                    turned(0)
                    mix(0)
                    turned(1)
                    mix(1)
                    turned(2)
                    mix(2)

                @block.scalar
                def _(act):
                    def evacuate(g):
                        for t in groups[g]:
                            act.wait_ge(S["tht"], t + 1)
                            nc.scalar.copy(tht[:, :, t * TP:(t + 1) * TP], ps[:, 4 + t % 2, 0:K * TP].rearrange("p (k s) -> p k s", k=K)).then_inc(S["tht_sb"], 1)

                    def normalise(g):
                        norm_rows_scalar(lt, nc, act, th, th, half(g, True), g + 1, S["thn_a"])

                    norm_root(lt, nc, act, threads[0], 1)
                    normalise(0)
                    norm_root(lt, nc, act, threads[1], 2)
                    evacuate(0)
                    normalise(1)
                    norm_root(lt, nc, act, threads[2], 3)
                    evacuate(1)
                    norm_root(lm, nc, act, groups[0], 1)
                    normalise(2)
                    norm_rows_scalar(lm, nc, act, mixed, mixed, groups[0], 1, s_mn)
                    evacuate(2)
                    norm_root(lm, nc, act, groups[1], 2)
                    norm_rows_scalar(lm, nc, act, mixed, mixed, groups[1], 2, s_mn)
                    norm_root(lm, nc, act, groups[2], 3)

                @block.gpsimd
                def _(pool):
                    c = Counts(pool)
                    for g in range(2):
                        at, n = slice(groups[g].start, groups[g].stop), len(groups[g])
                        pool.wait_ge(s_mn, groups[g].stop)
                        c.chain(s_gain, nc.gpsimd.tensor_tensor(mixed[:, at, :], mixed[:, at, :], bn_rows[:, 0, :].unsqueeze(1).to_broadcast([TP, n, D]), ALU.mult))
                        c.chain(s_gain, nc.gpsimd.tensor_tensor(mixed[:, at, :], mixed[:, at, :], bn_rows[:, 1, :].unsqueeze(1).to_broadcast([TP, n, D]), ALU.add))
                        c.chain(s_gain, nc.gpsimd.tensor_tensor(resid[:, at, :], resid[:, at, :], mixed[:, at, :], ALU.add))

                @block.vector
                def _(v):
                    c = Counts(v)

                    def add_and_measure(g):
                        for t in groups[g]:
                            v.wait_ge(S["beat"], t + 1)
                            ins = nc.vector.tensor_tensor(th[:, K * t:K * (t + 1), :], ps[0:TP, t % 4, :].rearrange("p (k d) -> p k d", k=K),
                                                          x1[:, t, :].unsqueeze(1).to_broadcast([TP, K, P]), ALU.add)
                            ins.then_inc(s_thr, 1)
                            v.wait_ge(s_thr, t + 1)
                            for n in range(K * t, K * (t + 1)):
                                ins = nc.vector.bn_stats(lt.stats[:, n, :], th[:, n, :])
                        c.chain(fv, ins)
                        norm_measure(lt, nc, c, fv, th, threads[g])

                    def normalise(g):
                        norm_factors(lt, nc, v, c, fv, threads[g], g + 1)
                        norm_rows(lt, nc, th, th, half(g, False), S["thn"])

                    def mixed_and_measure(g):
                        for t in groups[g]:
                            v.wait_ge(S["mix"], t + 1)
                            nc.vector.tensor_tensor(mixed[:, t, :], ps[0:TP, 6 + t % 2, 0:P], x1s[:, t, :], ALU.add).then_inc(S["mix_sb"], 1)
                            v.wait_ge(S["mix_sb"], t + 1)
                            ins = nc.vector.bn_stats(lm.stats[:, t, :], mixed[:, t, :])
                        c.chain(fv, ins)
                        norm_measure(lm, nc, c, fv, mixed, groups[g])

                    def finish(g):
                        at, n = slice(groups[g].start, groups[g].stop), len(groups[g])
                        norm_apply(lm, nc, v, c, fv, mixed, mixed, groups[g], g + 1)
                        c.chain(fv, nc.vector.tensor_tensor(mixed[:, at, :], mixed[:, at, :], bn_rows[:, 0, :].unsqueeze(1).to_broadcast([TP, n, D]), ALU.mult))
                        c.chain(fv, nc.vector.tensor_tensor(mixed[:, at, :], mixed[:, at, :], bn_rows[:, 1, :].unsqueeze(1).to_broadcast([TP, n, D]), ALU.add))
                        c.chain(fv, nc.vector.tensor_tensor(resid[:, at, :], resid[:, at, :], mixed[:, at, :], ALU.add))

                    add_and_measure(0)
                    normalise(0)
                    add_and_measure(1)
                    normalise(1)
                    add_and_measure(2)
                    mixed_and_measure(0)
                    normalise(2)
                    norm_factors(lm, nc, v, c, fv, groups[0], 1)
                    mixed_and_measure(1)
                    norm_factors(lm, nc, v, c, fv, groups[1], 2)
                    mixed_and_measure(2)
                    finish(2)


def expert_stage(nc, a, resid, ident, dram):
    E, NE = EXPERTS, EXPERTS + 1
    with ExitStack() as ctx:
        st = Stage(nc, ctx, "ffn")
        iota = st.sb("iota", [P, 8])
        w1 = st.sb("w1", [P, NE, P])
        w2 = st.sb("w2", [P, NE, P])
        gw = st.sb("gw", [E, P])
        gwt = st.sb("gwt", [P, E])
        b1 = st.sb("b1", [NE, P])
        b1c = st.sb("b1c", [P, NE])
        b2 = st.sb("b2", [E, P])
        sb2 = st.sb("sb2", [TP, P])
        xn = st.sb("xn", [TP, TILES, D])
        xt = st.sb("xt", [P, COLS])
        lg = st.sb("lg", [TP, TILES, E])
        red = st.sb("red", [TP, TILES, 4])
        top = st.sb("top", [TP, TILES, 8])
        topi = st.sb("topi", [TP, TILES, 8], U32)
        topf = st.sb("topf", [TP, TILES, 2])
        hot = st.sb("hot", [TP, TILES, 2, E])
        comb = st.sb("comb", [TP, TILES, E])
        ct = st.sb("ct", [E, COLS])
        h1 = st.sb("h1", [P, NE, COLS])
        ps = st.ps("ps")
        ln = Norm(st, "ln", TP, TILES)
        names = ("const", "w", "v", "xn", "xt_tp", "xt", "wtp", "wts", "lg", "sub", "e", "comb", "ct_tp", "ct", "h1", "h1_sb", "y", "acc", "sb2", "out")
        S = {n: st.sem(n) for n in names}
        EARLY = 4
        firsts = [(e, n) for e in [E, *range(E)] for n in range(3)]
        BEFORE = 3 * (EARLY + 1)
        passes = [(half, t) for half in range(2) for t in range(TILES)]
        def base_bank(t):
            return (2, 7)[t // 2 % 2]

        sums, done = [], {}
        for half in range(2):
            for t0 in range(0, TILES, 2):
                pair = range(t0, min(t0 + 2, TILES))
                if half == 0:
                    sums.append((half, t0, None))
                for e in range(EARLY):
                    for t in pair:
                        sums.append((half, t, e))
                for t in pair:
                    done[half, t] = len(sums)

        block = ctx.enter_context(nc.Block())

        @block.sync
        def _(sp):
            sp.dma_start(iota[:], const(a["consts"], "iota8")).then_inc(S["const"], 16)
            sp.dma_start(gw[:], a["L1_ffn_gate_w"]).then_inc(S["const"], 16)
            sp.dma_start(b1[0:E, :], a["L1_ffn_b1"]).then_inc(S["const"], 16)
            sp.dma_start(b1[E:NE, :], a["L1_ffn_sb1"].partition_broadcast(1)).then_inc(S["const"], 16)
            sp.dma_start(b2[:], a["L1_ffn_b2"]).then_inc(S["const"], 16)
            sp.dma_start(sb2[:], a["L1_ffn_sb2"].partition_broadcast(TP)).then_inc(S["const"], 16)
            full, last = rows_view(dram)
            for t0, t1 in ((0, 4), (4, 8), (8, TILES - 1)):
                sp.wait_ge(S["acc"], done[1, t1 - 1])
                sp.dma_start(full[:, t0:t1, :], resid[:, t0:t1, :]).then_inc(S["out"], 16)
            sp.wait_ge(S["acc"], done[1, TILES - 1])
            sp.dma_start(last, resid[0:LAST, TILES - 1, :]).then_inc(S["out"], 16)
            sp.wait_ge(S["out"], 64)

        @block.scalar
        def _(act):
            act.dma_start(w1[:, 0:E, :], a["L1_ffn_w1"].rearrange("e h f -> h e f")).then_inc(S["w"], 16)
            act.dma_start(w1[:, E, :], a["L1_ffn_sw1"]).then_inc(S["w"], 16)
            act.dma_start(w2[:, 0:E, :], a["L1_ffn_w2"].rearrange("e f h -> f e h")).then_inc(S["w"], 16)
            act.dma_start(w2[:, E, :], a["L1_ffn_sw2"]).then_inc(S["w"], 16)
            ln.scalar(nc, act)
            act.wait_ge(S["sub"], 1)
            nc.scalar.activation(lg[:], lg[:], ACT.Exp).then_inc(S["e"], 1)
            act.wait_ge(S["wts"], 2)
            for n, (e, m) in enumerate(firsts):
                at, wd = SPANS[m]
                act.wait_ge(S["h1"], n + 1)
                nc.scalar.activation(h1[:, e, at:at + wd], ps[:, n % 2, 0:wd], ACT.Relu, bias=b1c[:, e:e + 1]).then_inc(S["h1_sb"], 1)

        @block.gpsimd
        def _(pool):
            pool.wait_ge(S["xn"], TILES)
            pool.wait_ge(S["const"], 16 * 6)
            nc.gpsimd.tensor_tensor(resid[:], resid[:], sb2[:].unsqueeze(1).to_broadcast([TP, TILES, D]), ALU.add).then_inc(S["sb2"], 1)

        @block.tensor
        def _(pe):
            transpose_rows(nc, pe, xn, ident, ps, 0, S["xn"], S["xt_tp"])
            pe.wait_ge(S["const"], 16 * 6)
            nc.tensor.transpose(ps[:, 7, 0:E], gw[:], ident[0:E, 0:E])
            nc.tensor.transpose(ps[:, 7, 16:16 + NE], b1[:], ident[0:NE, 0:NE]).then_inc(S["wtp"], 1)
            pe.wait_ge(S["xt"], 3)
            pe.wait_ge(S["wts"], 2)
            for t in range(TILES):
                last = nc.tensor.matmul(ps[0:TP, 6, E * t:E * t + E], xt[:, t * TP:(t + 1) * TP], gwt[:], start=True, stop=True)
            last.then_inc(S["lg"], 1)
            pe.wait_ge(S["w"], 64)

            def first(n):
                e, m = firsts[n]
                at, wd = SPANS[m]
                if n >= 2:
                    pe.wait_ge(S["h1_sb"], n - 1)
                nc.tensor.matmul(ps[:, n % 2, 0:wd], w1[:, e, :], xt[:, at:at + wd], start=True, stop=True).then_inc(S["h1"], 1)

            for n in range(BEFORE):
                first(n)
            pe.wait_ge(S["comb"], 1)
            for t in range(TILES):
                last = nc.tensor.transpose(ps[0:E, 3 + t // 4, (t % 4) * TP:(t % 4) * TP + TP], comb[:, t, :], ident[0:TP, 0:TP])
            last.then_inc(S["ct_tp"], 1)
            for n in range(BEFORE, BEFORE + 3):
                first(n)
            pe.wait_ge(S["ct"], 3)
            for i, (half, t) in enumerate(passes):
                cols = slice(t * TP, (t + 1) * TP)
                if half == 0 and BEFORE + 3 + t < 3 * NE:
                    first(BEFORE + 3 + t)
                if i == 0:
                    pe.wait_ge(S["h1_sb"], 3 * (1 + EARLY))
                if i == TILES:
                    pe.wait_ge(S["h1_sb"], 3 * NE)
                if i >= 4:
                    pe.wait_ge(S["acc"], done[passes[i - 4]])
                if half == 0:
                    base = ps[0:TP, base_bank(t), (t % 2) * P:(t % 2) * P + P]
                    nc.tensor.matmul(base, ct[:, cols], b2[:], start=True, stop=False)
                    nc.tensor.matmul(base, h1[:, E, cols], w2[:, E, :], start=False, stop=True)
                for e in range(EARLY):
                    last = nc.tensor.matmul(ps[0:TP, 3 + i % 4, e * P:(e + 1) * P], h1[:, EARLY * half + e, cols], w2[:, EARLY * half + e, :], start=True, stop=True)
                last.then_inc(S["y"], 1)

        @block.vector
        def _(v):
            c = Counts(v)
            ln.vector(nc, v, c, S["v"], resid, xn, S["xn"])
            for n, (at, wd) in enumerate(SPANS):
                v.wait_ge(S["xt_tp"], n + 1)
                nc.vector.tensor_copy(xt[:, at:at + wd], ps[:, n, 0:wd]).then_inc(S["xt"], 1)
            v.wait_ge(S["wtp"], 1)
            nc.vector.tensor_copy(gwt[:], ps[:, 7, 0:E]).then_inc(S["wts"], 1)
            nc.vector.tensor_copy(b1c[:], ps[:, 7, 16:16 + NE]).then_inc(S["wts"], 1)
            v.wait_ge(S["lg"], 1)
            v.wait_ge(S["const"], 16 * 6)
            lgp = ps[0:TP, 6, 0:E * TILES].rearrange("p (t e) -> p t e", e=E)
            c.chain(S["v"], nc.vector.tensor_reduce(red[:, :, 0], lgp, AX_X, ALU.max))
            c.chain(S["sub"], nc.vector.tensor_tensor(lg[:], lgp, red[:, :, 0:1].to_broadcast([TP, TILES, E]), ALU.subtract))
            v.wait_ge(S["e"], 1)
            c.chain(S["v"], nc.vector.tensor_reduce(red[:, :, 1], lg[:], AX_X, ALU.add))
            c.chain(S["v"], nc.vector.reciprocal(red[:, :, 2], red[:, :, 1]))
            c.chain(S["v"], nc.vector.tensor_tensor(lg[:], lg[:], red[:, :, 2:3].to_broadcast([TP, TILES, E]), ALU.mult))
            for t in range(TILES):
                ins = nc.vector.max(top[:, t, :], lg[:, t, :])
            c.chain(S["v"], ins)
            for t in range(TILES):
                ins = nc.vector.max_index(topi[:, t, :], top[:, t, :], lg[:, t, :])
            c.chain(S["v"], ins)
            c.chain(S["v"], nc.vector.tensor_copy(topf[:], topi[:, :, 0:2]))
            c.chain(S["v"], nc.vector.tensor_tensor(red[:, :, 0], top[:, :, 0], top[:, :, 1], ALU.add))
            c.chain(S["v"], nc.vector.tensor_scalar(red[:, :, 0], red[:, :, 0], 1e-20, None, ALU.add))
            c.chain(S["v"], nc.vector.reciprocal(red[:, :, 1], red[:, :, 0]))
            c.chain(S["v"], nc.vector.tensor_tensor(red[:, :, 2:4], top[:, :, 0:2], red[:, :, 1:2].to_broadcast([TP, TILES, 2]), ALU.mult))
            for k in range(2):
                ins = nc.vector.tensor_tensor(hot[:, :, k, :], iota[0:TP, :].unsqueeze(1).to_broadcast([TP, TILES, E]),
                                              topf[:, :, k:k + 1].to_broadcast([TP, TILES, E]), ALU.is_equal)
            c.chain(S["v"], ins)
            for k in range(2):
                ins = nc.vector.tensor_tensor(hot[:, :, k, :], hot[:, :, k, :], red[:, :, 2 + k:3 + k].to_broadcast([TP, TILES, E]), ALU.mult)
            c.chain(S["v"], ins)
            c.chain(S["comb"], nc.vector.tensor_tensor(comb[:], hot[:, :, 0, :], hot[:, :, 1, :], ALU.add))
            v.wait_ge(S["ct_tp"], 1)
            for n, (at, wd) in enumerate(SPANS):
                nc.vector.tensor_copy(ct[:, at:at + wd], ps[0:E, 3 + n, 0:wd]).then_inc(S["ct"], 1)
            v.wait_ge(S["sb2"], 1)
            before, seen = {}, 0
            for n, (half, t, e) in enumerate(sums):
                i = passes.index((half, t))
                pair = range(t, min(t + 2, TILES))
                need = i + len(pair) if e is None else i + 1
                if need > seen:
                    v.wait_ge(S["y"], need)
                    seen = need
                if e is None:
                    nc.vector.tensor_tensor(resid[:, t:t + len(pair), :], ps[0:TP, base_bank(t), 0:len(pair) * P].rearrange("p (t d) -> p t d", d=P),
                                            resid[:, t:t + len(pair), :], ALU.add).then_inc(S["acc"], 1)
                    before.update({u: n + 1 for u in pair})
                else:
                    v.wait_ge(S["acc"], before[t])
                    nc.vector.scalar_tensor_tensor(out=resid[:, t, :], in0=ps[0:TP, 3 + i % 4, e * P:(e + 1) * P], scalar=comb[:, t, EARLY * half + e:EARLY * half + e + 1],
                                                   in1=resid[:, t, :], op0=ALU.mult, op1=ALU.add).then_inc(S["acc"], 1)
                    before[t] = n + 1


def vit_tower_kernel(nc, a, out):
    h0 = nc.dram_tensor("h0_rows", (NTOK, D), F32, kind="Internal").ap()
    tok_stage(nc, a, h0)
    s_weights = nc.alloc_semaphore("lstm_weights_loaded")
    SEMAPHORES.append(s_weights)
    with nc.sbuf_tensor("resid", [TP, TILES, D], F32) as resid, nc.sbuf_tensor("ident", [P, P], F32) as ident:
        with nc.sbuf_tensor("hs", [P, EXPERTS, COLS], F32) as hs, nc.sbuf_tensor("weight_max", [P, 2], F32) as weight_max:
            rel_attn_stage(nc, a, h0, resid, ident, hs, s_weights, weight_max)
            with nc.sbuf_tensor("gru_w", [P, 24, P], F32) as gru_w, nc.sbuf_tensor("row_stats", [TP, TILES, 6], F32) as stats:
                lstm_stage(nc, a, resid, ident, hs, s_weights, weight_max, gru_w, stats)
                clear_semaphores(nc)
                thread_stage(nc, a, resid, ident, hs, gru_w, stats)
        clear_semaphores(nc)
        expert_stage(nc, a, resid, ident, out.rearrange("b t d -> (b t) d"))


def kernel(**inputs):
    import concourse.bacc as _bacc
    from concourse.bass_utils import run_bass_kernel_spmd as _run

    nc = _bacc.Bacc("TRN2", target_bir_lowering=False, num_devices=1)
    arrays, args = {}, {}
    feeds = dict(inputs)
    feeds["consts"] = np.concatenate([np.pad(v, ((0, P - v.shape[0]), (0, 0))) for v in CONSTS.values()], 1)
    for name, value in feeds.items():
        v = np.ascontiguousarray(value)
        arrays[f"in_{name}_dram"] = v
        args[name] = nc.dram_tensor(f"in_{name}_dram", v.shape, mybir.dt.from_np(v.dtype), kind="ExternalInput").ap()
    out = nc.dram_tensor("out_0_dram", (IMGS, TOK, D), F32, kind="ExternalOutput").ap()
    vit_tower_kernel(nc, args, out)
    r = _run(nc, [arrays], core_ids=[0])
    return r.results[0]["out_0_dram"]
```
